# Optimizing a Trainium2 kernel written in Bass

```python
import numpy as np
import jax
import jax.numpy as jnp

def _softmax(x, axis=-1):
    return jax.nn.softmax(x, axis=axis)
def _gelu(x):
    return jax.nn.gelu(x, approximate=True)
def _silu(x):
    return jax.nn.silu(x)
def _sigmoid(x):
    return jax.nn.sigmoid(x)
def _layernorm(x, axis=-1, eps=1e-5):
    m = jnp.mean(x, axis=axis, keepdims=True)
    v = jnp.var(x, axis=axis, keepdims=True)
    return (x - m) / jnp.sqrt(v + eps)
def _scatter_add(tgt, idx, src, axis=0):
    return tgt.at[idx].add(src)
def _segment_sum(src, seg, n):
    return jax.ops.segment_sum(src, seg, n)

kernel_name = 'mk_conv_preact_d2_conv_nchw512_6231d8'

def setup_inputs(seed: int = 0):
    np.random.seed(seed)
    _w = jnp.asarray
    def _rec_inputs():
        import jax
        import jax.numpy as jnp
        _gk = jax.random.key(seed)
        x = 7.22e-05 + 1 * jax.random.normal(jax.random.fold_in(_gk, 1), (16, 512, 32, 32), jnp.float32)
        return x
    x = _rec_inputs()
    def _L0_conv_setup():
        import jax, jax.numpy as jnp
        import numpy as np
        DIM = 512
        HEADS = 8
        AGENT = 49
        POOL = 7
        EPS = 1e-05

        def _adaptive_avg_pool(x, out_hw):
            B, C, H, W = x.shape
            cs = jnp.cumsum(jnp.cumsum(x, axis=2), axis=3)
            cs = jnp.pad(cs, ((0, 0), (0, 0), (1, 0), (1, 0)))
            hs = np.floor(np.arange(out_hw) * H / out_hw).astype(np.int32)
            he = np.ceil((np.arange(out_hw) + 1) * H / out_hw).astype(np.int32)
            ws = np.floor(np.arange(out_hw) * W / out_hw).astype(np.int32)
            we = np.ceil((np.arange(out_hw) + 1) * W / out_hw).astype(np.int32)
            area = ((he - hs)[:, None] * (we - ws)[None, :]).astype(np.float32)
            s = cs[:, :, he][:, :, :, we] - cs[:, :, hs][:, :, :, we] - cs[:, :, he][:, :, :, ws] + cs[:, :, hs][:, :, :, ws]
            return s / area
        key = jax.random.key(seed)
        ks = jax.random.split(key, 8)
        d = DIM

        def w(k, shape, s=0.02):
            return jax.random.normal(k, shape, jnp.float32) * s
        return {'x': jax.random.normal(ks[0], (16, d, 32, 32), jnp.float32), 'H': 32, 'W': 32, 'q_w': w(ks[1], (d, d)), 'kv_w': w(ks[2], (2 * d, d)), 'dw_w': w(ks[3], (d, 1, 3, 3), 0.1), 'dw_b': jnp.zeros((d,), jnp.float32), 'bn_gamma': jnp.ones((d,), jnp.float32), 'bn_beta': jnp.zeros((d,), jnp.float32), 'bn_mean': jnp.zeros((d,), jnp.float32), 'bn_var': jnp.ones((d,), jnp.float32), 'pw_w': w(ks[4], (d, d, 1, 1)), 'pw_b': jnp.zeros((d,), jnp.float32), 'proj_w': w(ks[5], (d, d)), 'proj_b': jnp.zeros((d,), jnp.float32), 'enh1_w': w(ks[6], (d, d)), 'enh1_b': jnp.zeros((d,), jnp.float32), 'enh2_w': w(ks[7], (d, d)), 'enh2_b': jnp.zeros((d,), jnp.float32)}
    _L0_conv_all = _L0_conv_setup()
    _L0_conv_in = {k: v for k, v in _L0_conv_all.items() if k in ('q_w', 'kv_w', 'dw_w', 'dw_b', 'bn_gamma', 'bn_beta', 'bn_mean', 'bn_var', 'pw_w', 'pw_b', 'proj_w', 'proj_b', 'enh1_w', 'enh1_b', 'enh2_w', 'enh2_b', )}
    del _L0_conv_all

    def _L1_conv_setup():
        import jax, jax.numpy as jnp
        from jax import lax
        import numpy as np
        UP = 2
        DOWN = 2
        PADDING = (11, 10, 11, 10)
        GAIN = float(np.sqrt(2.0))
        SLOPE = 0.2
        CLAMP = 256.0
        UP_TAPS = 12
        IN_CUTOFF = 8.0
        OUT_CUTOFF = 8.0
        IN_HALF_WIDTH = 6.0
        OUT_HALF_WIDTH = 6.0
        TEMP_FS = 32.0

        def _design_lowpass(numtaps, cutoff, width, fs):
            nyq = fs / 2.0
            atten = 2.285 * (numtaps - 1) * np.pi * (width / nyq) + 7.95
            if atten > 50.0:
                beta = 0.1102 * (atten - 8.7)
            elif atten > 21.0:
                beta = 0.5842 * (atten - 21.0) ** 0.4 + 0.07886 * (atten - 21.0)
            else:
                beta = 0.0
            m = np.arange(numtaps) - (numtaps - 1) / 2.0
            c = cutoff / nyq
            h = c * np.sinc(c * m)
            h = h * np.kaiser(numtaps, beta)
            h = h / np.sum(h)
            return h.astype(np.float32)

        def _upfirdn2d_sep(x, f, up, down, pad, gain):
            N, C, H, W = x.shape
            fr = f[::-1].astype(x.dtype)
            kH = fr.reshape(1, 1, -1, 1)
            kW = fr.reshape(1, 1, 1, -1)
            px0, px1, py0, py1 = pad
            xr = x.reshape(N * C, 1, H, W)
            xr = lax.conv_general_dilated(xr, kH, window_strides=(down, 1), padding=((py0, py1 + up - 1), (0, 0)), lhs_dilation=(up, 1))
            xr = lax.conv_general_dilated(xr, kW, window_strides=(1, down), padding=((0, 0), (px0, px1 + up - 1)), lhs_dilation=(1, up))
            Ho, Wo = (xr.shape[2], xr.shape[3])
            return xr.reshape(N, C, Ho, Wo) * gain
        key = jax.random.key(seed)
        k1, k2 = jax.random.split(key)
        x = jax.random.normal(k1, (8, 512, 64, 64), dtype=jnp.float32)
        bias = jax.random.normal(k2, (512,), dtype=jnp.float32) * 0.1
        up_filter = jnp.asarray(_design_lowpass(UP_TAPS, IN_CUTOFF, IN_HALF_WIDTH * 2, TEMP_FS))
        down_filter = jnp.asarray(_design_lowpass(UP_TAPS, OUT_CUTOFF, OUT_HALF_WIDTH * 2, TEMP_FS))
        return {'x': x, 'bias': bias, 'up_filter': up_filter, 'down_filter': down_filter}
    _L1_conv_all = _L1_conv_setup()
    _L1_conv_in = {k: v for k, v in _L1_conv_all.items() if k in ('bias', 'up_filter', 'down_filter', )}
    del _L1_conv_all

    return {
        "x": x,
        "L0_conv_q_w": _L0_conv_in["q_w"],
        "L0_conv_kv_w": _L0_conv_in["kv_w"],
        "L0_conv_dw_w": _L0_conv_in["dw_w"],
        "L0_conv_dw_b": _L0_conv_in["dw_b"],
        "L0_conv_bn_gamma": _L0_conv_in["bn_gamma"],
        "L0_conv_bn_beta": _L0_conv_in["bn_beta"],
        "L0_conv_bn_mean": _L0_conv_in["bn_mean"],
        "L0_conv_bn_var": _L0_conv_in["bn_var"],
        "L0_conv_pw_w": _L0_conv_in["pw_w"],
        "L0_conv_pw_b": _L0_conv_in["pw_b"],
        "L0_conv_proj_w": _L0_conv_in["proj_w"],
        "L0_conv_proj_b": _L0_conv_in["proj_b"],
        "L0_conv_enh1_w": _L0_conv_in["enh1_w"],
        "L0_conv_enh1_b": _L0_conv_in["enh1_b"],
        "L0_conv_enh2_w": _L0_conv_in["enh2_w"],
        "L0_conv_enh2_b": _L0_conv_in["enh2_b"],
        "L1_conv_bias": _L1_conv_in["bias"],
        "L1_conv_up_filter": _L1_conv_in["up_filter"],
        "L1_conv_down_filter": _L1_conv_in["down_filter"],
    }

def reference(x, L0_conv_q_w, L0_conv_kv_w, L0_conv_dw_w, L0_conv_dw_b, L0_conv_bn_gamma, L0_conv_bn_beta, L0_conv_bn_mean, L0_conv_bn_var, L0_conv_pw_w, L0_conv_pw_b, L0_conv_proj_w, L0_conv_proj_b, L0_conv_enh1_w, L0_conv_enh1_b, L0_conv_enh2_w, L0_conv_enh2_b, L1_conv_bias, L1_conv_up_filter, L1_conv_down_filter):
    import jax
    import jax.numpy as jnp
    def _L0_conv_ref(x, H, W, q_w, kv_w, dw_w, dw_b, bn_gamma, bn_beta, bn_mean, bn_var, pw_w, pw_b, proj_w, proj_b, enh1_w, enh1_b, enh2_w, enh2_b):
        import jax, jax.numpy as jnp
        import numpy as np
        DIM = 512
        HEADS = 8
        AGENT = 49
        POOL = 7
        EPS = 1e-05

        def _adaptive_avg_pool(x, out_hw):
            B, C, H, W = x.shape
            cs = jnp.cumsum(jnp.cumsum(x, axis=2), axis=3)
            cs = jnp.pad(cs, ((0, 0), (0, 0), (1, 0), (1, 0)))
            hs = np.floor(np.arange(out_hw) * H / out_hw).astype(np.int32)
            he = np.ceil((np.arange(out_hw) + 1) * H / out_hw).astype(np.int32)
            ws = np.floor(np.arange(out_hw) * W / out_hw).astype(np.int32)
            we = np.ceil((np.arange(out_hw) + 1) * W / out_hw).astype(np.int32)
            area = ((he - hs)[:, None] * (we - ws)[None, :]).astype(np.float32)
            s = cs[:, :, he][:, :, :, we] - cs[:, :, hs][:, :, :, we] - cs[:, :, he][:, :, :, ws] + cs[:, :, hs][:, :, :, ws]
            return s / area
        B, C, H, W = x.shape
        N = H * W
        hd = C // HEADS
        scale = hd ** (-0.5)
        dn = ('NCHW', 'OIHW', 'NCHW')
        x_flat = x.reshape(B, C, N).transpose(0, 2, 1)
        q = (x_flat @ q_w.T).reshape(B, N, HEADS, hd).transpose(0, 2, 1, 3)
        kv = (x_flat @ kv_w.T).reshape(B, N, 2, HEADS, hd).transpose(2, 0, 3, 1, 4)
        k, v = (kv[0], kv[1])
        a = _adaptive_avg_pool(x, POOL)
        a = a.reshape(B, C, AGENT).transpose(0, 2, 1)
        a = a.reshape(B, C, POOL, POOL)
        a = jax.lax.conv_general_dilated(a, dw_w, (1, 1), 'SAME', feature_group_count=C, dimension_numbers=dn)
        a = a + dw_b[None, :, None, None]
        a = (a - bn_mean[None, :, None, None]) * jax.lax.rsqrt(bn_var + EPS)[None, :, None, None]
        a = a * bn_gamma[None, :, None, None] + bn_beta[None, :, None, None]
        a = jax.nn.relu(a)
        a = jax.lax.conv_general_dilated(a, pw_w, (1, 1), 'SAME', dimension_numbers=dn)
        a = a + pw_b[None, :, None, None]
        a = a.reshape(B, AGENT, C)
        a = a.reshape(B, HEADS, AGENT, hd)
        agent_attn = jax.nn.softmax(jnp.einsum('bhad,bhnd->bhan', a, k) * scale, axis=-1)
        agg = jnp.einsum('bhan,bhnd->bhad', agent_attn, v)
        q_attn = jax.nn.softmax(jnp.einsum('bhnd,bhad->bhna', q, a) * scale, axis=-1)
        enh = jnp.einsum('bhna,bhad->bhnd', q_attn, agg)
        enh = enh.transpose(0, 2, 1, 3).reshape(B, N, C)
        x_out = enh @ proj_w.T + proj_b
        out = jax.nn.relu(x_out @ enh1_w.T + enh1_b) @ enh2_w.T + enh2_b + x_out
        return out.reshape(B, C, H, W)

    def _L1_conv_ref(x, bias, up_filter, down_filter):
        import jax, jax.numpy as jnp
        from jax import lax
        import numpy as np
        UP = 2
        DOWN = 2
        PADDING = (11, 10, 11, 10)
        GAIN = float(np.sqrt(2.0))
        SLOPE = 0.2
        CLAMP = 256.0
        UP_TAPS = 12
        IN_CUTOFF = 8.0
        OUT_CUTOFF = 8.0
        IN_HALF_WIDTH = 6.0
        OUT_HALF_WIDTH = 6.0
        TEMP_FS = 32.0

        def _design_lowpass(numtaps, cutoff, width, fs):
            nyq = fs / 2.0
            atten = 2.285 * (numtaps - 1) * np.pi * (width / nyq) + 7.95
            if atten > 50.0:
                beta = 0.1102 * (atten - 8.7)
            elif atten > 21.0:
                beta = 0.5842 * (atten - 21.0) ** 0.4 + 0.07886 * (atten - 21.0)
            else:
                beta = 0.0
            m = np.arange(numtaps) - (numtaps - 1) / 2.0
            c = cutoff / nyq
            h = c * np.sinc(c * m)
            h = h * np.kaiser(numtaps, beta)
            h = h / np.sum(h)
            return h.astype(np.float32)

        def _upfirdn2d_sep(x, f, up, down, pad, gain):
            N, C, H, W = x.shape
            fr = f[::-1].astype(x.dtype)
            kH = fr.reshape(1, 1, -1, 1)
            kW = fr.reshape(1, 1, 1, -1)
            px0, px1, py0, py1 = pad
            xr = x.reshape(N * C, 1, H, W)
            xr = lax.conv_general_dilated(xr, kH, window_strides=(down, 1), padding=((py0, py1 + up - 1), (0, 0)), lhs_dilation=(up, 1))
            xr = lax.conv_general_dilated(xr, kW, window_strides=(1, down), padding=((0, 0), (px0, px1 + up - 1)), lhs_dilation=(1, up))
            Ho, Wo = (xr.shape[2], xr.shape[3])
            return xr.reshape(N, C, Ho, Wo) * gain
        y = _upfirdn2d_sep(x, up_filter, UP, 1, PADDING, float(UP * UP))
        y = y + bias[None, :, None, None]
        y = jnp.where(y >= 0, y, y * SLOPE) * GAIN
        y = jnp.clip(y, -CLAMP, CLAMP)
        y = _upfirdn2d_sep(y, down_filter, 1, DOWN, (0, 0, 0, 0), 1.0)
        return y

    def _gn(v, G=32, eps=1e-5):
        B_, C_, H_, W_ = v.shape
        g = v.reshape(B_, G, C_ // G, H_, W_)
        m = jnp.mean(g, axis=(2, 3, 4), keepdims=True)
        s = jnp.var(g, axis=(2, 3, 4), keepdims=True)
        return ((g - m) / jnp.sqrt(s + eps)).reshape(v.shape)

    def _ln_c(v, eps=1e-6):
        m = jnp.mean(v, axis=1, keepdims=True)
        s = jnp.var(v, axis=1, keepdims=True)
        return (v - m) / jnp.sqrt(s + eps)

    def _ln_t(v, eps=1e-5):
        m = jnp.mean(v, axis=-1, keepdims=True)
        s = jnp.var(v, axis=-1, keepdims=True)
        return (v - m) / jnp.sqrt(s + eps)

    def _to_tokens(v):
        B_, C_, H_, W_ = v.shape
        return v.reshape(B_, C_, H_ * W_).transpose(0, 2, 1)
    def _from_tokens(t, like):
        B_, C_, H_, W_ = like.shape
        return t.transpose(0, 2, 1).reshape(B_, C_, H_, W_)

    x = x + _L0_conv_ref(_gn(x), 32, 32, L0_conv_q_w, L0_conv_kv_w, L0_conv_dw_w, L0_conv_dw_b, L0_conv_bn_gamma, L0_conv_bn_beta, L0_conv_bn_mean, L0_conv_bn_var, L0_conv_pw_w, L0_conv_pw_b, L0_conv_proj_w, L0_conv_proj_b, L0_conv_enh1_w, L0_conv_enh1_b, L0_conv_enh2_w, L0_conv_enh2_b)
    x = x + _L1_conv_ref(_gn(x), L1_conv_bias, L1_conv_up_filter, L1_conv_down_filter)
    return x


_drawn_inputs = setup_inputs


def setup_inputs(seed=0):
    import zlib

    import numpy as np

    out = dict(_drawn_inputs(seed))
    spreads = {'L0_conv_dw_b': (0.0, 0.8),
     'L0_conv_bn_gamma': (1.0, 0.6),
     'L0_conv_bn_beta': (0.0, 0.8),
     'L0_conv_bn_mean': (0.0, 0.8),
     'L0_conv_bn_var': (1.0, 0.6),
     'L0_conv_pw_b': (0.0, 0.8),
     'L0_conv_proj_b': (0.0, 0.8),
     'L0_conv_enh1_b': (0.0, 2.0),
     'L0_conv_enh2_b': (0.0, 0.8)}
    factors = {'L0_conv_q_w': 8.0,
     'L0_conv_kv_w': 8.0,
     'L0_conv_dw_w': 8.0,
     'L0_conv_pw_w': 8.0,
     'L0_conv_proj_w': 8.0,
     'L0_conv_enh1_w': 4.32,
     'L1_conv_bias': 8.0}
    for name, (base, spread) in spreads.items():
        noise = np.random.default_rng([zlib.crc32(name.encode()), seed]).standard_normal(out[name].shape)
        drawn = base * np.exp(spread * noise) if base else spread * noise
        out[name] = jnp.asarray(drawn.astype(out[name].dtype))
    for name, factor in factors.items():
        out[name] = (out[name] * factor).astype(out[name].dtype)
    return out
```

```python
from contextlib import ExitStack

import concourse.bass as bass
from concourse import mybir

F32 = mybir.dt.float32
I32 = mybir.dt.int32
U32 = mybir.dt.uint32
ALU = mybir.AluOpType
ACT = mybir.ActivationFunctionType
AX = mybir.AxisListType

P = 128
B, C, H, W = 16, 512, 32, 32
N = H * W
CT = C // P
NT = N // P
HALF = 512
HEADS, POOL = 8, 7
AG = POOL * POOL
PAIR = 2 * AG
AGS = HEADS * AG
HD = C // HEADS
SCALE = float(HD) ** -0.5
GROUP = C // 32
GN_EPS, BN_EPS = 1e-5, 1e-5
SLOPE, CLAMP, ROOT2 = 0.2, 256.0, 2.0 ** 0.5
TAPS = 12

WIN = [(i * H // POOL, -(-(i + 1) * H // POOL)) for i in range(POOL)]

MR, MC = 4, 8
WH, WW = MR + 5, MC + 5
WIN_N = WH * WW
PT_N = 4 * MR * MC
PADH = 5 + 33 + MR
BANDS = [(0, PT_N, 0), (4, PT_N, 0), (8, PT_N, 0), (12, PT_N, 0), (16, PT_N, 0), (17, 32, 3),
         (21, PT_N, 0), (25, PT_N, 0), (29, PT_N, 0), (33, PT_N, 0)]
COLS = [0, 8, 16, 24, 32]
SPANS = [(max(0, n - 5), max(0, 5 - n), min(W, n + MC) - max(0, n - 5)) for n in COLS]
PATCHES = [(m, n, k, a) for m, k, a in BANDS for n in COLS]
NPATCH = len(PATCHES)
KEEP0, KEEP1 = 20, 30
RING = 4
XSLOTS = 4

CHAIN_BEFORE, CHAIN_IMAGE = 41, 57
PCHAIN_BEFORE, PCHAIN_IMAGE = 24, 21

BN_AT, POOL_AT, AGGR_AT, STAT_AT, XN_AT = 9, 10, 17, 18, 20
MIX_AT, PW_AT, TURN_AT = 24, 42, 48


def y_slot(p):
    if KEEP0 <= p < KEEP1:
        return RING + p - KEEP0
    return (p if p < KEEP0 else p - (KEEP1 - KEEP0)) % RING


def down_window(p, half):
    m, n, _, a_lo = PATCHES[p]
    k0, l0 = m - 5, n - 5
    k_lo, k_hi = max(16 * half, k0 + a_lo), min(16 * half + 16, k0 + WH)
    l_lo, l_hi = max(0, l0), min(W, l0 + WW)
    return k_lo, k_hi, l_lo, l_hi, k_lo - k0, k_hi - k0, l_lo - l0, l_hi - l0


def build(nc, x, wq, wk, wvT, pwT, projT, proj, w1T, w2T, dw_w, dw_b, bn_g, bn_b, bn_m, bn_v, pw_b,
          proj_b, enh1_b, enh2_b, bias, up_f, down_f, out, agent_dram, filt_dram):
    with ExitStack() as ctx:
        def sb(name, shape, dt=F32):
            return ctx.enter_context(nc.sbuf_tensor(name, shape, dt))

        def sem(name):
            return ctx.enter_context(nc.semaphore(name))

        w_q, w_k, w_vT, w_pwT, w_projT, w_p1, w_2T = [sb(n, [P, CT, C]) for n in (
            "w_q", "w_k", "w_vT", "w_pwT", "w_projT", "w_p1", "w_2T")]
        ident = sb("ident", [P, P])
        gmean = sb("gmean", [P, P])
        op_up = sb("op_up", [WIN_N + 1, PT_N])
        op_dn = sb("op_dn", [PT_N, WH, WW])
        m_bias = sb("m_bias", [PAIR, C])
        tapw = sb("tapw", [P, CT, 9])
        par = sb("par", [P, 8, CT])
        tapb = sb("tapb", [P, CT])
        b1p = sb("b1p", [P, CT])
        area = sb("area", [P, POOL, POOL])
        xin = sb("xin", [P, CT, N])
        xn = sb("xn", [P, CT, N])
        x2 = sb("x2", [P, CT, N])
        reg_m = sb("reg_m", [P, HEADS // 2, C])
        m_mat = reg_m[0:PAIR]
        prep = reg_m[:].rearrange("p t c -> p (t c)")
        at_bd = prep[:, 0:AGS].rearrange("p (t a) -> p t a", a=PAIR)
        pooled, conv, ctmp = [prep[:, AGS + k * CT * AG:AGS + (k + 1) * CT * AG]
                              .rearrange("p (t i j) -> p t i j", i=POOL, j=POOL) for k in range(3)]
        MIX = AGS + 4 * CT * AG
        mix_out = prep[0:AG, MIX:MIX + C]
        mix_in = prep[:, MIX + C:MIX + C + CT * AG].rearrange("p (t i j) -> p t i j", i=POOL, j=POOL)
        pwo = prep[:, AGS + 3 * CT * AG:AGS + 4 * CT * AG].rearrange("p (t a) -> p t a", a=AG)
        reg_f = sb("reg_f", [P, HEADS // 2, C])
        f_mat = reg_f
        xwin = reg_f
        reg_a = sb("reg_a", [P, NT * C + NT * AGS + 3 * CT * AGS])

        def part(start, *shape):
            n = 1
            for k in shape:
                n *= k
            names = "abcd"[:len(shape)]
            return reg_a[:, start:start + n].rearrange(f"p ({' '.join(names)}) -> p {' '.join(names)}",
                                                       **dict(zip(names, shape)))

        xT, pT = part(0, NT, C), part(NT * C, NT, AGS)
        pxT, g_k, g_q = [part(NT * (C + AGS) + k * CT * AGS, CT, AGS) for k in range(3)]
        BAND_N = PADH * WW
        XPAD = CT * len(COLS) * BAND_N
        xpad_run = part(0, CT, len(COLS), BAND_N)
        xpad = part(0, CT, len(COLS), BAND_N).rearrange("p t n (h w) -> p t n h w", w=WW)
        cpad = part(XPAD, CT, POOL + 2, POOL + 2)
        pw_in = reg_a[:, 0:CT * C].rearrange("p (t n) -> p t n", t=CT)
        p1_in = reg_a[:, CT * C:2 * CT * C].rearrange("p (t n) -> p t n", t=CT)
        reg_y = sb("reg_y", [P, 2 * CT * N])
        h1T = reg_y[:, 0:CT * N].rearrange("p (t n) -> p t n", t=CT)
        qT = reg_y[:, CT * N:2 * CT * N].rearrange("p (t n) -> p t n", t=CT)
        prob = reg_y[:, 0:2 * N].rearrange("p (s n) -> p s n", s=2)
        qp = reg_y[:, 2 * N:2 * N + 4 * AGS].rearrange("p (s a) -> p s a", s=4)
        YPT = (RING + KEEP1 - KEEP0) * HALF
        rowsum = reg_y[:, YPT:YPT + CT * POOL * W].rearrange("p (t i w) -> p t i w", t=CT, i=POOL)
        ypt = reg_y[:, 0:(RING + KEEP1 - KEEP0) * HALF].rearrange("p (s c) -> p s c", c=HALF)
        agg = sb("agg", [P, HEADS // 2, PAIR])
        at_in = sb("at_in", [PAIR, HEADS // 2, P])
        kmax = sb("kmax", [PAIR, HEADS // 2])
        ksum = sb("ksum", [PAIR, HEADS // 2])
        krec = sb("krec", [PAIR, HEADS // 2])
        qmax, qsum = sb("qmax", [P, 2, HEADS]), sb("qsum", [P, 2, HEADS])
        bns = sb("bns", [P, CT, 2, 6])
        stat = sb("stat", [P, CT, 2])
        gs = sb("gs", [P, CT, 2])
        nv, ny, nt1, nt2 = [sb(n, [P, CT]) for n in ("nv", "ny", "nt1", "nt2")]
        rstd = [sb(n, [P, CT]) for n in ("rstd0", "rstd1")]
        shift = [sb(n, [P, CT]) for n in ("shift0", "shift1")]

        idle = [sb(f"idle{j}", [P, 1]) for j in range(2)]
        fzero = sb("fzero", [2, 44])
        frow = [x2[0:WIN_N, 2, 2 * MR * j:2 * MR * j + 2 * MR] for j in range(2)]
        fcol = [x2[0:WIN_N, 3, 2 * MC * j:2 * MC * j + 2 * MC] for j in range(2)]
        psum = ctx.enter_context(nc.psum_tensor("psum", [P, 8, HALF], F32))

        w_load, row_load = sem("w_load"), sem("row_load")
        f_store, f_load = sem("f_store"), sem("f_load")
        pool_setup = sem("pool_setup")
        v_op, v_tap, v_p1, v_b1, v_dn, v_bias = [sem(n) for n in ("v_op", "v_tap", "v_p1", "v_b1", "v_dn", "v_bias")]
        pe_p1, pe_b1, pe_dn = sem("pe_p1"), sem("pe_b1"), sem("pe_dn")
        chain, pchain = sem("v_chain"), sem("pool_chain")
        x_loaded, x2_moved = sem("x_loaded"), sem("x2_moved")
        stat_ready, gstat_ready, norm_ready = sem("stat_ready"), sem("gstat_ready"), sem("norm_ready")
        stat1_ready, gstat1_ready, norm1_ready = sem("stat1_ready"), sem("gstat1_ready"), sem("norm1_ready")
        gs_read = [sem("gs0_read"), sem("gs1_read")]
        bn_ready, xn_ready, pool_ready, conv_ready = sem("bn_ready"), sem("xn_ready"), sem("pool_ready"), sem("conv_ready")
        pn_ready, mix_made, mix_ready, mix_stored, mix_loaded = (
            sem("pn_ready"), sem("mix_made"), sem("mix_ready"), sem("mix_stored"), sem("mix_loaded"))
        pw_ready, pwo_ready = sem("pw_ready"), sem("pwo_ready")
        at_stored, at_loaded, at_turned, at_ready = sem("at_stored"), sem("at_loaded"), sem("at_turned"), sem("at_ready")
        g_made = sem("g_made")
        g_ready = [sem("g_ready_dve"), sem("g_ready_act")]
        sk_ready, kmax_ready, prob_ready = sem("sk_ready"), sem("kmax_ready"), sem("prob_ready")
        xT_made, pT_made, pT_ready = sem("xT_made"), sem("pT_made"), sem("pT_ready")
        xT_ready = [sem("xT_ready_act"), sem("xT_ready_dve")]
        krec_ready = sem("krec_ready")
        sq_made, qsub_ready, qexp_ready, qrec_ready, qp_ready = (
            sem("sq_made"), sem("qsub_ready"), sem("qexp_ready"), sem("qrec_ready"), sem("qp_ready"))
        px_made, px_ready, agg_made, agg_ready = sem("px_made"), sem("px_ready"), sem("agg_made"), sem("agg_ready")
        f_made, f_ready, m_made, m_ready = sem("f_made"), sem("f_ready"), sem("m_made"), sem("m_ready")
        qT_made = sem("qT_made")
        qT_ready = [sem("qT_ready_act"), sem("qT_ready_dve")]
        h1_made, h1_ready, o_made, x2_ready = sem("h1_made"), sem("h1_ready"), sem("o_made"), sem("x2_ready")
        border_ready = sem("border_ready")
        xpad_ready = [sem("xpad_ready_act"), sem("xpad_ready_dve")]
        win_made = sem("win_made")
        win_ready = sem("win_ready")
        up_made, relu_ready, up_read, y_ready = sem("up_made"), sem("relu_ready"), sem("up_read"), sem("y_ready")
        z_made, z_ready = sem("z_made"), sem("z_ready")

        ctx.enter_context(nc.allow_non_contiguous_dma(reason="weights and small layouts"))
        block = ctx.enter_context(nc.Block())

        def tiles(w):
            return w.rearrange("(t p) n -> p t n", p=P)

        def cols(v):
            return v.rearrange("(t p) -> p t", p=P)

        def row(v):
            return v.rearrange("(a n) -> a n", a=1)

        def token_tile(nt):
            start = 2 * P * (nt // 2) + nt % 2
            return slice(start, start + 2 * P - 1, 2)

        def bcast(ap, shape):
            return ap.broadcast_to(shape)

        def carry(eng, mine):
            eng.tensor_tensor(idle[mine][:], ident[:, 0:1], ident[:, 1:2], ALU.mult)

        ROW_LOADS = 1 + XSLOTS

        @block.sync
        def _(sp):
            def load_x(i):
                for t in range(CT):
                    sp.dma_start(xin[:, t, :], x[i].rearrange("(t p) n -> t p n", p=P)[t]).then_inc(x_loaded, 16)

            def mix_bounce(i):
                sp.wait_ge(mix_ready, i + 1)
                sp.dma_start(agent_dram[1].rearrange("(a c) -> a c", a=AG), mix_out).then_inc(mix_stored, 16)
                sp.wait_ge(mix_stored, 16 * i + 16)
                sp.dma_start(mix_in.rearrange("p t i j -> p t (i j)"),
                             agent_dram[1].rearrange("(t p a) -> p t a", t=CT, p=P)).then_inc(mix_loaded, 16)

            def agent_bounce(i, first=False):
                sp.wait_ge(pwo_ready, i + 1)
                sp.dma_start(agent_dram[0].rearrange("(t p a) -> p t a", t=CT, p=P), pwo).then_inc(at_stored, 16)
                sp.wait_ge(at_stored, 16 * i + 16)
                if not first:
                    sp.wait_ge(at_turned, i)
                for hh in range(2):
                    src = agent_dram[0].rearrange("(t h i d) -> h i t d", t=HEADS // 2, h=2, i=AG)[hh]
                    sp.dma_start(at_in[AG * hh:AG * hh + AG, :, HD * hh:HD * hh + HD], src).then_inc(at_loaded, 16)

            def store(b, half):
                for t in range(CT):
                    sp.wait_ge(z_ready, 8 * b + 4 * half + t + 1)
                    sp.dma_start(out[b].rearrange("(t p) n -> t p n", p=P)[t, :, HALF * half:HALF * half + HALF],
                                 x2[:, t, HALF * half:HALF * half + HALF]).then_inc(x2_moved, 16)

            load_x(0)
            sp.dma_start(pw_in, tiles(proj)).then_inc(w_load, 16)
            sp.dma_start(p1_in, tiles(w1T)).then_inc(w_load, 16)
            sp.dma_start(tapw[:], dw_w.rearrange("(t p) k -> p t k", p=P)).then_inc(w_load, 16)
            for j, v in enumerate((dw_b, bn_g, bn_b, bn_m, bn_v, pw_b, enh1_b, proj_b)):
                sp.dma_start(par[:, j, :], cols(v)).then_inc(w_load, 16)
            for dst, src in ((w_pwT, pwT), (w_k, wk), (w_q, wq), (w_vT, wvT), (w_projT, projT), (w_2T, w2T)):
                sp.dma_start(dst[:], tiles(src)).then_inc(w_load, 16)
            sp.wait_ge(pool_setup, 1)
            sp.dma_start(m_bias[0:AG, :], row(proj_b).broadcast_to([AG, C])).then_inc(row_load, 16)
            sp.dma_start(x2[0:AG, 0, 0:C], row(enh2_b).broadcast_to([AG, C])).then_inc(x2_moved, 16)
            for s in range(XSLOTS):
                sp.dma_start(xwin[WIN_N:WIN_N + 1, s, :], row(bias)).then_inc(row_load, 16)
            sp.dma_start(filt_dram, fzero[:]).then_inc(f_store, 16)
            sp.wait_ge(f_store, 16)
            for j, f in enumerate((up_f, down_f)):
                sp.dma_start(filt_dram[j:j + 1, 16:16 + TAPS], row(f)).then_inc(f_store, 16)
            sp.wait_ge(f_store, 48)
            for j in range(2):
                for a in range(WH):
                    shifted = filt_dram[j:j + 1, 2 * a + 10:2 * a + 18].broadcast_to([WW, 8])
                    sp.dma_start(frow[j][WW * a:WW * a + WW, :], shifted).then_inc(f_load, 16)
                for c in range(WW):
                    shifted = filt_dram[j:j + 1, 2 * c + 2:2 * c + 18].broadcast_to([WH, 16])
                    sp.dma_start(fcol[j][c:c + WW * (WH - 1) + 1:WW, :], shifted).then_inc(f_load, 16)
            mix_bounce(0)
            agent_bounce(0, first=True)

            def image(b, ahead):
                if ahead:
                    sp.wait_ge(x2_ready, 8 * b + 8)
                    load_x(b + 1)
                    mix_bounce(b + 1)
                store(b, 0)
                if ahead:
                    agent_bounce(b + 1)
                store(b, 1)

            with sp.Fori(0, B - 1, 1) as b:
                image(b, True)
            image(B - 1, False)
            sp.wait_ge(x2_moved, 16 + 16 * 8 * B)

        @block.gpsimd
        def _(pool):
            links = [0]

            def link(ins, base, carried=True):
                links[0] += 1
                ins.then_inc(pchain, 1)
                pool.wait_ge(pchain, base + links[0])
                if not carried:
                    carry(pool, 0)

            pool.memset(ident[:], 0.0)
            pool.memset(gmean[:], 1.0 / GROUP)
            pool.memset(op_up[:], 1.0)
            for t in (m_bias, agg, at_in):
                pool.memset(t[:], 0.0)
            link(pool.memset(fzero[:], 0.0), 0)
            for i, (r0, r1) in enumerate(WIN):
                for par_j in range(2):
                    c0, c1 = WIN[par_j]
                    n = (r1 - r0) * (c1 - c0)
                    pool.memset(area[:, i, par_j:POOL:2], 1.0 / n)
            link(pool.affine_select(out=ident[:], in_=ident[:], compare_op=ALU.not_equal, fill=1.0, base=0,
                                    pattern=[[-1, P]], channel_multiplier=1), 0)
            gv = gmean[:].rearrange("p (g c) -> p g c", c=GROUP)
            link(pool.affine_select(out=gv, in_=gv, compare_op=ALU.is_ge, fill=0.0, base=0,
                                    pattern=[[-GROUP, P // GROUP], [0, GROUP]], channel_multiplier=1), 0)
            pool.affine_select(out=gv, in_=gv, compare_op=ALU.is_ge, fill=0.0, base=GROUP - 1,
                               pattern=[[GROUP, P // GROUP], [0, GROUP]], channel_multiplier=-1).then_inc(pool_setup, 1)

            def agent_conv(i, base):
                pool.wait_ge(pool_ready, i + 1)
                carry(pool, 0)
                link(pool.tensor_tensor(pooled.rearrange("p t i j -> p t (i j)"), pooled.rearrange("p t i j -> p t (i j)"),
                                        area[:].rearrange("p i j -> p (i j)").rearrange("p (o n) -> p o n", o=1)
                                        .broadcast_to([P, CT, AG]), ALU.mult), base)
                pool.wait_ge(norm_ready, i + 1)
                carry(pool, 0)
                for t in range(CT):
                    ins = pool.tensor_scalar(pooled[:, t], pooled[:, t], rstd[0][:, t:t + 1],
                                             shift[0][:, t:t + 1], ALU.mult, ALU.add)
                ins.then_inc(pn_ready, 1)
                pool.wait_ge(mix_loaded, 16 * i + 16)
                carry(pool, 0)
                link(pool.memset(cpad, 0.0), base, carried=False)
                for t in range(CT):
                    ins = pool.tensor_copy(cpad[:, t, 1:1 + POOL, 1:1 + POOL], mix_in[:, t])
                link(ins, base)
                pool.wait_ge(v_tap, 1)
                for k in range(9):
                    win = cpad[:, :, k // 3:k // 3 + POOL, k % 3:k % 3 + POOL]
                    tap = tapw[:, :, k:k + 1].rearrange("p t (a b) -> p t a b", a=1).broadcast_to([P, CT, POOL, POOL])
                    if k == 0:
                        link(pool.tensor_tensor(conv, win, tap, ALU.mult), base)
                    else:
                        link(pool.tensor_tensor(ctmp, win, tap, ALU.mult), base)
                        link(pool.tensor_tensor(conv, conv, ctmp, ALU.add), base)
                c3 = conv.rearrange("p t i j -> p t (i j)")
                tb = tapb[:].rearrange("p (t o) -> p t o", o=1).broadcast_to([P, CT, AG])
                link(pool.tensor_tensor(c3, c3, tb, ALU.add), base, carried=False)
                pool.tensor_scalar(c3, c3, 0.0, None, ALU.max).then_inc(conv_ready, 1)

            agent_conv(0, 0)
            assert links[0] == PCHAIN_BEFORE, ("PCHAIN_BEFORE", links[0])

            def image(b, ahead):
                links[0] = 0
                base = PCHAIN_BEFORE + PCHAIN_IMAGE * b
                for n in range(NT):
                    pool.wait_ge(qrec_ready, NT * b + n + 1)
                    e = qp[:, n % 4, :].rearrange("p (h a) -> p h a", h=HEADS)
                    r = qsum[:, n % 2, :].rearrange("p (h o) -> p h o", o=1).broadcast_to([P, HEADS, AG])
                    pool.tensor_tensor(e, e, r, ALU.mult).then_inc(qp_ready, 1)
                pool.wait_ge(agg_made, b + 1)
                carry(pool, 0)
                for t in range(CT):
                    pool.memset(xpad_run[:, t, :, 0:5 * WW], 0.0)
                    pool.memset(xpad_run[:, t, :, (5 + H) * WW:BAND_N], 0.0)
                    pool.memset(xpad[:, t, 0, 5:5 + H, 0:SPANS[0][1]], 0.0)
                    ins = pool.memset(xpad[:, t, len(COLS) - 1, 5:5 + H, SPANS[-1][2]:WW], 0.0)
                ins.then_inc(border_ready, 1)
                if ahead:
                    agent_conv(b + 1, base)
                    assert links[0] == PCHAIN_IMAGE, ("PCHAIN_IMAGE", links[0])

            with pool.Fori(0, B - 1, 1) as b:
                image(b, True)
            image(B - 1, False)

        @block.scalar
        def _(act):
            def copy(out_, in_, scale=1.0):
                return act.activation(out_, in_, ACT.Copy, scale=scale)

            def norm_x(i, t):
                act.wait_ge(norm_ready, i + 1)
                act.activation(xn[:, t, :], xin[:, t, :], ACT.Identity, scale=rstd[0][:, t:t + 1],
                               bias=shift[0][:, t:t + 1]).then_inc(xn_ready, 1)

            def turn_agents(i):
                act.wait_ge(at_turned, i + 1)
                copy(at_bd, psum[:, 4, 0:AGS].rearrange("p (t a) -> p t a", a=PAIR), SCALE).then_inc(at_ready, 1)

            def g_copy(i, g):
                act.wait_ge(g_made, 8 * i + g + 1)
                copy((g_k if g < CT else g_q)[:, g % CT, :], psum[:, 4 + g % 4, 0:AGS]).then_inc(g_ready[1], 1)

            for t in range(CT):
                norm_x(0, t)
            turn_agents(0)
            for g in range(1, 8, 2):
                g_copy(0, g)

            def image(b, ahead):
                def xT_copy(n):
                    act.wait_ge(xT_made, NT * b + n + 1)
                    copy(xT[:, n, :], psum[:, 4, :]).then_inc(xT_ready[0], 1)

                def k_exp(t):
                    act.wait_ge(kmax_ready, 4 * b + t + 1)
                    s0 = 2 * (t % 2)
                    act.activation(prob[0:PAIR, t % 2, :], psum[0:PAIR, s0:s0 + 2, :].rearrange("p s n -> p (s n)"),
                                   ACT.Exp, bias=kmax[:, t:t + 1], accum_out=ksum[:, t:t + 1]).then_inc(prob_ready, 1)

                def q_exp(n):
                    act.wait_ge(qsub_ready, NT * b + n + 1)
                    act.activation(qp[:, n % 4, :], qp[:, n % 4, :], ACT.Exp).then_inc(qexp_ready, 1)

                def px_copy(t):
                    act.wait_ge(px_made, 4 * b + t + 1)
                    copy(pxT[:, t, :], psum[:, t, 0:AGS]).then_inc(px_ready, 1)

                def qT_copy(n):
                    act.wait_ge(qT_made, NT * b + n + 1)
                    copy(qT[0:PAIR, :, P * n:P * n + P], psum[0:PAIR, 6, :].rearrange("p (t n) -> p t n", t=4))\
                        .then_inc(qT_ready[0], 1)

                for t in range(4):
                    xT_copy(2 * t)
                    k_exp(t)
                for n in range(4):
                    q_exp(n)
                px_copy(0)
                qT_copy(0)
                q_exp(4)
                px_copy(1)
                q_exp(5)
                px_copy(2)
                qT_copy(2)
                q_exp(6)
                px_copy(3)
                q_exp(7)
                qT_copy(4)
                qT_copy(6)
                act.wait_ge(krec_ready, b + 1)
                for t in range(4):
                    act.wait_ge(f_made, 4 * b + t + 1)
                    copy(f_mat[0:PAIR, t, :], psum[0:PAIR, 4 + t, :], krec[:, t:t + 1]).then_inc(f_ready, 1)
                for i in range(8):
                    nh, f = i // 4, i % 4
                    act.wait_ge(h1_made, 8 * b + i + 1)
                    act.activation(h1T[:, f, HALF * nh:HALF * nh + HALF], psum[:, i % 4, :], ACT.Relu,
                                   bias=b1p[:, f:f + 1]).then_inc(h1_ready, 1)
                act.wait_ge(norm1_ready, b + 1)
                for t in (0, 2):
                    for n, (c0, at, cn) in enumerate(SPANS):
                        ins = act.activation(xpad[:, t, n, 5:5 + H, at:at + cn],
                                             x2[:, t, :].rearrange("p (h w) -> p h w", h=H)[:, :, c0:c0 + cn],
                                             ACT.Identity, scale=rstd[1][:, t:t + 1], bias=shift[1][:, t:t + 1])
                    ins.then_inc(xpad_ready[0], 1)

                def win_copy(p):
                    act.wait_ge(win_made, NPATCH * b + p + 1)
                    copy(xwin[0:WIN_N, p % XSLOTS, :], psum[0:WIN_N, 4 + p % 2, :]).then_inc(win_ready, 1)

                def relu(p):
                    act.wait_ge(up_made, NPATCH * b + p + 1)
                    k = PATCHES[p][2]
                    act.activation(ypt[0:k, y_slot(p), :], psum[0:k, 6 + p % 2, :], ACT.Relu, scale=1.0 - SLOPE)\
                        .then_inc(relu_ready, 1)

                win_copy(0)
                win_copy(1)
                relu(0)
                for s in range(NPATCH):
                    if s + 2 < NPATCH:
                        win_copy(s + 2)
                    if s + 1 < NPATCH:
                        relu(s + 1)
                    if ahead:
                        if s in range(XN_AT, XN_AT + 2 * CT, 2):
                            norm_x(b + 1, (s - XN_AT) // 2)
                        if s == TURN_AT:
                            turn_agents(b + 1)
                if ahead:
                    for g in range(1, 8, 2):
                        g_copy(b + 1, g)

            act.wait_ge(v_b1, 1)
            with act.Fori(0, B - 1, 1) as b:
                image(b, True)
            image(B - 1, False)

        @block.vector
        def _(dve):
            links = [0]

            def link(ins, base, carried=True):
                links[0] += 1
                ins.then_inc(chain, 1)
                dve.wait_ge(chain, base + links[0])
                if not carried:
                    carry(dve, 1)

            def rsqrt(v, y, base):
                link(dve.tensor_scalar(nt1[:].bitcast(U32), v.bitcast(U32), 1, None, ALU.logical_shift_right), base)
                link(dve.tensor_scalar(y.bitcast(I32), nt1[:].bitcast(I32), -1.0, float(0x5F3759DF), ALU.mult, ALU.add), base)
                link(dve.tensor_scalar(v, v, -0.5, None, ALU.mult), base)
                for _ in range(4):
                    link(dve.tensor_tensor(nt1[:], y, v, ALU.mult), base)
                    link(dve.tensor_tensor(nt2[:], nt1[:], y, ALU.mult), base)
                    link(dve.scalar_tensor_tensor(y, nt2[:], 1.5, y, ALU.add, ALU.mult), base)

            def bn_stats(src, t, half, base, done=None):
                ins = dve.bn_stats(bns[:, t, half, :], src[:, t, HALF * half:HALF * half + HALF])
                return ins

            def channel_stats(base, ready):
                for t in range(CT):
                    ins = dve.bn_aggr(stat[:, t, :], bns[:, t])
                link(ins, base)
                link(dve.tensor_tensor(nt1[:], stat[:, :, 0], stat[:, :, 0], ALU.mult), base)
                dve.tensor_tensor(stat[:, :, 1], stat[:, :, 1], nt1[:], ALU.add).then_inc(ready, 1)

            def group_norm(i, bank, which, base, ready):
                dve.tensor_copy(gs[:].rearrange("p t s -> p (t s)"), psum[:, bank, 0:2 * CT]).then_inc(gs_read[which], 1)
                dve.wait_ge(gs_read[which], i + 1)
                link(dve.tensor_tensor(nt1[:], gs[:, :, 0], gs[:, :, 0], ALU.mult), base)
                link(dve.scalar_tensor_tensor(nv[:], gs[:, :, 1], GN_EPS, nt1[:], ALU.add, ALU.subtract), base)
                rsqrt(nv[:], rstd[which][:], base)
                dve.scalar_tensor_tensor(shift[which][:], gs[:, :, 0], -1.0, rstd[which][:], ALU.mult, ALU.mult)\
                    .then_inc(ready, 1)

            def pool_rows(i_img, i):
                r0, r1 = WIN[i]
                src = xin[:].rearrange("p t (h w) -> p t w h", h=H)[:, :, :, r0:r1]
                return dve.tensor_reduce(rowsum[:, :, i, :], src, AX.X, ALU.add)

            def pool_cols(j):
                c0, c1 = WIN[j]
                return dve.tensor_reduce(pooled.rearrange("p t i j -> p (t i) j")[:, :, j:j + 1],
                                         rowsum.rearrange("p t i w -> p (t i) w")[:, :, c0:c1], AX.X, ALU.add)

            def mix_copy(i, bank):
                dve.wait_ge(mix_made, i + 1)
                dve.tensor_copy(mix_out, psum[0:AG, bank, :]).then_inc(mix_ready, 1)

            def pwo_copy(i, bank, first=False):
                dve.wait_ge(pw_ready, i + 1)
                if not first:
                    dve.wait_ge(at_loaded, 32 * i)
                dve.tensor_tensor(pwo, psum[:, bank, 0:CT * AG].rearrange("p (t a) -> p t a", t=CT),
                                  par[:, 5, :].rearrange("p (t o) -> p t o", o=1).broadcast_to([P, CT, AG]), ALU.add)\
                    .then_inc(pwo_ready, 1)

            def g_copy(i, g):
                dve.wait_ge(g_made, 8 * i + g + 1)
                dve.tensor_copy((g_k if g < CT else g_q)[:, g % CT, :], psum[:, 4 + g % 4, 0:AGS]).then_inc(g_ready[0], 1)

            dve.wait_ge(f_load, 16 * 2 * (WH + WW))
            dve.wait_ge(pool_setup, 1)
            for j, (dst, gain) in enumerate(((op_up[0:WIN_N, :], 4.0), (x2[0:WIN_N, 1, 0:PT_N], ROOT2))):
                ins = dve.scalar_tensor_tensor(
                    dst.rearrange("p (r s) -> p r s", r=2 * MR),
                    frow[j].rearrange("p (r o) -> p r o", o=1).broadcast_to([WIN_N, 2 * MR, 2 * MC]), gain,
                    fcol[j].rearrange("p (o s) -> p o s", o=1).broadcast_to([WIN_N, 2 * MR, 2 * MC]), ALU.mult, ALU.mult)
            ins.then_inc(v_op, 1)
            dve.wait_ge(w_load, 16 * 17)
            link(dve.tensor_scalar(nv[:], par[:, 4, :], BN_EPS, None, ALU.add), 0)
            rsqrt(nv[:], ny[:], 0)
            link(dve.tensor_tensor(ny[:], ny[:], par[:, 1, :], ALU.mult), 0)
            link(dve.tensor_tensor(nt1[:], par[:, 0, :], par[:, 3, :], ALU.subtract), 0)
            link(dve.tensor_tensor(nt1[:], nt1[:], ny[:], ALU.mult), 0)
            link(dve.tensor_tensor(tapb[:], nt1[:], par[:, 2, :], ALU.add), 0)
            dve.tensor_tensor(tapw[:], tapw[:], ny[:].rearrange("p (t o) -> p t o", o=1).broadcast_to([P, CT, 9]),
                              ALU.mult).then_inc(v_tap, 1)
            dve.wait_ge(x2_moved, 16)
            dve.wait_ge(row_load, 16 * ROW_LOADS)
            dve.tensor_tensor(m_bias[0:AG, :], m_bias[0:AG, :], x2[0:AG, 0, 0:C], ALU.add).then_inc(v_bias, 1)
            for t in range(CT):
                dve.wait_ge(pe_p1, t + 1)
                dve.tensor_copy(w_p1[:, t, :], psum[:, t, :]).then_inc(v_p1, 1)
            dve.wait_ge(pe_b1, 1)
            dve.tensor_tensor(b1p[:], psum[:, 4, 0:CT], par[:, 6, :], ALU.add).then_inc(v_b1, 1)
            dve.wait_ge(pe_dn, 1)
            dve.tensor_copy(op_dn[:].rearrange("p a b -> p (a b)"), psum[:, 5, 0:WIN_N]).then_inc(v_dn, 1)
            dve.wait_ge(x_loaded, 16 * CT)
            for t in range(CT):
                for half in range(2):
                    ins = bn_stats(xin, t, half, 0)
            link(ins, 0)
            channel_stats(0, stat_ready)
            for i in range(POOL):
                ins = pool_rows(0, i)
            link(ins, 0)
            for j in range(POOL):
                ins = pool_cols(j)
            ins.then_inc(pool_ready, 1)
            dve.wait_ge(gstat_ready, 1)
            group_norm(0, 4, 0, 0, norm_ready)
            mix_copy(0, 7)
            pwo_copy(0, 5, first=True)
            for g in range(0, 8, 2):
                g_copy(0, g)
            assert links[0] == CHAIN_BEFORE, ("CHAIN_BEFORE", links[0])

            def image(b, ahead):
                links[0] = 0
                base = CHAIN_BEFORE + CHAIN_IMAGE * b

                def k_max(t):
                    dve.wait_ge(sk_ready, 4 * b + t + 1)
                    s0 = 2 * (t % 2)
                    dve.tensor_reduce(kmax[:, t:t + 1], psum[0:PAIR, s0:s0 + 2, :].rearrange("p s n -> p (s n)"),
                                      AX.X, ALU.max, negate=True).then_inc(kmax_ready, 1)

                def xT_copy(n):
                    dve.wait_ge(xT_made, NT * b + n + 1)
                    dve.tensor_copy(xT[:, n, :], psum[:, 5, :]).then_inc(xT_ready[1], 1)

                def pT_copy(t):
                    for q in range(2):
                        dve.wait_ge(pT_made, 8 * b + 2 * t + q + 1)
                        dve.tensor_copy(pT[:, 4 * q:4 * q + 4, PAIR * t:PAIR * t + PAIR],
                                        psum[:, 6 + q, 0:AGS].rearrange("p (n a) -> p n a", a=PAIR)).then_inc(pT_ready, 1)

                def q_sub(n):
                    dve.wait_ge(sq_made, NT * b + n + 1)
                    s = psum[:, 4 + n % 2, 0:AGS].rearrange("p (h a) -> p h a", h=HEADS)
                    link(dve.tensor_reduce(qmax[:, n % 2, :].rearrange("p (h o) -> p h o", o=1), s, AX.X, ALU.max), base)
                    dve.tensor_tensor(qp[:, n % 4, :].rearrange("p (h a) -> p h a", h=HEADS), s,
                                      qmax[:, n % 2, :].rearrange("p (h o) -> p h o", o=1).broadcast_to([P, HEADS, AG]),
                                      ALU.subtract).then_inc(qsub_ready, 1)

                def q_sum(n):
                    dve.wait_ge(qexp_ready, NT * b + n + 1)
                    if n >= 2:
                        dve.wait_ge(qp_ready, NT * b + n - 1)
                    link(dve.tensor_reduce(qsum[:, n % 2, :].rearrange("p (h o) -> p h o", o=1),
                                           qp[:, n % 4, :].rearrange("p (h a) -> p h a", h=HEADS), AX.X, ALU.add), base)
                    dve.reciprocal(qsum[:, n % 2, :], qsum[:, n % 2, :]).then_inc(qrec_ready, 1)

                def qT_copy(n):
                    dve.wait_ge(qT_made, NT * b + n + 1)
                    dve.tensor_copy(qT[0:PAIR, :, P * n:P * n + P], psum[0:PAIR, 7, :].rearrange("p (t n) -> p t n", t=4))\
                        .then_inc(qT_ready[1], 1)

                k_max(0)
                xT_copy(1)
                k_max(1)
                xT_copy(3)
                pT_copy(0)
                k_max(2)
                xT_copy(5)
                pT_copy(1)
                k_max(3)
                xT_copy(7)
                pT_copy(2)
                q_sub(0)
                q_sub(1)
                q_sum(0)
                pT_copy(3)
                for n in range(2, 5):
                    q_sub(n)
                    q_sum(n - 1)
                qT_copy(1)
                q_sub(5)
                q_sum(4)
                q_sub(6)
                q_sum(5)
                qT_copy(3)
                q_sub(7)
                q_sum(6)
                q_sum(7)
                dve.wait_ge(prob_ready, 4 * b + 4)
                dve.reciprocal(krec[:], ksum[:]).then_inc(krec_ready, 1)
                qT_copy(5)
                dve.wait_ge(agg_made, b + 1)
                for hh in range(2):
                    r, c = slice(HD * hh, HD * hh + HD), slice(AG * hh, AG * hh + AG)
                    ins = dve.tensor_copy(agg[r, :, c], psum[r, 0, 0:AGS].rearrange("p (t a) -> p t a", a=PAIR)[:, :, c])
                ins.then_inc(agg_ready, 1)
                qT_copy(7)
                dve.wait_ge(krec_ready, b + 1)
                for t in range(4):
                    dve.wait_ge(m_made, 4 * b + t + 1)
                    if t == 0:
                        ins = dve.scalar_tensor_tensor(m_mat[:, 0, :], psum[0:PAIR, 0, :], krec[:, 0:1], m_bias[:],
                                                       ALU.mult, ALU.add)
                    else:
                        ins = dve.tensor_scalar(m_mat[:, t, :], psum[0:PAIR, t, :], krec[:, t:t + 1], None, ALU.mult)
                    ins.then_inc(m_ready, 1)
                dve.wait_ge(x2_moved, 16 + 16 * 8 * b)
                for i in range(NT):
                    t, cs = i // 2, slice(HALF * (i % 2), HALF * (i % 2) + HALF)
                    dve.wait_ge(o_made, NT * b + i + 1)
                    dve.tensor_tensor(x2[:, t, cs], psum[:, 4 + i % 4, :], xin[:, t, cs], ALU.add).then_inc(x2_ready, 1)
                    if i:
                        dve.wait_ge(x2_ready, NT * b + i)
                        bn_stats(x2, (i - 1) // 2, (i - 1) % 2, base)
                dve.wait_ge(x2_ready, NT * b + NT)
                link(bn_stats(x2, CT - 1, 1, base), base, carried=False)
                channel_stats(base, stat1_ready)
                dve.wait_ge(gstat1_ready, b + 1)
                group_norm(b, 0, 1, base, norm1_ready)
                dve.wait_ge(norm1_ready, b + 1)
                for t in (1, 3):
                    for n, (c0, at, cn) in enumerate(SPANS):
                        ins = dve.tensor_scalar(xpad[:, t, n, 5:5 + H, at:at + cn],
                                                x2[:, t, :].rearrange("p (h w) -> p h w", h=H)[:, :, c0:c0 + cn],
                                                rstd[1][:, t:t + 1], shift[1][:, t:t + 1], ALU.mult, ALU.add)
                    ins.then_inc(xpad_ready[1], 1)

                def leaky(p):
                    dve.wait_ge(relu_ready, NPATCH * b + p + 1)
                    y = ypt[0:PATCHES[p][2], y_slot(p), :]
                    dve.scalar_tensor_tensor(y, psum[0:PATCHES[p][2], 6 + p % 2, :], SLOPE, y, ALU.mult, ALU.add)\
                        .then_inc(up_read, 1)

                def clip(p):
                    dve.wait_ge(up_read, NPATCH * b + p + 1)
                    y = ypt[0:PATCHES[p][2], y_slot(p), :]
                    dve.tensor_scalar(y, y, CLAMP / ROOT2, -CLAMP / ROOT2, ALU.min, ALU.max).then_inc(y_ready, 1)

                def z_add(half):
                    dve.wait_ge(z_made, 2 * b + half + 1)
                    cs = slice(HALF * half, HALF * half + HALF)
                    for t in range(CT):
                        dve.tensor_tensor(x2[:, t, cs], psum[:, t, :], x2[:, t, cs], ALU.add).then_inc(z_ready, 1)

                for s in range(NPATCH):
                    leaky(s)
                    if s == KEEP1 + 1:
                        z_add(0)
                    clip(s)
                    if not ahead:
                        continue
                    if BN_AT <= s < BN_AT + 2 * CT:
                        if s == BN_AT:
                            dve.wait_ge(x_loaded, 16 * CT * (b + 2))
                        k = s - BN_AT
                        ins = bn_stats(xin, k // 2, k % 2, base)
                        if s == BN_AT + 2 * CT - 1:
                            link(ins, base, carried=False)
                    if s == AGGR_AT:
                        channel_stats(base, stat_ready)
                    if s == STAT_AT:
                        dve.wait_ge(gstat_ready, b + 2)
                        group_norm(b + 1, 4 + (s + 3) % 2, 0, base, norm_ready)
                    if POOL_AT <= s < POOL_AT + POOL:
                        ins = pool_rows(b + 1, s - POOL_AT)
                        if s == POOL_AT + POOL - 1:
                            link(ins, base)
                            for j in range(POOL):
                                ins = pool_cols(j)
                            ins.then_inc(pool_ready, 1)
                    if s == MIX_AT:
                        mix_copy(b + 1, 4 + (s + 3) % 2)
                    if s == PW_AT:
                        pwo_copy(b + 1, 4 + (s + 3) % 2)
                z_add(1)
                if ahead:
                    for g in range(0, 8, 2):
                        g_copy(b + 1, g)
                    assert links[0] == CHAIN_IMAGE, ("CHAIN_IMAGE", links[0])

            with dve.Fori(0, B - 1, 1) as b:
                image(b, True)
            image(B - 1, False)

        @block.tensor
        def _(pe):
            def mm(out_, lhsT, rhs, start, stop, **kw):
                return pe.matmul(out_, lhsT, rhs, start=start, stop=stop, **kw)

            def group_stats(i, bank, ready, made):
                pe.wait_ge(ready, i + 1)
                mm(psum[:, bank, 0:2 * CT], gmean[:], stat[:].rearrange("p t s -> p (t s)"), True, True).then_inc(made, 1)

            def mix(i, bank):
                pe.wait_ge(pn_ready, i + 1)
                for t in range(CT):
                    ins = mm(psum[0:AG, bank, P * t:P * t + P], pooled[:, t].rearrange("p i j -> p (i j)"), ident[:],
                             True, True)
                ins.then_inc(mix_made, 1)

            def pointwise(i, bank):
                pe.wait_ge(conv_ready, i + 1)
                for o in range(CT):
                    for k in range(CT):
                        ins = mm(psum[:, bank, AG * o:AG * o + AG], w_pwT[:, k, P * o:P * o + P],
                                 conv[:, k].rearrange("p i j -> p (i j)"), k == 0, k == CT - 1)
                ins.then_inc(pw_ready, 1)

            def turn_agents(i):
                pe.wait_ge(at_loaded, 32 * (i + 1))
                for t in range(HEADS // 2):
                    ins = pe.transpose(psum[:, 4, PAIR * t:PAIR * t + PAIR], at_in[:, t, :], ident[0:PAIR, 0:PAIR])
                ins.then_inc(at_turned, 1)

            def fold_agents(i, prior):
                pe.wait_ge(at_ready, i + 1)
                for g in range(8):
                    prior(g)
                    w = w_k if g < CT else w_q
                    for t in range(HEADS // 2):
                        ins = mm(psum[:, 4 + g % 4, PAIR * t:PAIR * t + PAIR], w[:, t, P * (g % CT):P * (g % CT) + P],
                                 at_bd[:, t, :], True, True)
                    ins.then_inc(g_made, 1)

            pe.wait_ge(w_load, 16 * 17)
            for m in range(CT):
                for k in range(CT):
                    ins = mm(psum[:, m, :], pw_in[:, k, P * m:P * m + P], p1_in[:, k, :], k == 0, k == CT - 1)
                ins.then_inc(pe_p1, 1)
            for m in range(CT):
                for k in range(CT):
                    ins = mm(psum[:, 4, m:m + 1], p1_in[:, k, P * m:P * m + P], par[:, 7, k:k + 1], k == 0, k == CT - 1)
            ins.then_inc(pe_b1, 1)
            pe.wait_ge(v_op, 1)
            pe.transpose(psum[:, 5, 0:WIN_N], x2[0:WIN_N, 1, 0:PT_N], ident[0:WIN_N, 0:WIN_N]).then_inc(pe_dn, 1)
            pe.wait_ge(v_b1, 1)
            group_stats(0, 4, stat_ready, gstat_ready)
            pe.wait_ge(v_dn, 1)
            mix(0, 7)
            pointwise(0, 5)
            pe.wait_ge(norm_ready, 1)
            turn_agents(0)
            pe.wait_ge(v_p1, CT)

            def first_prior(g):
                if g == 1:
                    pe.wait_ge(pwo_ready, 1)
                if g >= 4:
                    pe.wait_ge(g_ready[g % 2], (g - 4) // 2 + 1)
            fold_agents(0, first_prior)
            pe.wait_ge(v_bias, 1)

            def image(b, ahead):
                def k_scores(t):
                    if t >= 2:
                        pe.wait_ge(prob_ready, 4 * b + t - 1)
                    for n in range(2):
                        for k in range(CT):
                            ins = mm(psum[0:PAIR, 2 * (t % 2) + n, :], g_k[:, k, PAIR * t:PAIR * t + PAIR],
                                     xn[:, k, HALF * n:HALF * n + HALF], k == 0, k == CT - 1)
                    ins.then_inc(sk_ready, 1)

                def turn_x(n):
                    if n >= 2:
                        pe.wait_ge(xT_ready[n % 2], 4 * b + n // 2)
                    for k in range(CT):
                        ins = pe.transpose(psum[:, 4 + n % 2, P * k:P * k + P], xn[:, k, P * n:P * n + P], ident[:])
                    ins.then_inc(xT_made, 1)

                def turn_p(t):
                    pe.wait_ge(prob_ready, 4 * b + t + 1)
                    for q in range(2):
                        if t:
                            pe.wait_ge(pT_ready, 8 * b + 2 * (t - 1) + q + 1)
                        for n in range(4):
                            ins = pe.transpose(psum[:, 6 + q, PAIR * n:PAIR * n + PAIR],
                                               prob[0:PAIR, t % 2, P * (4 * q + n):P * (4 * q + n) + P], ident[0:PAIR, 0:PAIR])
                        ins.then_inc(pT_made, 1)

                def q_scores(n):
                    if n < 2:
                        pe.wait_ge(xT_ready[n % 2], 4 * b + 4)
                    else:
                        pe.wait_ge(qsub_ready, NT * b + n - 1)
                    for k in range(CT):
                        ins = mm(psum[:, 4 + n % 2, 0:AGS], xn[:, k, token_tile(n)], g_q[:, k, :], k == 0, k == CT - 1)
                    ins.then_inc(sq_made, 1)

                def aggregate_x(t):
                    if t == 0:
                        pe.wait_ge(pT_ready, 8 * b + 8)
                    for n in range(NT):
                        ins = mm(psum[:, t, 0:AGS], xT[:, n, P * t:P * t + P], pT[:, n, :], n == 0, n == NT - 1)
                    ins.then_inc(px_made, 1)

                def turn_q(n):
                    pe.wait_ge(qp_ready, NT * b + n + 1)
                    if n >= 2:
                        pe.wait_ge(qT_ready[n % 2], 4 * b + n // 2)
                    for t in range(4):
                        ins = pe.transpose(psum[0:PAIR, 6 + n % 2, P * t:P * t + P],
                                           qp[:, n % 4, PAIR * t:PAIR * t + PAIR], ident[:])
                    ins.then_inc(qT_made, 1)

                for j in range(2):
                    pe.wait_ge(g_ready[j], 4 * (b + 1))
                pe.wait_ge(xn_ready, CT * (b + 1))
                k_scores(0)
                turn_x(0)
                turn_x(1)
                k_scores(1)
                turn_x(2)
                turn_x(3)
                turn_p(0)
                k_scores(2)
                turn_x(4)
                turn_x(5)
                turn_p(1)
                k_scores(3)
                turn_x(6)
                turn_x(7)
                turn_p(2)
                q_scores(0)
                q_scores(1)
                turn_p(3)
                q_scores(2)
                q_scores(3)
                for t in range(CT):
                    aggregate_x(t)
                    turn_q(t)
                    q_scores(4 + t)
                turn_q(4)
                turn_q(5)
                pe.wait_ge(px_ready, 4 * b + 4)
                for t in range(4):
                    for k in range(CT):
                        ins = mm(psum[:, 0, PAIR * t:PAIR * t + PAIR], w_vT[:, k, P * t:P * t + P],
                                 pxT[:, k, PAIR * t:PAIR * t + PAIR], k == 0, k == CT - 1)
                ins.then_inc(agg_made, 1)
                turn_q(6)
                turn_q(7)
                pe.wait_ge(agg_ready, b + 1)
                for t in range(4):
                    if t == 0:
                        pe.wait_ge(qsub_ready, NT * b + NT)
                    if t >= 2:
                        pe.wait_ge(qT_ready[t % 2], 4 * b + 4)
                    mm(psum[0:PAIR, 4 + t, :], agg[:, t, :], w_p1[:, t, :], True, True).then_inc(f_made, 1)
                for t in range(4):
                    mm(psum[0:PAIR, t, :], agg[:, t, :], w_projT[:, t, :], True, True).then_inc(m_made, 1)
                for i in range(8):
                    nh, f = i // 4, i % 4
                    if i == 0:
                        pe.wait_ge(f_ready, 4 * b + 4)
                    if i < 4:
                        pe.wait_ge(m_ready, 4 * b + i + 1)
                    else:
                        pe.wait_ge(h1_ready, 8 * b + i - 3)
                    for t in range(4):
                        ins = mm(psum[:, i % 4, :], f_mat[0:PAIR, t, P * f:P * f + P],
                                 qT[0:PAIR, t, HALF * nh:HALF * nh + HALF], t == 0, t == 3)
                    ins.then_inc(h1_made, 1)
                for i in range(NT):
                    if i % 4 == 0:
                        pe.wait_ge(h1_ready, 8 * b + i + 4)
                    if i >= 4:
                        pe.wait_ge(x2_ready, NT * b + i - 3)
                    for t in range(4):
                        mm(psum[:, 4 + i % 4, :], qT[0:PAIR, t, P * i:P * i + P], m_mat[:, t, :], t == 0, False)
                    for k in range(CT):
                        ins = mm(psum[:, 4 + i % 4, :], h1T[:, k, P * i:P * i + P], w_2T[:, k, :], False, k == CT - 1)
                    ins.then_inc(o_made, 1)

                def cut(p):
                    if p < 2:
                        pe.wait_ge(x2_ready, NT * b + NT)
                    elif ahead and p - 3 == STAT_AT:
                        pe.wait_ge(gs_read[0], b + 2)
                    elif ahead and p - 3 == MIX_AT:
                        pe.wait_ge(mix_ready, b + 2)
                    elif ahead and p - 3 == PW_AT:
                        pe.wait_ge(pwo_ready, b + 2)
                    else:
                        pe.wait_ge(win_ready, NPATCH * b + p - 1)
                    m, n = PATCHES[p][0], COLS.index(PATCHES[p][1])
                    for t in range(CT):
                        ins = pe.transpose(psum[0:WIN_N, 4 + p % 2, P * t:P * t + P], xpad_run[:, t, n, WW * m:WW * (m + WH)], ident[:])
                    ins.then_inc(win_made, 1)

                def up(p):
                    pe.wait_ge(win_ready, NPATCH * b + p + 1)
                    if p >= 2:
                        pe.wait_ge(up_read, NPATCH * b + p - 1)
                    k = PATCHES[p][2]
                    mm(psum[0:k, 6 + p % 2, :], op_up[:, 0:k], xwin[0:WIN_N + 1, p % XSLOTS, :], True, True)\
                        .then_inc(up_made, 1)

                def down(p, half, t, start, stop):
                    k = PATCHES[p][2]
                    k0, k1, l0, l1, a0, a1, c0, c1 = down_window(p, half)
                    z = psum[:, t, :].rearrange("p (k l) -> p k l", l=W)[:, k0 - 16 * half:k1 - 16 * half, l0:l1]
                    return mm(z, ypt[0:k, y_slot(p), P * t:P * t + P], op_dn[0:k, a0:a1, c0:c1], start, stop,
                              skip_group_check=True)

                group_stats(b, 0, stat1_ready, gstat1_ready)
                pe.wait_ge(border_ready, b + 1)
                for j in range(2):
                    pe.wait_ge(xpad_ready[j], 2 * b + 2)
                cut(0)
                cut(1)
                up(0)
                for s in range(NPATCH + 1):
                    if s + 2 < NPATCH:
                        cut(s + 2)
                    if ahead and s == STAT_AT:
                        pe.wait_ge(win_ready, NPATCH * b + s + 2)
                        group_stats(b + 1, 4 + (s + 3) % 2, stat_ready, gstat_ready)
                    if ahead and s == MIX_AT:
                        pe.wait_ge(win_ready, NPATCH * b + s + 2)
                        mix(b + 1, 4 + (s + 3) % 2)
                    if ahead and s == PW_AT:
                        pe.wait_ge(win_ready, NPATCH * b + s + 2)
                        pointwise(b + 1, 4 + (s + 3) % 2)
                    if ahead and s == TURN_AT:
                        pe.wait_ge(win_ready, NPATCH * (b + 1))
                        turn_agents(b + 1)
                    if s + 1 < NPATCH:
                        up(s + 1)
                    if s == KEEP1 + 1:
                        for t in range(CT):
                            pe.wait_ge(z_ready, 8 * b + t + 1)
                            for p in range(KEEP0, KEEP1):
                                down(p, 1, t, p == KEEP0, False)
                    if s:
                        p = s - 1
                        pe.wait_ge(y_ready, NPATCH * b + p + 1)
                        half = int(p >= KEEP1)
                        for t in range(CT):
                            ins = down(p, half, t, p == 0, p in (KEEP1 - 1, NPATCH - 1))
                        if p in (KEEP1 - 1, NPATCH - 1):
                            ins.then_inc(z_made, 1)
                if ahead:
                    def prior(g):
                        if g < 2:
                            pe.wait_ge(win_ready, NPATCH * (b + 1))
                        elif g < 4:
                            pe.wait_ge(up_read, NPATCH * (b + 1))
                        else:
                            pe.wait_ge(g_ready[g % 2], 4 * (b + 1) + (g - 4) // 2 + 1)
                    fold_agents(b + 1, prior)

            with pe.Fori(0, B - 1, 1) as b:
                image(b, True)
            image(B - 1, False)


def kernel(**inputs):
    import numpy as np
    import concourse.bacc as bacc
    from concourse.bass_utils import run_bass_kernel_spmd as run

    def a(name):
        return np.asarray(inputs[name])

    kv = a("L0_conv_kv_w")
    arrays = {
        "x": a("x").reshape(B, C, N),
        "wq": a("L0_conv_q_w"), "wk": kv[:C], "wvT": kv[C:].T,
        "pwT": a("L0_conv_pw_w").reshape(C, C).T,
        "projT": a("L0_conv_proj_w").T, "proj": a("L0_conv_proj_w"),
        "w1T": a("L0_conv_enh1_w").T, "w2T": a("L0_conv_enh2_w").T,
        "dw_w": a("L0_conv_dw_w").reshape(C, 9), "dw_b": a("L0_conv_dw_b"),
        "bn_g": a("L0_conv_bn_gamma"), "bn_b": a("L0_conv_bn_beta"),
        "bn_m": a("L0_conv_bn_mean"), "bn_v": a("L0_conv_bn_var"),
        "pw_b": a("L0_conv_pw_b"), "proj_b": a("L0_conv_proj_b"),
        "enh1_b": a("L0_conv_enh1_b"), "enh2_b": a("L0_conv_enh2_b"),
        "bias": a("L1_conv_bias"), "up_f": a("L1_conv_up_filter")[::-1], "down_f": a("L1_conv_down_filter"),
    }
    arrays = {f"in_{k}": np.ascontiguousarray(v) for k, v in arrays.items()}
    nc = bacc.Bacc("TRN2", target_bir_lowering=False, num_devices=1)
    args = [nc.dram_tensor(k, v.shape, mybir.dt.from_np(v.dtype), kind="ExternalInput").ap() for k, v in arrays.items()]
    out = nc.dram_tensor("out", (B, C, N), F32, kind="ExternalOutput").ap()
    agent_dram = nc.dram_tensor("agent_scratch", (2, C * AG), F32, kind="Internal").ap()
    filt_dram = nc.dram_tensor("filter_scratch", (2, 44), F32, kind="Internal").ap()
    build(nc, *args, out, agent_dram, filt_dram)
    got = run(nc, [arrays], core_ids=[0]).results[0]["out"]
    return got.reshape(B, C, H, W)
```

```python
from contextlib import ExitStack

import concourse.bass as bass
from concourse import mybir

F32 = mybir.dt.float32
F32R = mybir.dt.float32r
I32 = mybir.dt.int32
U32 = mybir.dt.uint32
ALU = mybir.AluOpType
ACT = mybir.ActivationFunctionType
AX = mybir.AxisListType

P = 128
B, C, H, W = 16, 512, 32, 32
N = H * W
CT = C // P
NT = N // P
HALF = 512
HEADS, POOL = 8, 7
AG = POOL * POOL
PAIR = 2 * AG
AGS = HEADS * AG
HD = C // HEADS
SCALE = float(HD) ** -0.5
GROUP = C // 32
GN_EPS, BN_EPS = 1e-5, 1e-5
SLOPE, CLAMP, ROOT2 = 0.2, 256.0, 2.0 ** 0.5
TAPS = 12
FILT = TAPS + 32

WIN = [(i * H // POOL, -(-(i + 1) * H // POOL)) for i in range(POOL)]

MR, MC = 4, 8
PHASES = (2 * H + TAPS - 2) // 2
WH, WW = MR + 5, MC + 5
WIN_N = WH * WW
PT_N = 4 * MR * MC
ROWS, COLS = range(0, PHASES, MR), range(0, PHASES, MC)
PADH = 5 + ROWS[-1] + MR
SPANS = [(max(0, n - 5), max(0, 5 - n), min(W, n + MC) - max(0, n - 5)) for n in COLS]
PATCHES = [(m, n) for m in ROWS for n in COLS]
ITEMS = len(PATCHES) // 2
STEPS = 2 * ITEMS
RING = 4

CHAIN_BEFORE, CHAIN_IMAGE = 36, 77
PCHAIN_BEFORE, PCHAIN_IMAGE = 24, 27

STAT1_AT, NORM1_AT, PAD1_AT = 1, 2, 8
BN_AT, ROWS_AT, STAT_AT, NORM_AT, XN_AT = 4, 12, 17, 18, 24
MIX_AT, PW_AT, TURN_AT = 27, 42, 47
NORM_PARTS = 6


BANK_ROWS = HALF // W
SECTION_OF = [0 if m - 5 + WH <= BANK_ROWS else 1 if m - 5 < BANK_ROWS else 2 for m, n in PATCHES]
SECTION_PATCHES = [[p for p in range(len(PATCHES)) if SECTION_OF[p] == z] for z in range(3)]
SECTION_ROWS = [(max(0, PATCHES[ps[0]][0] - 5), min(H, PATCHES[ps[-1]][0] - 5 + WH)) for ps in SECTION_PATCHES]
Z_AT = {ITEMS * pair + SECTION_PATCHES[z][-1] // 2 + 2: (pair, z) for pair in range(2) for z in range(3)}
Z_LAST = (1, 2)


def z_bank(pair, z, c):
    return 2 * ((3 * pair + z) % 2) + c


def down_part(p):
    z = SECTION_OF[p]
    k0, l0, first = PATCHES[p][0] - 5, PATCHES[p][1] - 5, SECTION_ROWS[z][0]
    k_lo, k_hi, l_lo, l_hi = max(0, k0), min(H, k0 + WH), max(0, l0), min(W, l0 + WW)
    return (z, slice(k_lo - first, k_hi - first), slice(l_lo, l_hi),
            slice(k_lo - k0, k_hi - k0), slice(l_lo - l0, l_hi - l0))


def build(nc, x, wq, wk, wvT, pwT, projT, proj, w1T, w2T, dw_w, dw_b, bn_g, bn_b, bn_m, bn_v, pw_b,
          proj_b, enh1_b, enh2_b, bias, up_f, down_f, out, agent_dram, filt_dram):
    with ExitStack() as ctx:
        def sb(name, shape, dt=F32):
            return ctx.enter_context(nc.sbuf_tensor(name, shape, dt))

        def overlay(name, shape):
            with nc.sbuf_tensor(name, shape, F32) as full:
                pass
            return full, sb(name + "_r", shape, F32R)

        def sem(name):
            return ctx.enter_context(nc.semaphore(name))

        w_q, w_k, w_vT, w_projT, w_p1 = [sb(n, [P, CT, C]) for n in ("w_q", "w_k", "w_vT", "w_projT", "w_p1")]
        w_2T_hl = sb("w_2T_hl", [P, 2, CT, C], F32R)
        ident = sb("ident", [P, P])
        gmean = sb("gmean", [P, P])
        op_up = sb("op_up", [WIN_N + 2, 2, PT_N])
        op_dn = sb("op_dn", [PT_N, WH, WW])
        m_bias = sb("m_bias", [PAIR, C])
        tapw = sb("tapw", [P, CT, 9])
        par = sb("par", [P, 8, CT])
        tapb = sb("tapb", [P, CT])
        b1p = sb("b1p", [P, CT])
        area = sb("area", [P, POOL, POOL])
        xin = sb("xin", [P, CT, N])
        xn, xn_r = overlay("xn", [P, CT, N])
        x2, x2_r = overlay("x2", [P, CT, N])
        reg_m, reg_m_r = overlay("reg_m", [P, HEADS // 2, C])
        m_hi = reg_m_r[0:PAIR]
        prep = reg_m[:].rearrange("p t c -> p (t c)")
        at_bd = prep[:, 0:AGS].rearrange("p (t a) -> p t a", a=PAIR)
        pooled, conv, ctmp = [prep[:, AGS + k * CT * AG:AGS + (k + 1) * CT * AG]
                              .rearrange("p (t i j) -> p t i j", i=POOL, j=POOL) for k in range(3)]
        MIX = AGS + 4 * CT * AG
        mix_out = prep[0:AG, MIX:MIX + C]
        mix_in = prep[:, MIX + C:MIX + C + CT * AG].rearrange("p (t i j) -> p t i j", i=POOL, j=POOL)
        pwo = prep[:, AGS + 3 * CT * AG:AGS + 4 * CT * AG].rearrange("p (t a) -> p t a", a=AG)
        xwin, reg_f = overlay("xwin", [P, RING, C])
        f_hi = reg_f[0:PAIR]
        reg_a, reg_a_r = overlay("reg_a", [P, NT * C + NT * AGS + 3 * CT * AGS])

        def part(start, *shape, of=reg_a):
            n = 1
            for k in shape:
                n *= k
            names = "abcd"[:len(shape)]
            return of[:, start:start + n].rearrange(f"p ({' '.join(names)}) -> p {' '.join(names)}",
                                                       **dict(zip(names, shape)))

        xT, pT = part(0, NT, C), part(NT * C, NT, AGS)
        pxT, g_k, g_q = [part(NT * (C + AGS) + k * CT * AGS, CT, AGS) for k in range(3)]
        BAND_N = PADH * WW
        XPAD = CT * len(COLS) * BAND_N
        xpad_run = part(0, CT, len(COLS), BAND_N)
        xpad = part(0, CT, len(COLS), BAND_N).rearrange("p t n (h w) -> p t n h w", w=WW)
        LOW = 2 * len(COLS) * BAND_N
        f_lo = part(LOW, CT, C, of=reg_a_r)[0:PAIR]
        m_lo = part(LOW + CT * C, CT, C, of=reg_a_r)[0:PAIR]
        m_tmp = part(LOW + 2 * CT * C, C)[0:PAIR]
        h1_tmp = part(LOW + 2 * CT * C, 2, HALF)
        pw_in, p1_in, w2_in = [part(k * CT * C, CT, C) for k in range(3)]
        reg_y, reg_y_r = overlay("reg_y", [P, 2 * CT * N])
        h1_hi = reg_y_r[:, 0:CT * N].rearrange("p (t n) -> p t n", t=CT)
        h1_lo = xn_r
        qT_hi = reg_y_r[:, CT * N:2 * CT * N].rearrange("p (n t s) -> p n t s", n=NT, t=4)
        qT_lo = x2_r[:].rearrange("p c (h t s) -> p (c h) t s", h=2, t=4)
        kmax_run, ksum_run = reg_y[:, 0:AGS], reg_y[:, AGS:2 * AGS]
        qp = reg_y[:, 2 * N:2 * N + 4 * AGS].rearrange("p (s a) -> p s a", s=4)
        YPT = RING * HALF
        rowsum = reg_y[:, YPT:YPT + CT * POOL * W].rearrange("p (t i w) -> p t i w", t=CT, i=POOL)
        CPAD = YPT + CT * POOL * W
        cpad = reg_y[:, CPAD:CPAD + CT * (POOL + 2) ** 2].rearrange("p (t i j) -> p t i j", t=CT, i=POOL + 2)
        PWT = CPAD + CT * (POOL + 2) ** 2
        w_pwT = reg_y[:, PWT:PWT + CT * C].rearrange("p (t n) -> p t n", t=CT)
        ypt = reg_y[:, 0:RING * HALF].rearrange("p (s c) -> p s c", c=HALF)
        agg = sb("agg", [P, HEADS // 2, PAIR])
        ATI = PWT + CT * C
        at_in = reg_y[0:PAIR, ATI:ATI + CT * P].rearrange("p (t d) -> p t d", t=HEADS // 2)
        kmax = sb("kmax", [PAIR, HEADS // 2])
        ones = sb("ones", [P, 1])
        krec = sb("krec", [PAIR, HEADS // 2])
        qmax, qsum = sb("qmax", [P, 2, HEADS]), sb("qsum", [P, 2, HEADS])
        bns = sb("bns", [P, CT, 2, 6])
        stat = sb("stat", [P, CT, 2])
        gs = sb("gs", [P, CT, 2])
        small = sb("small", [P, 8, CT])
        nv, ny, nt1, nt2 = [small[:, k, :] for k in range(4)]
        rstd, shift = [small[:, 4 + k, :] for k in range(2)], [small[:, 6 + k, :] for k in range(2)]

        idle = [sb(f"idle{j}", [P, 8]) for j in range(2)]
        carried = [0, 0]
        fzero = x2[0:2, 1, HALF:HALF + FILT]
        frow = [x2[0:WIN_N, 2, 2 * MR * j:2 * MR * j + 2 * MR] for j in range(2)]
        fcol = [x2[0:WIN_N, 3, 2 * MC * j:2 * MC * j + 2 * MC] for j in range(2)]
        psum = ctx.enter_context(nc.psum_tensor("psum", [P, 8, HALF], F32))

        par_load, row_load = sem("par_load"), sem("row_load")
        p1_load, kq_load, v_load, proj_load, w2_load = [sem(n) for n in ("p1_load", "kq_load", "v_load", "proj_load", "w2_load")]
        f_store, f_load = sem("f_store"), sem("f_load")
        pool_setup = sem("pool_setup")
        w_split, pw_load = sem("w_split"), sem("pw_load")
        h1_full, h1_low = sem("h1_full"), sem("h1_low")
        f_low, m_high, m_low, qT_low = sem("f_low"), sem("m_high"), sem("m_low"), sem("qT_low")
        v_op, v_tap, v_p1, v_b1, v_dn, v_bias = [sem(n) for n in ("v_op", "v_tap", "v_p1", "v_b1", "v_dn", "v_bias")]
        pe_p1, pe_b1, pe_dn = sem("pe_p1"), sem("pe_b1"), sem("pe_dn")
        chain, pchain = sem("v_chain"), sem("pool_chain")
        x_first = [sem(f"x_first{t}") for t in range(CT)]
        x_loaded, x2_moved = sem("x_loaded"), sem("x2_moved")
        stat_ready, gstat_ready, norm_ready = sem("stat_ready"), sem("gstat_ready"), sem("norm_ready")
        stat1_ready, gstat1_ready, norm1_ready = sem("stat1_ready"), sem("gstat1_ready"), sem("norm1_ready")
        gs_read = [sem("gs0_read"), sem("gs1_read")]
        xn_ready, pool_ready, conv_ready = sem("xn_ready"), sem("pool_ready"), sem("conv_ready")
        pn_ready, mix_made, mix_ready, mix_stored, mix_loaded = (
            sem("pn_ready"), sem("mix_made"), sem("mix_ready"), sem("mix_stored"), sem("mix_loaded"))
        pw_ready, pwo_ready = sem("pw_ready"), sem("pwo_ready")
        at_stored, at_loaded, at_turned, at_ready = sem("at_stored"), sem("at_loaded"), sem("at_turned"), sem("at_ready")
        g_made = sem("g_made")
        g_ready = [sem("g_ready_dve"), sem("g_ready_act")]
        sk_made, sT_ready, kmax_run_ready = sem("sk_made"), sem("sT_ready"), sem("kmax_run_ready")
        kmax_turned, kmax_ready, kmax_spread = sem("kmax_turned"), sem("kmax_ready"), sem("kmax_spread")
        ksub_ready, kexp_ready, ksum_run_ready, ksum_made = sem("ksub_ready"), sem("kexp_ready"), sem("ksum_run_ready"), sem("ksum_made")
        xT_made = sem("xT_made")
        xT_ready = [sem("xT_ready_act"), sem("xT_ready_dve")]
        krec_ready = sem("krec_ready")
        sq_made, qsub_ready, qexp_ready, qrec_ready, qp_ready = (
            sem("sq_made"), sem("qsub_ready"), sem("qexp_ready"), sem("qrec_ready"), sem("qp_ready"))
        px_made, px_ready, agg_made, agg_ready = sem("px_made"), sem("px_ready"), sem("agg_made"), sem("agg_ready")
        f_made, f_ready, m_made, m_ready = sem("f_made"), sem("f_ready"), sem("m_made"), sem("m_ready")
        qT_made = sem("qT_made")
        qT_ready = [sem("qT_ready_act"), sem("qT_ready_dve")]
        h1_made, h1_ready, o_made, x2_ready = sem("h1_made"), sem("h1_ready"), sem("o_made"), sem("x2_ready")
        border_ready = sem("border_ready")
        xpad_ready = [sem("xpad_ready_act"), sem("xpad_ready_dve")]
        win_made, win_ready = sem("win_made"), sem("win_ready")
        up_made, relu_ready, up_read = sem("up_made"), sem("relu_ready"), sem("up_read")
        y_ready = sem("y_ready")
        z_made, z_ready = sem("z_made"), sem("z_ready")

        ctx.enter_context(nc.allow_non_contiguous_dma(reason="weights and small layouts"))
        block = ctx.enter_context(nc.Block())

        def tiles(w):
            return w.rearrange("(t p) n -> p t n", p=P)

        def cols(v):
            return v.rearrange("(t p) -> p t", p=P)

        def row(v):
            return v.rearrange("(a n) -> a n", a=1)

        def token_tile(nt):
            start = 2 * P * (nt // 2) + nt % 2
            return slice(start, start + 2 * P - 1, 2)

        def carry(eng, mine):
            k = carried[mine] % 8
            carried[mine] += 1
            eng.tensor_tensor(idle[mine][:, k:k + 1], ident[:, 0:1], ident[:, 1:2], ALU.mult)

        ROW_LOADS = 1 + 2 * RING

        def flat(ap):
            return ap.rearrange("p t n -> p (t n)")

        @block.sync
        def _(sp):
            def load_x(i, first=False):
                for t in range(CT):
                    sp.dma_start(xin[:, t, :], x[i].rearrange("(t p) n -> t p n", p=P)[t])\
                        .then_inc(x_first[t] if first else x_loaded, 16)

            def load_pw():
                sp.dma_start(w_pwT, tiles(pwT)).then_inc(pw_load, 16)

            def mix_bounce(i):
                sp.wait_ge(mix_ready, i + 1)
                sp.dma_start(agent_dram[1].rearrange("(a c) -> a c", a=AG), mix_out).then_inc(mix_stored, 16)
                sp.wait_ge(mix_stored, 16 * i + 16)
                sp.dma_start(mix_in.rearrange("p t i j -> p t (i j)"),
                             agent_dram[1].rearrange("(t p a) -> p t a", t=CT, p=P)).then_inc(mix_loaded, 16)

            def agent_bounce(i, first=False):
                sp.wait_ge(pwo_ready, i + 1)
                sp.dma_start(agent_dram[0].rearrange("(t p a) -> p t a", t=CT, p=P), pwo).then_inc(at_stored, 16)
                sp.wait_ge(at_stored, 16 * i + 16)
                if not first:
                    sp.wait_ge(at_turned, i)
                for hh in range(2):
                    src = agent_dram[0].rearrange("(t h i d) -> h i t d", t=HEADS // 2, h=2, i=AG)[hh]
                    sp.dma_start(at_in[AG * hh:AG * hh + AG, :, HD * hh:HD * hh + HD], src).then_inc(at_loaded, 16)

            def store(b, pair, half):
                sp.wait_ge(z_ready, 12 * b + 6 * pair + (4 if half == 0 else 6))
                for c in range(2):
                    t = 2 * pair + c
                    sp.dma_start(out[b].rearrange("(t p) n -> t p n", p=P)[t, :, HALF * half:HALF * half + HALF],
                                 x2[:, t, HALF * half:HALF * half + HALF]).then_inc(x2_moved, 16)

            load_x(0, first=True)
            sp.wait_ge(pool_setup, 1)
            sp.dma_start(m_bias[0:AG, :], row(proj_b).broadcast_to([AG, C])).then_inc(row_load, 16)
            sp.dma_start(x2[0:AG, 0, 0:C], row(enh2_b).broadcast_to([AG, C])).then_inc(x2_moved, 16)
            for pair in range(2):
                half_bias = bias[2 * P * pair:2 * P * pair + 2 * P].rearrange("(a b n) -> a b n", a=1, b=1)
                for k in range(RING):
                    sp.dma_start(xwin[WIN_N + pair:WIN_N + pair + 1, k, :].rearrange("p (j c) -> p j c", j=2),
                                 half_bias.broadcast_to([1, 2, 2 * P])).then_inc(row_load, 16)
            sp.dma_start(filt_dram, fzero).then_inc(f_store, 16)
            sp.wait_ge(f_store, 16)
            for j, f in enumerate((up_f, down_f)):
                sp.dma_start(filt_dram[j:j + 1, 16:16 + TAPS], row(f)).then_inc(f_store, 16)
            sp.wait_ge(f_store, 48)
            for j in range(2):
                for dst, start, steps in ((frow[j], 10, [[2, WH], [0, WW], [1, 2 * MR]]),
                                          (fcol[j], 2, [[0, WH], [2, WW], [1, 2 * MC]])):
                    sp.dma_start(dst,
                                 bass.AP(tensor=filt_dram.tensor, offset=FILT * j + start, ap=steps)).then_inc(f_load, 16)
            mix_bounce(0)
            agent_bounce(0, first=True)

            def image(b, ahead):
                if ahead:
                    sp.wait_ge(x2_ready, 8 * b + 8)
                    load_x(b + 1)
                    load_pw()
                store(b, 0, 0)
                store(b, 0, 1)
                if ahead:
                    mix_bounce(b + 1)
                store(b, 1, 0)
                if ahead:
                    agent_bounce(b + 1)
                store(b, 1, 1)

            with sp.Fori(0, B - 1, 1) as b:
                image(b, True)
            image(B - 1, False)
            sp.wait_ge(x2_moved, 16 + 16 * 8 * B)

        @block.gpsimd
        def _(pool):
            links = [0]

            def link(ins, base, carried=True):
                links[0] += 1
                ins.then_inc(pchain, 1)
                pool.wait_ge(pchain, base + links[0])
                if not carried:
                    carry(pool, 0)

            pool.memset(ident[:], 0.0)
            pool.memset(gmean[:], 1.0 / GROUP)
            pool.memset(ones[:], 1.0)
            pool.memset(op_up[:], 1.0)
            for t in (m_bias, agg):
                pool.memset(t[:], 0.0)
            link(pool.memset(fzero, 0.0), 0)
            for i, (r0, r1) in enumerate(WIN):
                for par_j in range(2):
                    c0, c1 = WIN[par_j]
                    n = (r1 - r0) * (c1 - c0)
                    pool.memset(area[:, i, par_j:POOL:2], 1.0 / n)
            link(pool.affine_select(out=ident[:], in_=ident[:], compare_op=ALU.not_equal, fill=1.0, base=0,
                                    pattern=[[-1, P]], channel_multiplier=1), 0)
            gv = gmean[:].rearrange("p (g c) -> p g c", c=GROUP)
            link(pool.affine_select(out=gv, in_=gv, compare_op=ALU.is_ge, fill=0.0, base=0,
                                    pattern=[[-GROUP, P // GROUP], [0, GROUP]], channel_multiplier=1), 0)
            pool.affine_select(out=op_up[:, 0], in_=op_up[:, 0], compare_op=ALU.is_ge, fill=0.0, base=WIN_N,
                               pattern=[[0, PT_N]], channel_multiplier=-1)
            pool.affine_select(out=op_up[:, 1], in_=op_up[:, 1], compare_op=ALU.is_ge, fill=0.0, base=-WIN_N - 1,
                               pattern=[[0, PT_N]], channel_multiplier=1)
            pool.affine_select(out=gv, in_=gv, compare_op=ALU.is_ge, fill=0.0, base=GROUP - 1,
                               pattern=[[GROUP, P // GROUP], [0, GROUP]], channel_multiplier=-1).then_inc(pool_setup, 1)

            def agent_conv(i, base):
                pool.wait_ge(pool_ready, i + 1)
                carry(pool, 0)
                pool.memset(at_in, 0.0)
                link(pool.tensor_tensor(pooled.rearrange("p t i j -> p t (i j)"), pooled.rearrange("p t i j -> p t (i j)"),
                                        area[:].rearrange("p i j -> p (i j)").rearrange("p (o n) -> p o n", o=1)
                                        .broadcast_to([P, CT, AG]), ALU.mult), base)
                pool.wait_ge(norm_ready, i + 1)
                carry(pool, 0)
                for t in range(CT):
                    ins = pool.tensor_scalar(pooled[:, t], pooled[:, t], rstd[0][:, t:t + 1],
                                             shift[0][:, t:t + 1], ALU.mult, ALU.add)
                ins.then_inc(pn_ready, 1)
                pool.wait_ge(mix_loaded, 16 * i + 16)
                carry(pool, 0)
                link(pool.memset(cpad, 0.0), base, carried=False)
                for t in range(CT):
                    ins = pool.tensor_copy(cpad[:, t, 1:1 + POOL, 1:1 + POOL], mix_in[:, t])
                link(ins, base)
                pool.wait_ge(v_tap, 1)
                for k in range(9):
                    win = cpad[:, :, k // 3:k // 3 + POOL, k % 3:k % 3 + POOL]
                    tap = tapw[:, :, k:k + 1].rearrange("p t (a b) -> p t a b", a=1).broadcast_to([P, CT, POOL, POOL])
                    if k == 0:
                        link(pool.tensor_tensor(conv, win, tap, ALU.mult), base)
                    else:
                        link(pool.tensor_tensor(ctmp, win, tap, ALU.mult), base)
                        link(pool.tensor_tensor(conv, conv, ctmp, ALU.add), base)
                c3 = conv.rearrange("p t i j -> p t (i j)")
                tb = tapb[:].rearrange("p (t o) -> p t o", o=1).broadcast_to([P, CT, AG])
                link(pool.tensor_tensor(c3, c3, tb, ALU.add), base, carried=False)
                pool.tensor_scalar(c3, c3, 0.0, None, ALU.max).then_inc(conv_ready, 1)

            agent_conv(0, 0)
            assert links[0] == PCHAIN_BEFORE, ("PCHAIN_BEFORE", links[0])

            def image(b, ahead):
                links[0] = 0
                base = PCHAIN_BEFORE + PCHAIN_IMAGE * b
                for n in range(NT):
                    pool.wait_ge(qrec_ready, NT * b + n + 1)
                    e = qp[:, n % 4, :].rearrange("p (h a) -> p h a", h=HEADS)
                    r = qsum[:, n % 2, :].rearrange("p (h o) -> p h o", o=1).broadcast_to([P, HEADS, AG])
                    pool.tensor_tensor(e, e, r, ALU.mult).then_inc(qp_ready, 1)
                    if n == 1:
                        pool.wait_ge(kexp_ready, NT * b + NT)
                        for k in range(1, NT):
                            ins = pool.tensor_tensor(ksum_run, pT[:, 0, :] if k == 1 else ksum_run, pT[:, k, :], ALU.add)
                            if k < NT - 1:
                                link(ins, base)
                        ins.then_inc(ksum_run_ready, 1)

                def border(t):
                    pool.memset(xpad_run[:, t, :, 0:5 * WW], 0.0)
                    pool.memset(xpad_run[:, t, :, (5 + H) * WW:BAND_N], 0.0)
                    pool.memset(xpad[:, t, 0, 5:5 + H, 0:SPANS[0][1]], 0.0)
                    pool.memset(xpad[:, t, len(COLS) - 1, 5:5 + H, SPANS[-1][2]:WW], 0.0).then_inc(border_ready, 1)

                pool.wait_ge(agg_made, b + 1)
                carry(pool, 0)
                border(0)
                border(1)
                for i in range(8):
                    nh, f = i // 4, i % 4
                    cs = slice(HALF * nh, HALF * nh + HALF)
                    pool.wait_ge(h1_full, 8 * b + i + 1)
                    pool.tensor_tensor(h1_lo[:, f, cs], h1_tmp[:, i % 2, :], h1_hi[:, f, cs].bitcast(F32), ALU.subtract)\
                        .then_inc(h1_low, 1)

                pool.wait_ge(x2_ready, NT * b + NT)
                carry(pool, 0)
                border(2)
                border(3)
                if ahead:
                    agent_conv(b + 1, base)
                if ahead:
                    assert links[0] == PCHAIN_IMAGE, ("PCHAIN_IMAGE", links[0])

            with pool.Fori(0, B - 1, 1) as b:
                image(b, True)
            image(B - 1, False)

        @block.scalar
        def _(act):
            def copy(out_, in_, scale=1.0):
                return act.activation(out_, in_, ACT.Copy, scale=scale)

            def norm_x(i, t):
                act.wait_ge(norm_ready, i + 1)
                act.activation(xn[:, t, :], xin[:, t, :], ACT.Identity, scale=rstd[0][:, t:t + 1],
                               bias=shift[0][:, t:t + 1]).then_inc(xn_ready, 1)

            def turn_agents(i):
                act.wait_ge(at_turned, i + 1)
                copy(at_bd, psum[:, 1, 0:AGS].rearrange("p (t a) -> p t a", a=PAIR), SCALE).then_inc(at_ready, 1)

            def g_copy(i, g):
                act.wait_ge(g_made, 8 * i + g + 1)
                copy((g_k if g < CT else g_q)[:, g % CT, :], psum[:, 4 + g % 4, 0:AGS]).then_inc(g_ready[1], 1)

            act.dma_start(tapw[:], dw_w.rearrange("(t p) k -> p t k", p=P)).then_inc(par_load, 16)
            for j, v in enumerate((dw_b, bn_g, bn_b, bn_m, bn_v, pw_b, enh1_b, proj_b)):
                act.dma_start(par[:, j, :], cols(v)).then_inc(par_load, 16)
            for dst, src, loaded in ((pw_in, proj, p1_load), (p1_in, w1T, p1_load), (w_pwT, pwT, pw_load), (w_k[:], wk, kq_load),
                                     (w_q[:], wq, kq_load), (w_vT[:], wvT, v_load), (w_projT[:], projT, proj_load),
                                     (w2_in, w2T, w2_load)):
                act.dma_start(dst, tiles(src)).then_inc(loaded, 16)
            for t in range(CT):
                norm_x(0, t)
            turn_agents(0)
            for g in range(1, 8, 2):
                g_copy(0, g)

            def image(b, ahead):
                def xT_copy(n):
                    act.wait_ge(xT_made, NT * b + n + 1)
                    copy(xT[:, n, :], psum[:, 4, :]).then_inc(xT_ready[0], 1)

                def sT_copy(n):
                    act.wait_ge(sk_made, NT * b + n + 1)
                    copy(pT[:, n, :], psum[:, n % 4, 0:AGS]).then_inc(sT_ready, 1)

                def k_exp(n):
                    act.wait_ge(ksub_ready, NT * b + n + 1)
                    act.activation(pT[:, n, :], pT[:, n, :], ACT.Exp).then_inc(kexp_ready, 1)

                def q_exp(n):
                    act.wait_ge(qsub_ready, NT * b + n + 1)
                    act.activation(qp[:, n % 4, :], qp[:, n % 4, :], ACT.Exp).then_inc(qexp_ready, 1)

                def px_copy(t):
                    act.wait_ge(px_made, 4 * b + t + 1)
                    copy(pxT[:, t, :], psum[:, t, 0:AGS]).then_inc(px_ready, 1)

                def qT_copy(n):
                    act.wait_ge(qT_made, NT * b + n + 1)
                    copy(qT_hi[0:PAIR, n], psum[0:PAIR, 6, :].rearrange("p (t n) -> p t n", t=4))\
                        .then_inc(qT_ready[0], 1)

                for n in range(NT):
                    sT_copy(n)
                    if n % 2 == 0:
                        xT_copy(n)
                q_exp(0)
                q_exp(1)
                for n in range(NT):
                    k_exp(n)
                q_exp(2)
                q_exp(3)
                px_copy(0)
                qT_copy(0)
                q_exp(4)
                px_copy(1)
                q_exp(5)
                px_copy(2)
                qT_copy(2)
                q_exp(6)
                px_copy(3)
                q_exp(7)
                qT_copy(4)
                qT_copy(6)
                act.wait_ge(krec_ready, b + 1)
                for t in range(4):
                    act.wait_ge(f_made, 4 * b + t + 1)
                    copy(f_hi[:, t, :], psum[0:PAIR, 4 + t, :], krec[:, t:t + 1]).then_inc(f_ready, 1)
                for t in range(1, 4):
                    act.wait_ge(m_made, 4 * b + t + 1)
                    copy(m_hi[:, t, :], psum[0:PAIR, t, :], krec[:, t:t + 1]).then_inc(m_high, 1)
                for i in range(8):
                    nh, f = i // 4, i % 4
                    act.wait_ge(h1_made, 8 * b + i + 1)
                    act.activation(h1_hi[:, f, HALF * nh:HALF * nh + HALF], psum[:, (4 + i) % 8, :], ACT.Relu,
                                   bias=b1p[:, f:f + 1]).then_inc(h1_ready, 1)
                def pad(t, n):
                    c0, at, cn = SPANS[n]
                    act.activation(xpad[:, t, n, 5:5 + H, at:at + cn],
                                   x2[:, t, :].rearrange("p (h w) -> p h w", h=H)[:, :, c0:c0 + cn],
                                   ACT.Identity, scale=rstd[1][:, t:t + 1], bias=shift[1][:, t:t + 1])\
                        .then_inc(xpad_ready[0], 1)

                act.wait_ge(norm1_ready, 2 * b + 1)
                for n in range(len(COLS)):
                    pad(0, n)

                def win_copy(s):
                    act.wait_ge(win_made, STEPS * b + s + 1)
                    copy(xwin[0:WIN_N, s % RING, :], psum[0:WIN_N, 4 + s % 2, :]).then_inc(win_ready, 1)

                def relu(s):
                    act.wait_ge(up_made, STEPS * b + s + 1)
                    act.activation(ypt[:, s % RING, :], psum[:, 6 + s % 2, :], ACT.Relu, scale=1.0 - SLOPE)\
                        .then_inc(relu_ready, 1)

                win_copy(0)
                win_copy(1)
                relu(0)
                for s in range(STEPS):
                    if s + 2 < STEPS:
                        win_copy(s + 2)
                    if s + 1 < STEPS:
                        relu(s + 1)
                    if PAD1_AT <= s < PAD1_AT + len(COLS):
                        if s == PAD1_AT:
                            act.wait_ge(norm1_ready, 2 * b + 2)
                        pad(2, s - PAD1_AT)
                    if ahead:
                        if XN_AT <= s < XN_AT + CT:
                            norm_x(b + 1, s - XN_AT)
                        if s == TURN_AT:
                            turn_agents(b + 1)
                if ahead:
                    for g in range(1, 8, 2):
                        g_copy(b + 1, g)

            act.wait_ge(v_b1, 1)
            with act.Fori(0, B - 1, 1) as b:
                image(b, True)
            image(B - 1, False)

        @block.vector
        def _(dve):
            links = [0]

            def link(ins, base, carried=True):
                links[0] += 1
                ins.then_inc(chain, 1)
                dve.wait_ge(chain, base + links[0])
                if not carried:
                    carry(dve, 1)

            def rsqrt(v, y, base, part=None):
                a, c = nt1[:, 0:v.shape[1]], nt2[:, 0:v.shape[1]]
                if part in (None, 0):
                    link(dve.tensor_scalar(a.bitcast(U32), v.bitcast(U32), 1, None, ALU.logical_shift_right), base)
                    link(dve.tensor_scalar(y.bitcast(I32), a.bitcast(I32), -1.0, float(0x5F3759DF), ALU.mult, ALU.add), base)
                    link(dve.tensor_scalar(v, v, -0.5, None, ALU.mult), base)
                for step in range(1, 4):
                    if part in (None, step):
                        link(dve.tensor_tensor(a, y, v, ALU.mult), base)
                        link(dve.tensor_tensor(c, a, y, ALU.mult), base)
                        link(dve.scalar_tensor_tensor(y, c, 1.5, y, ALU.add, ALU.mult), base)

            def bn_stats(src, t, half):
                return dve.bn_stats(bns[:, t, half, :], src[:, t, HALF * half:HALF * half + HALF])

            def channel_stats(tiles_, base, ready):
                for t in tiles_:
                    ins = dve.bn_aggr(stat[:, t, :], bns[:, t])
                ts = slice(tiles_[0], tiles_[-1] + 1)
                link(ins, base)
                link(dve.tensor_tensor(nt1[:, 0:len(tiles_)], stat[:, ts, 0], stat[:, ts, 0], ALU.mult), base)
                dve.tensor_tensor(stat[:, ts, 1], stat[:, ts, 1], nt1[:, 0:len(tiles_)], ALU.add).then_inc(ready, 1)

            def group_norm(made, i, bank, which, tiles_, base, ready, part=None):
                n = len(tiles_)
                ts = slice(tiles_[0], tiles_[-1] + 1)
                if part in (None, 0):
                    dve.wait_ge(made, i + 1)
                    dve.tensor_copy(gs[:, ts, :].rearrange("p t s -> p (t s)"), psum[:, bank, 0:2 * n])\
                        .then_inc(gs_read[which], 1)
                    dve.wait_ge(gs_read[which], i + 1)
                    link(dve.tensor_tensor(nt1[:, 0:n], gs[:, ts, 0], gs[:, ts, 0], ALU.mult), base)
                    link(dve.scalar_tensor_tensor(nv[:, 0:n], gs[:, ts, 1], GN_EPS, nt1[:, 0:n], ALU.add, ALU.subtract), base)
                if part is None:
                    rsqrt(nv[:, 0:n], rstd[which][:, ts], base)
                elif 1 <= part <= 4:
                    rsqrt(nv[:, 0:n], rstd[which][:, ts], base, part - 1)
                if part in (None, NORM_PARTS - 1):
                    dve.scalar_tensor_tensor(shift[which][:, ts], gs[:, ts, 0], -1.0, rstd[which][:, ts], ALU.mult, ALU.mult)\
                        .then_inc(ready, 1)

            def pool_rows(i_img, i):
                r0, r1 = WIN[i]
                src = xin[:].rearrange("p t (h w) -> p t w h", h=H)[:, :, :, r0:r1]
                return dve.tensor_reduce(rowsum[:, :, i, :], src, AX.X, ALU.add)

            def pool_cols(j):
                c0, c1 = WIN[j]
                return dve.tensor_reduce(pooled.rearrange("p t i j -> p (t i) j")[:, :, j:j + 1],
                                         rowsum.rearrange("p t i w -> p (t i) w")[:, :, c0:c1], AX.X, ALU.add)

            def mix_copy(i, bank):
                dve.wait_ge(mix_made, i + 1)
                dve.tensor_copy(mix_out, psum[0:AG, bank, :]).then_inc(mix_ready, 1)

            def pwo_copy(i, bank, first=False):
                dve.wait_ge(pw_ready, i + 1)
                if not first:
                    dve.wait_ge(at_loaded, 32 * i)
                dve.tensor_tensor(pwo, psum[:, bank, 0:CT * AG].rearrange("p (t a) -> p t a", t=CT),
                                  par[:, 5, :].rearrange("p (t o) -> p t o", o=1).broadcast_to([P, CT, AG]), ALU.add)\
                    .then_inc(pwo_ready, 1)

            def g_copy(i, g):
                dve.wait_ge(g_made, 8 * i + g + 1)
                dve.tensor_copy((g_k if g < CT else g_q)[:, g % CT, :], psum[:, 4 + g % 4, 0:AGS]).then_inc(g_ready[0], 1)

            dve.wait_ge(pool_setup, 1)
            for t in range(CT):
                dve.wait_ge(x_first[t], 16)
                for half in range(2):
                    ins = bn_stats(xin, t, half)
            link(ins, 0)
            channel_stats(range(CT), 0, stat_ready)
            for i in range(POOL):
                ins = pool_rows(0, i)
            link(ins, 0)
            for j in range(POOL):
                ins = pool_cols(j)
            ins.then_inc(pool_ready, 1)
            group_norm(gstat_ready, 0, 4, 0, range(CT), 0, norm_ready)
            dve.wait_ge(par_load, 16 * 9)
            link(dve.tensor_scalar(nv, par[:, 4, :], BN_EPS, None, ALU.add), 0)
            rsqrt(nv, ny, 0)
            link(dve.tensor_tensor(ny, ny, par[:, 1, :], ALU.mult), 0)
            link(dve.tensor_tensor(nt1, par[:, 0, :], par[:, 3, :], ALU.subtract), 0)
            link(dve.tensor_tensor(nt1, nt1, ny, ALU.mult), 0)
            link(dve.tensor_tensor(tapb[:], nt1, par[:, 2, :], ALU.add), 0)
            dve.tensor_tensor(tapw[:], tapw[:], ny.rearrange("p (t o) -> p t o", o=1).broadcast_to([P, CT, 9]),
                              ALU.mult).then_inc(v_tap, 1)
            mix_copy(0, 7)
            for t in range(CT):
                dve.wait_ge(pe_p1, t + 1)
                dve.tensor_copy(w_p1[:, t, :], psum[:, t, :]).then_inc(v_p1, 1)
            dve.wait_ge(pe_b1, 1)
            dve.tensor_tensor(b1p[:], psum[:, 6, 0:CT], par[:, 6, :], ALU.add).then_inc(v_b1, 1)
            dve.wait_ge(f_load, 16 * 4)
            for j, dst, gain in ((0, op_up[0:WIN_N, 0], 4.0), (0, op_up[0:WIN_N, 1], 4.0), (1, x2[0:WIN_N, 1, 0:PT_N], ROOT2)):
                ins = dve.scalar_tensor_tensor(
                    dst.rearrange("p (r s) -> p r s", r=2 * MR),
                    frow[j].rearrange("p (r o) -> p r o", o=1).broadcast_to([WIN_N, 2 * MR, 2 * MC]), gain,
                    fcol[j].rearrange("p (o s) -> p o s", o=1).broadcast_to([WIN_N, 2 * MR, 2 * MC]), ALU.mult, ALU.mult)
            ins.then_inc(v_op, 1)
            dve.wait_ge(row_load, 16 * ROW_LOADS)
            dve.wait_ge(x2_moved, 16)
            dve.tensor_tensor(m_bias[0:AG, :], m_bias[0:AG, :], x2[0:AG, 0, 0:C], ALU.add).then_inc(v_bias, 1)
            pwo_copy(0, 5, first=True)
            dve.wait_ge(pe_dn, 1)
            dve.tensor_copy(op_dn[:].rearrange("p a b -> p (a b)"), psum[:, 6, 0:WIN_N]).then_inc(v_dn, 1)
            dve.wait_ge(w2_load, 16)
            link(dve.tensor_copy(flat(w_2T_hl[:, 0]), flat(w2_in)), 0)
            dve.tensor_tensor(flat(w_2T_hl[:, 1]), flat(w2_in), flat(w_2T_hl[:, 0]).bitcast(F32), ALU.subtract).then_inc(w_split, 1)
            for g in range(0, 8, 2):
                g_copy(0, g)
            assert links[0] == CHAIN_BEFORE, ("CHAIN_BEFORE", links[0])

            def image(b, ahead):
                links[0] = 0
                base = CHAIN_BEFORE + CHAIN_IMAGE * b

                def k_max(n):
                    dve.wait_ge(sT_ready, NT * b + n + 1)
                    ins = dve.tensor_tensor(kmax_run, pT[:, 0, :] if n == 1 else kmax_run, pT[:, n, :], ALU.max)
                    if n < NT - 1:
                        link(ins, base)
                    else:
                        ins.then_inc(kmax_run_ready, 1)

                def k_max_end():
                    dve.wait_ge(kmax_turned, b + 1)
                    dve.tensor_reduce(kmax[:], psum[0:PAIR, 6, :].rearrange("p (t n) -> p t n", t=4), AX.X, ALU.max)\
                        .then_inc(kmax_ready, 1)

                def k_sub(n):
                    if n == 0:
                        dve.wait_ge(kmax_spread, b + 1)
                    dve.tensor_tensor(pT[:, n, :], pT[:, n, :], psum[:, 7, 0:AGS], ALU.subtract).then_inc(ksub_ready, 1)

                def xT_copy(n):
                    dve.wait_ge(xT_made, NT * b + n + 1)
                    dve.tensor_copy(xT[:, n, :], psum[:, 5, :]).then_inc(xT_ready[1], 1)

                def q_sub(n):
                    dve.wait_ge(sq_made, NT * b + n + 1)
                    s = psum[:, 4 + n % 2, 0:AGS].rearrange("p (h a) -> p h a", h=HEADS)
                    link(dve.tensor_reduce(qmax[:, n % 2, :].rearrange("p (h o) -> p h o", o=1), s, AX.X, ALU.max), base)
                    dve.tensor_tensor(qp[:, n % 4, :].rearrange("p (h a) -> p h a", h=HEADS), s,
                                      qmax[:, n % 2, :].rearrange("p (h o) -> p h o", o=1).broadcast_to([P, HEADS, AG]),
                                      ALU.subtract).then_inc(qsub_ready, 1)

                def q_sum(n):
                    dve.wait_ge(qexp_ready, NT * b + n + 1)
                    if n >= 2:
                        dve.wait_ge(qp_ready, NT * b + n - 1)
                    link(dve.tensor_reduce(qsum[:, n % 2, :].rearrange("p (h o) -> p h o", o=1),
                                           qp[:, n % 4, :].rearrange("p (h a) -> p h a", h=HEADS), AX.X, ALU.add), base)
                    dve.reciprocal(qsum[:, n % 2, :], qsum[:, n % 2, :]).then_inc(qrec_ready, 1)

                def qT_rest(n):
                    hi, src = qT_hi[0:PAIR, n], psum[0:PAIR, 6 + n % 2, :].rearrange("p (t n) -> p t n", t=4)
                    if n % 2:
                        dve.wait_ge(qT_made, NT * b + n + 1)
                        dve.tensor_copy(hi, src).then_inc(qT_ready[1], 1)
                    dve.wait_ge(qT_ready[n % 2], 4 * b + n // 2 + 1)
                    dve.tensor_tensor(qT_lo[0:PAIR, n], src, hi.bitcast(F32), ALU.subtract).then_inc(qT_low, 1)

                for n in range(1, NT):
                    k_max(n)
                    if n % 2:
                        xT_copy(n)
                q_sub(0)
                k_max_end()
                q_sub(1)
                q_sum(0)
                for n in range(NT):
                    k_sub(n)
                q_sum(1)
                for n in range(2, 5):
                    q_sub(n)
                    if n > 2:
                        q_sum(n - 1)
                dve.wait_ge(x2_moved, 16 + 16 * 8 * b)
                qT_rest(0)
                qT_rest(1)
                q_sub(5)
                q_sum(4)
                q_sub(6)
                q_sum(5)
                qT_rest(2)
                qT_rest(3)
                q_sub(7)
                q_sum(6)
                q_sum(7)
                qT_rest(4)
                qT_rest(5)
                dve.wait_ge(ksum_made, b + 1)
                dve.reciprocal(krec[:], psum[0:PAIR, 1, 0:CT]).then_inc(krec_ready, 1)
                dve.wait_ge(agg_made, b + 1)
                for hh in range(2):
                    r, c = slice(HD * hh, HD * hh + HD), slice(AG * hh, AG * hh + AG)
                    ins = dve.tensor_copy(agg[r, :, c], psum[r, 0, 0:AGS].rearrange("p (t a) -> p t a", a=PAIR)[:, :, c])
                ins.then_inc(agg_ready, 1)
                qT_rest(6)
                qT_rest(7)
                dve.wait_ge(krec_ready, b + 1)

                def rest(low, high, src, t, ready, n):
                    dve.wait_ge(ready, n)
                    return dve.scalar_tensor_tensor(low[:, t, :], src, krec[:, t:t + 1], high[:, t, :].bitcast(F32),
                                                    ALU.mult, ALU.subtract)

                for t in range(4):
                    rest(f_lo, f_hi, psum[0:PAIR, 4 + t, :], t, f_ready, 4 * b + t + 1).then_inc(f_low, 1)
                dve.wait_ge(m_made, 4 * b + 1)
                link(dve.scalar_tensor_tensor(m_tmp, psum[0:PAIR, 0, :], krec[:, 0:1], m_bias[:], ALU.mult, ALU.add), base)
                link(dve.tensor_copy(m_hi[:, 0, :], m_tmp), base)
                link(dve.tensor_tensor(m_lo[:, 0, :], m_tmp, m_hi[:, 0, :].bitcast(F32), ALU.subtract), base, carried=False)

                def h1_again(i):
                    dve.wait_ge(h1_ready, 8 * b + i + 1)
                    if i >= 2:
                        dve.wait_ge(h1_low, 8 * b + i - 1)
                    dve.tensor_scalar(h1_tmp[:, i % 2, :], psum[:, (4 + i) % 8, :], b1p[:, i % 4:i % 4 + 1], 0.0,
                                      ALU.add, ALU.max).then_inc(h1_full, 1)

                for t in range(1, 4):
                    rest(m_lo, m_hi, psum[0:PAIR, t, :], t, m_high, 3 * b + t).then_inc(m_low, 1)
                for i in range(8):
                    h1_again(i)

                def pad(t, n):
                    c0, at, cn = SPANS[n]
                    dve.tensor_scalar(xpad[:, t, n, 5:5 + H, at:at + cn],
                                      x2[:, t, :].rearrange("p (h w) -> p h w", h=H)[:, :, c0:c0 + cn],
                                      rstd[1][:, t:t + 1], shift[1][:, t:t + 1], ALU.mult, ALU.add)\
                        .then_inc(xpad_ready[1], 1)

                for i in range(NT):
                    t, cs = i // 2, slice(HALF * (i % 2), HALF * (i % 2) + HALF)
                    dve.wait_ge(o_made, NT * b + i + 1)
                    dve.tensor_tensor(x2[:, t, cs], psum[:, (4 + i) % 8, :], xin[:, t, cs], ALU.add).then_inc(x2_ready, 1)
                    if i:
                        dve.wait_ge(x2_ready, NT * b + i)
                        ins = bn_stats(x2, (i - 1) // 2, (i - 1) % 2)
                    if i == 4:
                        link(ins, base, carried=False)
                        channel_stats(range(2), base, stat1_ready)
                    if i == 6:
                        group_norm(gstat1_ready, 2 * b, 7, 1, range(2), base, norm1_ready)
                        dve.wait_ge(norm1_ready, 2 * b + 1)
                        for n in range(len(COLS)):
                            pad(1, n)
                dve.wait_ge(x2_ready, NT * b + NT)
                link(bn_stats(x2, CT - 1, 1), base, carried=False)
                channel_stats(range(2, CT), base, stat1_ready)

                def leaky(s):
                    dve.wait_ge(relu_ready, STEPS * b + s + 1)
                    y = ypt[:, s % RING, :]
                    dve.scalar_tensor_tensor(y, psum[:, 6 + s % 2, :], SLOPE, y, ALU.mult, ALU.add).then_inc(up_read, 1)

                def clamp(s):
                    dve.wait_ge(up_read, STEPS * b + s + 1)
                    y = ypt[:, s % RING, :]
                    dve.tensor_scalar(y, y, CLAMP / ROOT2, -CLAMP / ROOT2, ALU.min, ALU.max).then_inc(y_ready, 1)

                def z_add(pair, z):
                    dve.wait_ge(z_made, 6 * b + 3 * pair + z + 1)
                    if z:
                        dve.wait_ge(z_ready, 12 * b + 6 * pair + 2 * z)
                    r0, r1 = SECTION_ROWS[z]
                    for c in range(2):
                        xs = x2[:, 2 * pair + c, W * r0:W * r1]
                        dve.tensor_tensor(xs, psum[:, z_bank(pair, z, c), 0:W * (r1 - r0)], xs, ALU.add).then_inc(z_ready, 1)

                for s in range(STEPS):
                    leaky(s)
                    clamp(s)
                    if s in Z_AT:
                        z_add(*Z_AT[s])
                    if 0 <= s - NORM1_AT < NORM_PARTS:
                        group_norm(gstat1_ready, 2 * b + 1, 3, 1, range(2, CT), base, norm1_ready, s - NORM1_AT)
                    if 0 <= s - PAD1_AT < len(COLS):
                        if s == PAD1_AT:
                            dve.wait_ge(norm1_ready, 2 * b + 2)
                        pad(3, s - PAD1_AT)
                    if not ahead:
                        continue
                    if 0 <= s - BN_AT < 2 * CT:
                        if s == BN_AT:
                            dve.wait_ge(x_loaded, 16 * CT * (b + 1))
                        ins = bn_stats(xin, (s - BN_AT) // 2, (s - BN_AT) % 2)
                        if s == BN_AT + 2 * CT - 1:
                            link(ins, base, carried=False)
                            channel_stats(range(CT), base, stat_ready)
                    if 0 <= s - ROWS_AT < POOL:
                        ins = pool_rows(b + 1, s - ROWS_AT)
                        if s == ROWS_AT + POOL - 1:
                            link(ins, base)
                            for j in range(POOL):
                                ins = pool_cols(j)
                            ins.then_inc(pool_ready, 1)
                    if 0 <= s - NORM_AT < NORM_PARTS:
                        group_norm(gstat_ready, b + 1, 2, 0, range(CT), base, norm_ready, s - NORM_AT)
                    if s == MIX_AT + 1:
                        mix_copy(b + 1, 0)
                    if s == PW_AT + 1:
                        pwo_copy(b + 1, 0)
                z_add(*Z_LAST)
                if ahead:
                    for g in range(0, 8, 2):
                        g_copy(b + 1, g)
                    assert links[0] == CHAIN_IMAGE, ("CHAIN_IMAGE", links[0])

            with dve.Fori(0, B - 1, 1) as b:
                image(b, True)
            image(B - 1, False)

        @block.tensor
        def _(pe):
            def mm(out_, lhsT, rhs, start, stop, **kw):
                return pe.matmul(out_, lhsT, rhs, start=start, stop=stop, **kw)

            def mm3(out_, a_hi, a_lo, b_hi, b_lo, first, last):
                mm(out_, a_hi, b_lo, first, False)
                mm(out_, a_lo, b_hi, False, False)
                return mm(out_, a_hi, b_hi, False, last)

            def group_stats(i, bank, tiles_, ready, made):
                pe.wait_ge(ready, i + 1)
                ts = slice(tiles_[0], tiles_[-1] + 1)
                mm(psum[:, bank, 0:2 * len(tiles_)], gmean[:], stat[:, ts, :].rearrange("p t s -> p (t s)"), True, True)\
                    .then_inc(made, 1)

            def mix(i, bank):
                pe.wait_ge(pn_ready, i + 1)
                for t in range(CT):
                    ins = mm(psum[0:AG, bank, P * t:P * t + P], pooled[:, t].rearrange("p i j -> p (i j)"), ident[:],
                             True, True)
                ins.then_inc(mix_made, 1)

            def pointwise(i, bank):
                pe.wait_ge(pw_load, 16 * (i + 1))
                pe.wait_ge(conv_ready, i + 1)
                for o in range(CT):
                    for k in range(CT):
                        ins = mm(psum[:, bank, AG * o:AG * o + AG], w_pwT[:, k, P * o:P * o + P],
                                 conv[:, k].rearrange("p i j -> p (i j)"), k == 0, k == CT - 1)
                ins.then_inc(pw_ready, 1)

            def turn_agents(i):
                pe.wait_ge(at_loaded, 32 * (i + 1))
                for t in range(HEADS // 2):
                    ins = pe.transpose(psum[:, 1, PAIR * t:PAIR * t + PAIR], at_in[:, t, :], ident[0:PAIR, 0:PAIR])
                ins.then_inc(at_turned, 1)

            def fold_agents(i, prior):
                pe.wait_ge(at_ready, i + 1)
                for g in range(8):
                    prior(g)
                    w = w_k if g < CT else w_q
                    for t in range(HEADS // 2):
                        ins = mm(psum[:, 4 + g % 4, PAIR * t:PAIR * t + PAIR], w[:, t, P * (g % CT):P * (g % CT) + P],
                                 at_bd[:, t, :], True, True)
                    ins.then_inc(g_made, 1)

            pe.wait_ge(pool_setup, 1)
            group_stats(0, 4, range(CT), stat_ready, gstat_ready)
            mix(0, 7)
            pe.wait_ge(p1_load, 32)
            for m in range(CT):
                for k in range(CT):
                    ins = mm(psum[:, m, :], pw_in[:, k, P * m:P * m + P], p1_in[:, k, :], k == 0, k == CT - 1)
                ins.then_inc(pe_p1, 1)
            pe.wait_ge(par_load, 16 * 9)
            for m in range(CT):
                for k in range(CT):
                    ins = mm(psum[:, 6, m:m + 1], p1_in[:, k, P * m:P * m + P], par[:, 7, k:k + 1], k == 0, k == CT - 1)
            ins.then_inc(pe_b1, 1)
            pointwise(0, 5)
            pe.wait_ge(v_b1, 1)
            pe.wait_ge(v_op, 1)
            pe.transpose(psum[:, 6, 0:WIN_N], x2[0:WIN_N, 1, 0:PT_N], ident[0:WIN_N, 0:WIN_N]).then_inc(pe_dn, 1)
            pe.wait_ge(v_p1, CT)
            turn_agents(0)
            pe.wait_ge(gs_read[0], 1)
            pe.wait_ge(kq_load, 32)

            def first_prior(g):
                if g == 1:
                    pe.wait_ge(pwo_ready, 1)
                if g == 2:
                    pe.wait_ge(v_dn, 1)
                if g == 3:
                    pe.wait_ge(mix_ready, 1)
                if g >= 4:
                    pe.wait_ge(g_ready[g % 2], (g - 4) // 2 + 1)
            fold_agents(0, first_prior)
            pe.wait_ge(v_bias, 1)
            pe.wait_ge(w_split, 1)
            pe.wait_ge(v_load, 16)
            pe.wait_ge(proj_load, 16)

            def image(b, ahead):
                def k_scores(n):
                    if n >= 4:
                        pe.wait_ge(sT_ready, NT * b + n - 3)
                    for k in range(CT):
                        ins = mm(psum[:, n % 4, 0:AGS], xn[:, k, P * n:P * n + P], g_k[:, k, :], k == 0, k == CT - 1)
                    ins.then_inc(sk_made, 1)

                def turn_max():
                    pe.wait_ge(kmax_run_ready, b + 1)
                    for t in range(4):
                        ins = pe.transpose(psum[0:PAIR, 6, P * t:P * t + P], kmax_run[:, PAIR * t:PAIR * t + PAIR], ident[:])
                    ins.then_inc(kmax_turned, 1)

                def spread_max():
                    pe.wait_ge(kmax_ready, b + 1)
                    for t in range(4):
                        ins = mm(psum[:, 7, PAIR * t:PAIR * t + PAIR], kmax[:, t:t + 1].broadcast_to([PAIR, P]),
                                 ident[0:PAIR, 0:PAIR], True, True)
                    ins.then_inc(kmax_spread, 1)

                def turn_x(n):
                    if n >= 2:
                        pe.wait_ge(xT_ready[n % 2], 4 * b + n // 2)
                    for k in range(CT):
                        ins = pe.transpose(psum[:, 4 + n % 2, P * k:P * k + P], xn[:, k, P * n:P * n + P], ident[:])
                    ins.then_inc(xT_made, 1)

                def q_scores(n):
                    if n < 2:
                        pe.wait_ge(xT_ready[n % 2], 4 * b + 4)
                    else:
                        pe.wait_ge(qsub_ready, NT * b + n - 1)
                    for k in range(CT):
                        ins = mm(psum[:, 4 + n % 2, 0:AGS], xn[:, k, token_tile(n)], g_q[:, k, :], k == 0, k == CT - 1)
                    ins.then_inc(sq_made, 1)

                def aggregate_x(t):
                    if t == 0:
                        pe.wait_ge(kexp_ready, NT * b + NT)
                    for n in range(NT):
                        ins = mm(psum[:, t, 0:AGS], xT[:, n, P * t:P * t + P], pT[:, n, :], n == 0, n == NT - 1)
                    ins.then_inc(px_made, 1)

                def turn_q(n):
                    pe.wait_ge(qp_ready, NT * b + n + 1)
                    if n >= 2:
                        pe.wait_ge(qT_low, NT * b + n - 1)
                    for t in range(4):
                        ins = pe.transpose(psum[0:PAIR, 6 + n % 2, P * t:P * t + P],
                                           qp[:, n % 4, PAIR * t:PAIR * t + PAIR], ident[:])
                    ins.then_inc(qT_made, 1)

                for j in range(2):
                    pe.wait_ge(g_ready[j], 4 * (b + 1))
                pe.wait_ge(xn_ready, CT * (b + 1))
                for n in range(NT):
                    k_scores(n)
                    turn_x(n)
                q_scores(0)
                turn_max()
                q_scores(1)
                spread_max()
                q_scores(2)
                q_scores(3)
                for t in range(CT):
                    aggregate_x(t)
                    turn_q(t)
                    q_scores(4 + t)
                turn_q(4)
                turn_q(5)
                pe.wait_ge(px_ready, 4 * b + 4)
                pe.wait_ge(ksum_run_ready, b + 1)
                for t in range(4):
                    ins = mm(psum[0:PAIR, 1, t:t + 1], ksum_run[:, PAIR * t:PAIR * t + PAIR], ones[:], True, True)
                ins.then_inc(ksum_made, 1)
                for t in range(4):
                    for k in range(CT):
                        ins = mm(psum[:, 0, PAIR * t:PAIR * t + PAIR], w_vT[:, k, P * t:P * t + P],
                                 pxT[:, k, PAIR * t:PAIR * t + PAIR], k == 0, k == CT - 1)
                ins.then_inc(agg_made, 1)
                turn_q(6)
                turn_q(7)
                pe.wait_ge(agg_ready, b + 1)
                for t in range(4):
                    if t == 0:
                        pe.wait_ge(qsub_ready, NT * b + NT)
                    if t >= 2:
                        pe.wait_ge(qT_low, NT * b + NT - 2 + t - 1)
                    mm(psum[0:PAIR, 4 + t, :], agg[:, t, :], w_p1[:, t, :], True, True).then_inc(f_made, 1)
                for t in range(4):
                    mm(psum[0:PAIR, t, :], agg[:, t, :], w_projT[:, t, :], True, True).then_inc(m_made, 1)
                for i in range(8):
                    nh, f = i // 4, i % 4
                    if i == 0:
                        pe.wait_ge(qT_low, NT * b + NT)
                    if i < 4:
                        if i == 0:
                            pe.wait_ge(f_low, 4 * b + 4)
                    elif i == 4:
                        pe.wait_ge(m_low, 3 * b + 3)
                    ns, fs = slice(4 * nh, 4 * nh + 4), slice(P * f, P * f + P)
                    for t in range(4):
                        ins = mm3(psum[:, (4 + i) % 8, :], f_hi[:, t, fs], f_lo[:, t, fs],
                                  qT_hi[0:PAIR, ns, t, :], qT_lo[0:PAIR, ns, t, :], t == 0, t == 3)
                    ins.then_inc(h1_made, 1)
                for i in range(NT):
                    if i % 4 == 0:
                        pe.wait_ge(h1_low, 8 * b + i + 4)
                        pe.wait_ge(h1_ready, 8 * b + i + 4)
                    bank = psum[:, (4 + i) % 8, :]
                    for t in range(4):
                        mm3(bank, qT_hi[0:PAIR, i, t, :], qT_lo[0:PAIR, i, t, :], m_hi[:, t, :], m_lo[:, t, :], t == 0, False)
                    for k in range(CT):
                        ts = slice(P * i, P * i + P)
                        ins = mm3(bank, h1_hi[:, k, ts], h1_lo[:, k, ts], w_2T_hl[:, 0, k, :], w_2T_hl[:, 1, k, :],
                                  False, k == CT - 1)
                    ins.then_inc(o_made, 1)
                    if i == 5:
                        pe.wait_ge(x2_ready, NT * b + 4)
                        group_stats(2 * b, 7, range(2), stat1_ready, gstat1_ready)

                def cut(s):
                    if s >= 2:
                        pe.wait_ge(win_ready, STEPS * b + s - 1)
                    pair, item = s // ITEMS, s % ITEMS
                    for j in range(2):
                        m, n = PATCHES[2 * item + j]
                        for c in range(2):
                            at = P * (2 * j + c)
                            ins = pe.transpose(psum[0:WIN_N, 4 + s % 2, at:at + P],
                                               xpad_run[:, 2 * pair + c, n // MC, WW * m:WW * (m + WH)], ident[:])
                    ins.then_inc(win_made, 1)

                def up(s):
                    pe.wait_ge(win_ready, STEPS * b + s + 1)
                    if s >= 2:
                        pe.wait_ge(up_read, STEPS * b + s - 1)
                    rows, pair = slice(0, WIN_N + 2), s // ITEMS
                    mm(psum[:, 6 + s % 2, :], op_up[:, pair, :], xwin[rows, s % RING, :], True, True).then_inc(up_made, 1)

                def down(s):
                    pe.wait_ge(y_ready, STEPS * b + s + 1)
                    pair, item = s // ITEMS, s % ITEMS
                    for j in range(2):
                        p = 2 * item + j
                        z, ks, ls, ws, wl = down_part(p)
                        first, last = p == SECTION_PATCHES[z][0], p == SECTION_PATCHES[z][-1]
                        if first and 3 * pair + z >= 2:
                            pe.wait_ge(z_ready, 12 * b + 2 * (3 * pair + z) - 2)
                        if first and (pair, z) == (0, 1):
                            pe.wait_ge(gs_read[1], 2 * b + 2)
                        if first and (pair, z) == (1, 0) and ahead:
                            pe.wait_ge(gs_read[0], b + 2)
                        if first and (pair, z) == (1, 1) and ahead:
                            pe.wait_ge(mix_ready, b + 2)
                        for c in range(2):
                            out_ = psum[:, z_bank(pair, z, c), :].rearrange("p (k l) -> p k l", l=W)[:, ks, ls]
                            at = P * (2 * j + c)
                            ins = mm(out_, ypt[:, s % RING, at:at + P], op_dn[:, ws, wl], first, last, skip_group_check=True)
                        if last:
                            ins.then_inc(z_made, 1)

                pe.wait_ge(border_ready, CT * b + 2)
                for j in range(2):
                    pe.wait_ge(xpad_ready[j], 2 * len(COLS) * b + len(COLS))
                cut(0)
                cut(1)
                up(0)
                for s in range(STEPS + 1):
                    if s == 0:
                        pe.wait_ge(x2_ready, NT * b + NT)
                    if s + 2 == ITEMS:
                        pe.wait_ge(border_ready, CT * (b + 1))
                        for j in range(2):
                            pe.wait_ge(xpad_ready[j], 2 * len(COLS) * (b + 1))
                    if s + 2 < STEPS:
                        cut(s + 2)
                    if s + 1 < STEPS:
                        up(s + 1)
                    if s:
                        down(s - 1)
                    if s == STAT1_AT:
                        group_stats(2 * b + 1, 3, range(2, CT), stat1_ready, gstat1_ready)
                    if not ahead:
                        continue
                    if s == STAT_AT:
                        pe.wait_ge(z_ready, 12 * b + 4)
                        group_stats(b + 1, 2, range(CT), stat_ready, gstat_ready)
                    if s == MIX_AT:
                        pe.wait_ge(z_ready, 12 * b + 6)
                        mix(b + 1, 0)
                    if s == PW_AT:
                        pe.wait_ge(z_ready, 12 * b + 10)
                        pointwise(b + 1, 0)
                    if s == TURN_AT:
                        turn_agents(b + 1)
                if ahead:
                    def prior(g):
                        if g < 2:
                            pe.wait_ge(win_ready, STEPS * (b + 1))
                        elif g < 4:
                            pe.wait_ge(up_read, STEPS * (b + 1))
                        else:
                            pe.wait_ge(g_ready[g % 2], 4 * (b + 1) + (g - 4) // 2 + 1)
                    fold_agents(b + 1, prior)

            with pe.Fori(0, B - 1, 1) as b:
                image(b, True)
            image(B - 1, False)


def kernel(**inputs):
    import numpy as np
    import concourse.bacc as bacc
    from concourse.bass_utils import run_bass_kernel_spmd as run

    def a(name):
        return np.asarray(inputs[name])

    kv = a("L0_conv_kv_w")
    arrays = {
        "x": a("x").reshape(B, C, N),
        "wq": a("L0_conv_q_w"), "wk": kv[:C], "wvT": kv[C:].T,
        "pwT": a("L0_conv_pw_w").reshape(C, C).T,
        "projT": a("L0_conv_proj_w").T, "proj": a("L0_conv_proj_w"),
        "w1T": a("L0_conv_enh1_w").T, "w2T": a("L0_conv_enh2_w").T,
        "dw_w": a("L0_conv_dw_w").reshape(C, 9), "dw_b": a("L0_conv_dw_b"),
        "bn_g": a("L0_conv_bn_gamma"), "bn_b": a("L0_conv_bn_beta"),
        "bn_m": a("L0_conv_bn_mean"), "bn_v": a("L0_conv_bn_var"),
        "pw_b": a("L0_conv_pw_b"), "proj_b": a("L0_conv_proj_b"),
        "enh1_b": a("L0_conv_enh1_b"), "enh2_b": a("L0_conv_enh2_b"),
        "bias": a("L1_conv_bias"), "up_f": a("L1_conv_up_filter")[::-1], "down_f": a("L1_conv_down_filter"),
    }
    arrays = {f"in_{k}": np.ascontiguousarray(v) for k, v in arrays.items()}
    nc = bacc.Bacc("TRN2", target_bir_lowering=False, num_devices=1)
    args = [nc.dram_tensor(k, v.shape, mybir.dt.from_np(v.dtype), kind="ExternalInput").ap() for k, v in arrays.items()]
    out = nc.dram_tensor("out", (B, C, N), F32, kind="ExternalOutput").ap()
    agent_dram = nc.dram_tensor("agent_scratch", (2, C * AG), F32, kind="Internal").ap()
    filt_dram = nc.dram_tensor("filter_scratch", (2, FILT), F32, kind="Internal").ap()
    build(nc, *args, out, agent_dram, filt_dram)
    got = run(nc, [arrays], core_ids=[0]).results[0]["out"]
    return got.reshape(B, C, H, W)
```

```python
from contextlib import ExitStack

import concourse.bass as bass
from concourse import mybir

F32 = mybir.dt.float32
F32R = mybir.dt.float32r
I32 = mybir.dt.int32
U32 = mybir.dt.uint32
ALU = mybir.AluOpType
ACT = mybir.ActivationFunctionType
AX = mybir.AxisListType

P = 128
B, C, H, W = 16, 512, 32, 32
N = H * W
CT = C // P
NT = N // P
HALF = 512
HEADS, POOL = 8, 7
AG = POOL * POOL
PAIR = 2 * AG
AGS = HEADS * AG
HD = C // HEADS
SCALE = float(HD) ** -0.5
GROUP = C // 32
GN_EPS, BN_EPS = 1e-5, 1e-5
SLOPE, CLAMP, ROOT2 = 0.2, 256.0, 2.0 ** 0.5
TAPS = 12
FILT = TAPS + 32

WIN = [(i * H // POOL, -(-(i + 1) * H // POOL)) for i in range(POOL)]

MR, MC = 4, 8
PHASES = (2 * H + TAPS - 2) // 2
WH, WW = MR + 5, MC + 5
WIN_N = WH * WW
PT_N = 4 * MR * MC
ROWS, COLS = range(0, PHASES, MR), range(0, PHASES, MC)
PADH = 5 + ROWS[-1] + MR
SPANS = [(max(0, n - 5), max(0, 5 - n), min(W, n + MC) - max(0, n - 5)) for n in COLS]
PATCHES = [(m, n) for m in ROWS for n in COLS]
ITEMS = len(PATCHES) // 2
STEPS = 2 * ITEMS
RING = 4

CHAIN_BEFORE, CHAIN_IMAGE = 36, 77
PCHAIN_BEFORE, PCHAIN_IMAGE = 24, 27

STAT1_AT, NORM1_AT, PAD1_AT = 1, 2, 8
BN_AT, ROWS_AT, STAT_AT, NORM_AT, XN_AT = 4, 12, 17, 18, 24
MIX_AT, PW_AT, TURN_AT = 27, 42, 47
NORM_PARTS = 6
COLS_AT = {ROWS_AT + POOL: (0, 1, 2), ROWS_AT + POOL + 1: (3, 4), ROWS_AT + POOL + 2: (5, 6)}
POOL_XT = (3, 5, 7)
VECTOR_XT = tuple(n for n in range(NT) if n not in POOL_XT)
PX_BANKS = (0, 4, 5, 2)


BANK_ROWS = HALF // W
SECTION_OF = [0 if m - 5 + WH <= BANK_ROWS else 1 if m - 5 < BANK_ROWS else 2 for m, n in PATCHES]
SECTION_PATCHES = [[p for p in range(len(PATCHES)) if SECTION_OF[p] == z] for z in range(3)]
SECTION_ROWS = [(max(0, PATCHES[ps[0]][0] - 5), min(H, PATCHES[ps[-1]][0] - 5 + WH)) for ps in SECTION_PATCHES]
Z_AT = {ITEMS * pair + SECTION_PATCHES[z][-1] // 2 + 2: (pair, z) for pair in range(2) for z in range(3)}
Z_LAST = (1, 2)


def z_bank(pair, z, c):
    return 2 * ((3 * pair + z) % 2) + c


def down_part(p):
    z = SECTION_OF[p]
    k0, l0, first = PATCHES[p][0] - 5, PATCHES[p][1] - 5, SECTION_ROWS[z][0]
    k_lo, k_hi, l_lo, l_hi = max(0, k0), min(H, k0 + WH), max(0, l0), min(W, l0 + WW)
    return (z, slice(k_lo - first, k_hi - first), slice(l_lo, l_hi),
            slice(k_lo - k0, k_hi - k0), slice(l_lo - l0, l_hi - l0))


def build(nc, x, wq, wk, wvT, pwT, projT, proj, w1T, w2T, dw_w, dw_b, bn_g, bn_b, bn_m, bn_v, pw_b,
          proj_b, enh1_b, enh2_b, bias, up_f, down_f, out, agent_dram, filt_dram):
    with ExitStack() as ctx:
        def sb(name, shape, dt=F32):
            return ctx.enter_context(nc.sbuf_tensor(name, shape, dt))

        def overlay(name, shape):
            with nc.sbuf_tensor(name, shape, F32) as full:
                pass
            return full, sb(name + "_r", shape, F32R)

        def sem(name):
            return ctx.enter_context(nc.semaphore(name))

        w_q, w_k, w_vT, w_projT, w_p1 = [sb(n, [P, CT, C]) for n in ("w_q", "w_k", "w_vT", "w_projT", "w_p1")]
        w_2T_hl = sb("w_2T_hl", [P, 2, CT, C], F32R)
        ident = sb("ident", [P, P])
        gmean = sb("gmean", [P, P])
        op_up = sb("op_up", [WIN_N + 2, 2, PT_N])
        op_dn = sb("op_dn", [PT_N, WH, WW])
        m_bias = sb("m_bias", [PAIR, C])
        tapw = sb("tapw", [P, CT, 9])
        par = sb("par", [P, 8, CT])
        tapb = sb("tapb", [P, CT])
        b1p = sb("b1p", [P, CT])
        area = sb("area", [P, POOL, POOL])
        xin = sb("xin", [P, CT, N])
        xn, xn_r = overlay("xn", [P, CT, N])
        x2, x2_r = overlay("x2", [P, CT, N])
        reg_m, reg_m_r = overlay("reg_m", [P, HEADS // 2, C])
        m_hi = reg_m_r[0:PAIR]
        prep = reg_m[:].rearrange("p t c -> p (t c)")
        at_bd = prep[:, 0:AGS].rearrange("p (t a) -> p t a", a=PAIR)
        pooled, conv, ctmp = [prep[:, AGS + k * CT * AG:AGS + (k + 1) * CT * AG]
                              .rearrange("p (t i j) -> p t i j", i=POOL, j=POOL) for k in range(3)]
        MIX = AGS + 4 * CT * AG
        mix_out = prep[0:AG, MIX:MIX + C]
        mix_in = prep[:, MIX + C:MIX + C + CT * AG].rearrange("p (t i j) -> p t i j", i=POOL, j=POOL)
        pwo = prep[:, AGS + 3 * CT * AG:AGS + 4 * CT * AG].rearrange("p (t a) -> p t a", a=AG)
        xwin, reg_f = overlay("xwin", [P, RING, C])
        f_hi = reg_f[0:PAIR]
        reg_a, reg_a_r = overlay("reg_a", [P, NT * C + NT * AGS + 3 * CT * AGS])

        def part(start, *shape, of=reg_a):
            n = 1
            for k in shape:
                n *= k
            names = "abcd"[:len(shape)]
            return of[:, start:start + n].rearrange(f"p ({' '.join(names)}) -> p {' '.join(names)}",
                                                       **dict(zip(names, shape)))

        xT, pT = part(0, NT, C), part(NT * C, NT, AGS)
        pxT = part(NT * (C + AGS), CT, AGS)
        g_k_hi, g_q_hi = [part(NT * (C + AGS) + k * CT * AGS, CT, AGS, of=reg_a_r) for k in (1, 2)]
        g_k_lo = reg_m_r[:].rearrange("p t c -> p (t c)")[:, AGS:AGS + CT * AGS].rearrange("p (t a) -> p t a", t=CT)
        x_ring = [reg_f[:, 0:2], reg_f[:, 2:4], part(NT * (C + AGS), 2, C, of=reg_a_r)]
        BAND_N = PADH * WW
        xpad_run = part(0, CT, len(COLS), BAND_N)
        xpad = part(0, CT, len(COLS), BAND_N).rearrange("p t n (h w) -> p t n h w", w=WW)
        LOW = 2 * len(COLS) * BAND_N
        f_lo = part(LOW, CT, C, of=reg_a_r)[0:PAIR]
        m_lo = part(LOW + CT * C, CT, C, of=reg_a_r)[0:PAIR]
        m_tmp = part(LOW + 2 * CT * C, C)[0:PAIR]
        h1_tmp = part(LOW + 2 * CT * C, 2, HALF)
        pw_in, p1_in, w2_in = [part(k * CT * C, CT, C) for k in range(3)]
        reg_y, reg_y_r = overlay("reg_y", [P, 2 * CT * N])
        h1_hi = reg_y_r[:, 0:CT * N].rearrange("p (t n) -> p t n", t=CT)
        h1_lo = xn_r
        qT_hi = reg_y_r[:, CT * N:2 * CT * N].rearrange("p (n t s) -> p n t s", n=NT, t=4)
        qT_lo = x2_r[:].rearrange("p c (h t s) -> p (c h) t s", h=2, t=4)
        kmax_run, ksum_run = reg_y[:, 0:AGS], reg_y[:, AGS:2 * AGS]
        qp = reg_y[:, 2 * AGS:6 * AGS].rearrange("p (s a) -> p s a", s=4)
        g_q_lo = reg_y_r[:, 6 * AGS:(6 + CT) * AGS].rearrange("p (t a) -> p t a", t=CT)
        YPT = RING * HALF
        rowsum = reg_y[:, YPT:YPT + CT * POOL * W].rearrange("p (t i w) -> p t i w", t=CT, i=POOL)
        CPAD = YPT + CT * POOL * W
        cpad = reg_y[:, CPAD:CPAD + CT * (POOL + 2) ** 2].rearrange("p (t i j) -> p t i j", t=CT, i=POOL + 2)
        PWT = CPAD + CT * (POOL + 2) ** 2
        w_pwT = reg_y[:, PWT:PWT + CT * C].rearrange("p (t n) -> p t n", t=CT)
        ypt = reg_y[:, 0:RING * HALF].rearrange("p (s c) -> p s c", c=HALF)
        agg = sb("agg", [P, HEADS // 2, PAIR])
        ATI = PWT + CT * C
        at_in = reg_y[0:PAIR, ATI:ATI + CT * P].rearrange("p (t d) -> p t d", t=HEADS // 2)
        kmax = sb("kmax", [PAIR, HEADS // 2])
        ones = sb("ones", [P, 1])
        krec = sb("krec", [PAIR, HEADS // 2])
        qmax, qsum = sb("qmax", [P, 2, HEADS]), sb("qsum", [P, 2, HEADS])
        bns = sb("bns", [P, CT, 2, 6])
        stat = sb("stat", [P, CT, 2])
        gs = sb("gs", [P, CT, 2])
        small = sb("small", [P, 8, CT])
        nv, ny, nt1, nt2 = [small[:, k, :] for k in range(4)]
        rstd, shift = [small[:, 4 + k, :] for k in range(2)], [small[:, 6 + k, :] for k in range(2)]

        idle = [sb(f"idle{j}", [P, 8]) for j in range(2)]
        carried = [0, 0]
        fzero = x2[0:2, 1, HALF:HALF + FILT]
        frow = [x2[0:WIN_N, 2, 2 * MR * j:2 * MR * j + 2 * MR] for j in range(2)]
        fcol = [x2[0:WIN_N, 3, 2 * MC * j:2 * MC * j + 2 * MC] for j in range(2)]
        psum = ctx.enter_context(nc.psum_tensor("psum", [P, 8, HALF], F32))

        par_load, row_load = sem("par_load"), sem("row_load")
        p1_load, kq_load, v_load, proj_load, w2_load = [sem(n) for n in ("p1_load", "kq_load", "v_load", "proj_load", "w2_load")]
        f_store, f_load = sem("f_store"), sem("f_load")
        pool_setup = sem("pool_setup")
        w_split, pw_load = sem("w_split"), sem("pw_load")
        h1_full, h1_low = sem("h1_full"), sem("h1_low")
        f_low, m_high, m_low, qT_low = sem("f_low"), sem("m_high"), sem("m_low"), sem("qT_low")
        v_op, v_tap, v_p1, v_b1, v_dn, v_bias = [sem(n) for n in ("v_op", "v_tap", "v_p1", "v_b1", "v_dn", "v_bias")]
        pe_p1, pe_b1, pe_dn = sem("pe_p1"), sem("pe_b1"), sem("pe_dn")
        chain, pchain = sem("v_chain"), sem("pool_chain")
        x_first = [sem(f"x_first{t}") for t in range(CT)]
        x_loaded, x2_moved = sem("x_loaded"), sem("x2_moved")
        stat_ready, gstat_ready, norm_ready = sem("stat_ready"), sem("gstat_ready"), sem("norm_ready")
        stat1_ready, gstat1_ready, norm1_ready = sem("stat1_ready"), sem("gstat1_ready"), sem("norm1_ready")
        gs_read = [sem("gs0_read"), sem("gs1_read")]
        xn_ready, pool_ready, conv_ready = sem("xn_ready"), sem("pool_ready"), sem("conv_ready")
        pn_ready, mix_made, mix_ready, mix_stored, mix_loaded = (
            sem("pn_ready"), sem("mix_made"), sem("mix_ready"), sem("mix_stored"), sem("mix_loaded"))
        pw_ready, pwo_ready = sem("pw_ready"), sem("pwo_ready")
        at_stored, at_loaded, at_turned, at_ready = sem("at_stored"), sem("at_loaded"), sem("at_turned"), sem("at_ready")
        g_made = sem("g_made")
        g_high, g_low = sem("g_high"), sem("g_low")
        x_high, x_low = sem("x_high"), sem("x_low")
        xT_high, p_high, p_low, px_step = sem("xT_high"), sem("p_high"), sem("p_low"), sem("px_step")
        xT_low = [sem("xT_low_dve"), sem("xT_low_pool")]
        bias_load = sem("bias_load")
        sk_made, sT_ready, kmax_run_ready = sem("sk_made"), sem("sT_ready"), sem("kmax_run_ready")
        kmax_turned, kmax_ready, kmax_spread = sem("kmax_turned"), sem("kmax_ready"), sem("kmax_spread")
        ksub_ready, kexp_ready, ksum_run_ready, ksum_made = sem("ksub_ready"), sem("kexp_ready"), sem("ksum_run_ready"), sem("ksum_made")
        xT_made = sem("xT_made")
        xT_ready = [sem("xT_ready_act"), sem("xT_ready_dve")]
        krec_ready = sem("krec_ready")
        sq_made, qsub_ready, qexp_ready, qrec_ready, qp_ready = (
            sem("sq_made"), sem("qsub_ready"), sem("qexp_ready"), sem("qrec_ready"), sem("qp_ready"))
        px_made, px_ready, agg_made, agg_ready = sem("px_made"), sem("px_ready"), sem("agg_made"), sem("agg_ready")
        f_made, f_ready, m_made = sem("f_made"), sem("f_ready"), sem("m_made")
        qT_made = sem("qT_made")
        qT_ready = [sem("qT_ready_act"), sem("qT_ready_dve")]
        h1_made, h1_ready, o_made, x2_ready = sem("h1_made"), sem("h1_ready"), sem("o_made"), sem("x2_ready")
        border_ready = sem("border_ready")
        xpad_ready = [sem("xpad_ready_act"), sem("xpad_ready_dve")]
        win_made, win_ready = sem("win_made"), sem("win_ready")
        up_made, relu_ready, up_read = sem("up_made"), sem("relu_ready"), sem("up_read")
        y_ready = sem("y_ready")
        z_made, z_ready = sem("z_made"), sem("z_ready")

        ctx.enter_context(nc.allow_non_contiguous_dma(reason="weights and small layouts"))
        block = ctx.enter_context(nc.Block())

        def tiles(w):
            return w.rearrange("(t p) n -> p t n", p=P)

        def cols(v):
            return v.rearrange("(t p) -> p t", p=P)

        def row(v):
            return v.rearrange("(a n) -> a n", a=1)

        def token_tile(nt):
            start = 2 * P * (nt // 2) + nt % 2
            return slice(start, start + 2 * P - 1, 2)

        def carry(eng, mine):
            k = carried[mine] % 8
            carried[mine] += 1
            eng.tensor_tensor(idle[mine][:, k:k + 1], ident[:, 0:1], ident[:, 1:2], ALU.mult)

        def ring(n, k):
            return x_ring[n % 3][:, k, :].rearrange("p (t s) -> p t s", t=CT)

        def xT_ring(n, k):
            if n % 3 < 2:
                return reg_f[:, 2 * (n % 3) + k, :]
            return reg_y_r[:, 6 * AGS + HALF * k:6 * AGS + HALF * k + HALF]

        def pT_ring(n, k):
            if n % 4 < 2:
                return part(NT * (C + AGS) + AGS * (2 * (n % 4) + k), AGS, of=reg_a_r)
            return g_k_lo[:, 2 * (n % 4 - 2) + k, :]

        def xT_low_part(eng, n):
            return eng.tensor_tensor(xT_ring(n, 1), xT[:, n, :], xT_ring(n, 0).bitcast(F32), ALU.subtract)

        def flat(ap):
            return ap.rearrange("p t n -> p (t n)")

        @block.sync
        def _(sp):
            def load_x(i, first=False):
                for t in range(CT):
                    sp.dma_start(xin[:, t, :], x[i].rearrange("(t p) n -> t p n", p=P)[t])\
                        .then_inc(x_first[t] if first else x_loaded, 16)

            def load_pw():
                sp.dma_start(w_pwT, tiles(pwT)).then_inc(pw_load, 16)

            def mix_bounce(i):
                sp.wait_ge(mix_ready, i + 1)
                sp.dma_start(agent_dram[1].rearrange("(a c) -> a c", a=AG), mix_out).then_inc(mix_stored, 16)
                sp.wait_ge(mix_stored, 16 * i + 16)
                sp.dma_start(mix_in.rearrange("p t i j -> p t (i j)"),
                             agent_dram[1].rearrange("(t p a) -> p t a", t=CT, p=P)).then_inc(mix_loaded, 16)

            def agent_bounce(i, first=False):
                sp.wait_ge(pwo_ready, i + 1)
                sp.dma_start(agent_dram[0].rearrange("(t p a) -> p t a", t=CT, p=P), pwo).then_inc(at_stored, 16)
                sp.wait_ge(at_stored, 16 * i + 16)
                if not first:
                    sp.wait_ge(at_turned, i)
                for hh in range(2):
                    src = agent_dram[0].rearrange("(t h i d) -> h i t d", t=HEADS // 2, h=2, i=AG)[hh]
                    sp.dma_start(at_in[AG * hh:AG * hh + AG, :, HD * hh:HD * hh + HD], src).then_inc(at_loaded, 16)

            def store(b, pair, half):
                sp.wait_ge(z_ready, 12 * b + 6 * pair + (4 if half == 0 else 6))
                for c in range(2):
                    t = 2 * pair + c
                    sp.dma_start(out[b].rearrange("(t p) n -> t p n", p=P)[t, :, HALF * half:HALF * half + HALF],
                                 x2[:, t, HALF * half:HALF * half + HALF]).then_inc(x2_moved, 16)

            load_x(0, first=True)
            sp.wait_ge(pool_setup, 1)
            sp.dma_start(m_bias[0:AG, :], row(proj_b).broadcast_to([AG, C])).then_inc(row_load, 16)
            sp.dma_start(x2[0:AG, 0, 0:C], row(enh2_b).broadcast_to([AG, C])).then_inc(x2_moved, 16)
            sp.dma_start(filt_dram, fzero).then_inc(f_store, 16)
            sp.wait_ge(f_store, 16)
            for j, f in enumerate((up_f, down_f)):
                sp.dma_start(filt_dram[j:j + 1, 16:16 + TAPS], row(f)).then_inc(f_store, 16)
            sp.wait_ge(f_store, 48)
            for j in range(2):
                for dst, start, steps in ((frow[j], 10, [[2, WH], [0, WW], [1, 2 * MR]]),
                                          (fcol[j], 2, [[0, WH], [2, WW], [1, 2 * MC]])):
                    sp.dma_start(dst,
                                 bass.AP(tensor=filt_dram.tensor, offset=FILT * j + start, ap=steps)).then_inc(f_load, 16)
            mix_bounce(0)
            agent_bounce(0, first=True)

            def image(b, ahead):
                sp.wait_ge(px_made, CT * (b + 1))
                for pair in range(2):
                    sp.dma_start(xwin[WIN_N + pair:WIN_N + pair + 1].rearrange("p k (j c) -> p (k j) c", j=2),
                                 bass.AP(tensor=bias.tensor, offset=2 * P * pair, ap=[[0, 2 * RING], [1, 2 * P]]))\
                        .then_inc(bias_load, 16)
                if ahead:
                    sp.wait_ge(x2_ready, 8 * b + 8)
                    load_x(b + 1)
                    load_pw()
                store(b, 0, 0)
                store(b, 0, 1)
                if ahead:
                    mix_bounce(b + 1)
                store(b, 1, 0)
                if ahead:
                    agent_bounce(b + 1)
                store(b, 1, 1)

            with sp.Fori(0, B - 1, 1) as b:
                image(b, True)
            image(B - 1, False)
            sp.wait_ge(x2_moved, 16 + 16 * 8 * B)

        @block.gpsimd
        def _(pool):
            links = [0]

            def link(ins, base, carried=True):
                links[0] += 1
                ins.then_inc(pchain, 1)
                pool.wait_ge(pchain, base + links[0])
                if not carried:
                    carry(pool, 0)

            pool.memset(ident[:], 0.0)
            pool.memset(gmean[:], 1.0 / GROUP)
            pool.memset(ones[:], 1.0)
            pool.memset(op_up[:], 1.0)
            for t in (m_bias, agg):
                pool.memset(t[:], 0.0)
            link(pool.memset(fzero, 0.0), 0)
            for i, (r0, r1) in enumerate(WIN):
                for par_j in range(2):
                    c0, c1 = WIN[par_j]
                    n = (r1 - r0) * (c1 - c0)
                    pool.memset(area[:, i, par_j:POOL:2], 1.0 / n)
            link(pool.affine_select(out=ident[:], in_=ident[:], compare_op=ALU.not_equal, fill=1.0, base=0,
                                    pattern=[[-1, P]], channel_multiplier=1), 0)
            gv = gmean[:].rearrange("p (g c) -> p g c", c=GROUP)
            link(pool.affine_select(out=gv, in_=gv, compare_op=ALU.is_ge, fill=0.0, base=0,
                                    pattern=[[-GROUP, P // GROUP], [0, GROUP]], channel_multiplier=1), 0)
            pool.affine_select(out=op_up[:, 0], in_=op_up[:, 0], compare_op=ALU.is_ge, fill=0.0, base=WIN_N,
                               pattern=[[0, PT_N]], channel_multiplier=-1)
            pool.affine_select(out=op_up[:, 1], in_=op_up[:, 1], compare_op=ALU.is_ge, fill=0.0, base=-WIN_N - 1,
                               pattern=[[0, PT_N]], channel_multiplier=1)
            pool.affine_select(out=gv, in_=gv, compare_op=ALU.is_ge, fill=0.0, base=GROUP - 1,
                               pattern=[[GROUP, P // GROUP], [0, GROUP]], channel_multiplier=-1).then_inc(pool_setup, 1)

            def agent_conv(i, base):
                pool.wait_ge(pool_ready, i + 1)
                carry(pool, 0)
                pool.memset(at_in, 0.0)
                link(pool.tensor_tensor(pooled.rearrange("p t i j -> p t (i j)"), pooled.rearrange("p t i j -> p t (i j)"),
                                        area[:].rearrange("p i j -> p (i j)").rearrange("p (o n) -> p o n", o=1)
                                        .broadcast_to([P, CT, AG]), ALU.mult), base)
                pool.wait_ge(norm_ready, i + 1)
                carry(pool, 0)
                for t in range(CT):
                    ins = pool.tensor_scalar(pooled[:, t], pooled[:, t], rstd[0][:, t:t + 1],
                                             shift[0][:, t:t + 1], ALU.mult, ALU.add)
                ins.then_inc(pn_ready, 1)
                pool.wait_ge(mix_loaded, 16 * i + 16)
                carry(pool, 0)
                link(pool.memset(cpad, 0.0), base, carried=False)
                for t in range(CT):
                    ins = pool.tensor_copy(cpad[:, t, 1:1 + POOL, 1:1 + POOL], mix_in[:, t])
                link(ins, base)
                pool.wait_ge(v_tap, 1)
                for k in range(9):
                    win = cpad[:, :, k // 3:k // 3 + POOL, k % 3:k % 3 + POOL]
                    tap = tapw[:, :, k:k + 1].rearrange("p t (a b) -> p t a b", a=1).broadcast_to([P, CT, POOL, POOL])
                    if k == 0:
                        link(pool.tensor_tensor(conv, win, tap, ALU.mult), base)
                    else:
                        link(pool.tensor_tensor(ctmp, win, tap, ALU.mult), base)
                        link(pool.tensor_tensor(conv, conv, ctmp, ALU.add), base)
                c3 = conv.rearrange("p t i j -> p t (i j)")
                tb = tapb[:].rearrange("p (t o) -> p t o", o=1).broadcast_to([P, CT, AG])
                link(pool.tensor_tensor(c3, c3, tb, ALU.add), base, carried=False)
                pool.tensor_scalar(c3, c3, 0.0, None, ALU.max).then_inc(conv_ready, 1)

            agent_conv(0, 0)
            assert links[0] == PCHAIN_BEFORE, ("PCHAIN_BEFORE", links[0])

            def image(b, ahead):
                links[0] = 0
                base = PCHAIN_BEFORE + PCHAIN_IMAGE * b
                for n in range(NT):
                    pool.wait_ge(qrec_ready, NT * b + n + 1)
                    e = qp[:, n % 4, :].rearrange("p (h a) -> p h a", h=HEADS)
                    r = qsum[:, n % 2, :].rearrange("p (h o) -> p h o", o=1).broadcast_to([P, HEADS, AG])
                    pool.tensor_tensor(e, e, r, ALU.mult).then_inc(qp_ready, 1)
                    if n == NT - 1:
                        for k in range(1, NT):
                            if k in (1, 3, 5):
                                pool.wait_ge(xT_high, NT * b + k + 3)
                                xT_low_part(pool, k + 2).then_inc(xT_low[1], 1)
                            pool.wait_ge(kexp_ready, NT * b + k + 1)
                            ins = pool.tensor_tensor(ksum_run, pT[:, 0, :] if k == 1 else ksum_run, pT[:, k, :], ALU.add)
                            if k < NT - 1:
                                link(ins, base)
                        ins.then_inc(ksum_run_ready, 1)

                def border(t):
                    pool.memset(xpad_run[:, t, :, 0:5 * WW], 0.0)
                    pool.memset(xpad_run[:, t, :, (5 + H) * WW:BAND_N], 0.0)
                    pool.memset(xpad[:, t, 0, 5:5 + H, 0:SPANS[0][1]], 0.0)
                    pool.memset(xpad[:, t, len(COLS) - 1, 5:5 + H, SPANS[-1][2]:WW], 0.0).then_inc(border_ready, 1)

                pool.wait_ge(agg_made, b + 1)
                carry(pool, 0)
                border(0)
                border(1)
                for i in range(8):
                    nh, f = i // 4, i % 4
                    cs = slice(HALF * nh, HALF * nh + HALF)
                    pool.wait_ge(h1_full, 8 * b + i + 1)
                    pool.tensor_tensor(h1_lo[:, f, cs], h1_tmp[:, i % 2, :], h1_hi[:, f, cs].bitcast(F32), ALU.subtract)\
                        .then_inc(h1_low, 1)

                pool.wait_ge(x2_ready, NT * b + NT)
                carry(pool, 0)
                border(2)
                border(3)
                if ahead:
                    agent_conv(b + 1, base)
                if ahead:
                    assert links[0] == PCHAIN_IMAGE, ("PCHAIN_IMAGE", links[0])

            with pool.Fori(0, B - 1, 1) as b:
                image(b, True)
            image(B - 1, False)

        @block.scalar
        def _(act):
            def copy(out_, in_, scale=1.0):
                return act.activation(out_, in_, ACT.Copy, scale=scale)

            def norm_x(i, t):
                act.wait_ge(norm_ready, i + 1)
                act.activation(xn[:, t, :], xin[:, t, :], ACT.Identity, scale=rstd[0][:, t:t + 1],
                               bias=shift[0][:, t:t + 1]).then_inc(xn_ready, 1)

            def turn_agents(i):
                act.wait_ge(at_turned, i + 1)
                copy(at_bd, psum[:, 1, 0:AGS].rearrange("p (t a) -> p t a", a=PAIR), SCALE).then_inc(at_ready, 1)

            def g_copy(i, g):
                act.wait_ge(g_made, 8 * i + g + 1)
                copy((g_k_hi if g < CT else g_q_hi)[:, g % CT, :], psum[:, 4 + g % 4, 0:AGS]).then_inc(g_high, 1)

            def x_split(i, n):
                if n == 0:
                    act.wait_ge(xn_ready, CT * (i + 1))
                if n >= 3:
                    act.wait_ge(sq_made, NT * i + n - 2)
                copy(ring(n, 0), xn[:, :, token_tile(n)]).then_inc(x_high, 1)

            act.dma_start(tapw[:], dw_w.rearrange("(t p) k -> p t k", p=P)).then_inc(par_load, 16)
            for j, v in enumerate((dw_b, bn_g, bn_b, bn_m, bn_v, pw_b, enh1_b, proj_b)):
                act.dma_start(par[:, j, :], cols(v)).then_inc(par_load, 16)
            for dst, src, loaded in ((pw_in, proj, p1_load), (p1_in, w1T, p1_load), (w_pwT, pwT, pw_load), (w_k[:], wk, kq_load),
                                     (w_q[:], wq, kq_load), (w_vT[:], wvT, v_load), (w_projT[:], projT, proj_load),
                                     (w2_in, w2T, w2_load)):
                act.dma_start(dst, tiles(src)).then_inc(loaded, 16)
            for t in range(CT):
                norm_x(0, t)
            turn_agents(0)
            x_split(0, 0)
            x_split(0, 1)
            for g in range(8):
                g_copy(0, g)

            def image(b, ahead):
                def xT_copy(n):
                    act.wait_ge(xT_made, NT * b + n + 1)
                    copy(xT[:, n, :], psum[:, 4, :]).then_inc(xT_ready[0], 1)

                def sT_copy(n):
                    act.wait_ge(sk_made, NT * b + n + 1)
                    copy(pT[:, n, :], psum[:, n % 2, 0:AGS]).then_inc(sT_ready, 1)


                def k_exp(n):
                    act.wait_ge(ksub_ready, NT * b + n + 1)
                    act.activation(pT[:, n, :], pT[:, n, :], ACT.Exp).then_inc(kexp_ready, 1)

                def q_exp(n):
                    act.wait_ge(qsub_ready, NT * b + n + 1)
                    act.activation(qp[:, n % 4, :], qp[:, n % 4, :], ACT.Exp).then_inc(qexp_ready, 1)

                def xT_split(n):
                    act.wait_ge(xT_ready[n % 2], 4 * b + n // 2 + 1)
                    if n < 3:
                        act.wait_ge(sq_made, NT * b + (7 if n == 0 else 8))
                    else:
                        act.wait_ge(px_step, 7 * b + n - 2)
                    copy(xT_ring(n, 0), xT[:, n, :]).then_inc(xT_high, 1)

                def p_split(n):
                    act.wait_ge(kexp_ready, NT * b + n + 1)
                    copy(pT_ring(n, 0), pT[:, n, :]).then_inc(p_high, 1)

                def px_copy(t):
                    act.wait_ge(px_made, 4 * b + t + 1)
                    copy(pxT[:, t, :], psum[:, PX_BANKS[t], 0:AGS]).then_inc(px_ready, 1)

                def qT_copy(n):
                    act.wait_ge(qT_made, NT * b + n + 1)
                    copy(qT_hi[0:PAIR, n], psum[0:PAIR, 6, :].rearrange("p (t n) -> p t n", t=4))\
                        .then_inc(qT_ready[0], 1)

                for n in range(NT):
                    if 2 <= n + 1 < NT:
                        x_split(b, n + 1)
                    sT_copy(n)
                    if n % 2 == 0:
                        xT_copy(n)
                    if n:
                        q_exp(n - 1)
                    if n >= 3 and n % 2:
                        qT_copy(n - 3)
                xT_split(0)
                k_exp(0)
                p_split(0)
                xT_split(1)
                k_exp(1)
                p_split(1)
                q_exp(7)
                for n in range(2, NT):
                    xT_split(n)
                    k_exp(n)
                    p_split(n)
                    if n == 2:
                        qT_copy(6)
                for t in range(4):
                    px_copy(t)
                act.wait_ge(krec_ready, b + 1)
                for t in range(4):
                    act.wait_ge(f_made, 4 * b + t + 1)
                    copy(f_hi[:, t, :], psum[0:PAIR, 4 + t, :], krec[:, t:t + 1]).then_inc(f_ready, 1)
                for t in range(1, 4):
                    act.wait_ge(m_made, 4 * b + t + 1)
                    copy(m_hi[:, t, :], psum[0:PAIR, t, :], krec[:, t:t + 1]).then_inc(m_high, 1)
                for i in range(8):
                    nh, f = i // 4, i % 4
                    act.wait_ge(h1_made, 8 * b + i + 1)
                    act.activation(h1_hi[:, f, HALF * nh:HALF * nh + HALF], psum[:, (4 + i) % 8, :], ACT.Relu,
                                   bias=b1p[:, f:f + 1]).then_inc(h1_ready, 1)
                def pad(t, n):
                    c0, at, cn = SPANS[n]
                    act.activation(xpad[:, t, n, 5:5 + H, at:at + cn],
                                   x2[:, t, :].rearrange("p (h w) -> p h w", h=H)[:, :, c0:c0 + cn],
                                   ACT.Identity, scale=rstd[1][:, t:t + 1], bias=shift[1][:, t:t + 1])\
                        .then_inc(xpad_ready[0], 1)

                act.wait_ge(norm1_ready, 2 * b + 1)
                for n in range(len(COLS)):
                    pad(0, n)

                def win_copy(s):
                    act.wait_ge(win_made, STEPS * b + s + 1)
                    copy(xwin[0:WIN_N, s % RING, :], psum[0:WIN_N, 4 + s % 2, :]).then_inc(win_ready, 1)

                def relu(s):
                    act.wait_ge(up_made, STEPS * b + s + 1)
                    act.activation(ypt[:, s % RING, :], psum[:, 6 + s % 2, :], ACT.Relu, scale=1.0 - SLOPE)\
                        .then_inc(relu_ready, 1)

                win_copy(0)
                win_copy(1)
                relu(0)
                for s in range(STEPS):
                    if s + 2 < STEPS:
                        win_copy(s + 2)
                    if s + 1 < STEPS:
                        relu(s + 1)
                    if PAD1_AT <= s < PAD1_AT + len(COLS):
                        if s == PAD1_AT:
                            act.wait_ge(norm1_ready, 2 * b + 2)
                        pad(2, s - PAD1_AT)
                    if ahead:
                        if XN_AT <= s < XN_AT + CT:
                            norm_x(b + 1, s - XN_AT)
                        if s == TURN_AT:
                            turn_agents(b + 1)
                if ahead:
                    x_split(b + 1, 0)
                    x_split(b + 1, 1)
                    for g in range(8):
                        g_copy(b + 1, g)

            act.wait_ge(v_b1, 1)
            with act.Fori(0, B - 1, 1) as b:
                image(b, True)
            image(B - 1, False)

        @block.vector
        def _(dve):
            links = [0]

            def link(ins, base, carried=True):
                links[0] += 1
                ins.then_inc(chain, 1)
                dve.wait_ge(chain, base + links[0])
                if not carried:
                    carry(dve, 1)

            def rsqrt(v, y, base, part=None):
                a, c = nt1[:, 0:v.shape[1]], nt2[:, 0:v.shape[1]]
                if part in (None, 0):
                    link(dve.tensor_scalar(a.bitcast(U32), v.bitcast(U32), 1, None, ALU.logical_shift_right), base)
                    link(dve.tensor_scalar(y.bitcast(I32), a.bitcast(I32), -1.0, float(0x5F3759DF), ALU.mult, ALU.add), base)
                    link(dve.tensor_scalar(v, v, -0.5, None, ALU.mult), base)
                for step in range(1, 4):
                    if part in (None, step):
                        link(dve.tensor_tensor(a, y, v, ALU.mult), base)
                        link(dve.tensor_tensor(c, a, y, ALU.mult), base)
                        link(dve.scalar_tensor_tensor(y, c, 1.5, y, ALU.add, ALU.mult), base)

            def bn_stats(src, t, half):
                return dve.bn_stats(bns[:, t, half, :], src[:, t, HALF * half:HALF * half + HALF])

            def channel_stats(tiles_, base, ready):
                for t in tiles_:
                    ins = dve.bn_aggr(stat[:, t, :], bns[:, t])
                ts = slice(tiles_[0], tiles_[-1] + 1)
                link(ins, base)
                link(dve.tensor_tensor(nt1[:, 0:len(tiles_)], stat[:, ts, 0], stat[:, ts, 0], ALU.mult), base)
                dve.tensor_tensor(stat[:, ts, 1], stat[:, ts, 1], nt1[:, 0:len(tiles_)], ALU.add).then_inc(ready, 1)

            def group_norm(made, i, bank, which, tiles_, base, ready, part=None):
                n = len(tiles_)
                ts = slice(tiles_[0], tiles_[-1] + 1)
                if part in (None, 0):
                    dve.wait_ge(made, i + 1)
                    dve.tensor_copy(gs[:, ts, :].rearrange("p t s -> p (t s)"), psum[:, bank, 0:2 * n])\
                        .then_inc(gs_read[which], 1)
                    dve.wait_ge(gs_read[which], i + 1)
                    link(dve.tensor_tensor(nt1[:, 0:n], gs[:, ts, 0], gs[:, ts, 0], ALU.mult), base)
                    link(dve.scalar_tensor_tensor(nv[:, 0:n], gs[:, ts, 1], GN_EPS, nt1[:, 0:n], ALU.add, ALU.subtract), base)
                if part is None:
                    rsqrt(nv[:, 0:n], rstd[which][:, ts], base)
                elif 1 <= part <= 4:
                    rsqrt(nv[:, 0:n], rstd[which][:, ts], base, part - 1)
                if part in (None, NORM_PARTS - 1):
                    dve.scalar_tensor_tensor(shift[which][:, ts], gs[:, ts, 0], -1.0, rstd[which][:, ts], ALU.mult, ALU.mult)\
                        .then_inc(ready, 1)

            def pool_rows(i_img, i):
                r0, r1 = WIN[i]
                src = xin[:].rearrange("p t (h w) -> p t w h", h=H)[:, :, :, r0:r1]
                return dve.tensor_reduce(rowsum[:, :, i, :], src, AX.X, ALU.add)

            def pool_cols(j):
                c0, c1 = WIN[j]
                return dve.tensor_reduce(pooled.rearrange("p t i j -> p (t i) j")[:, :, j:j + 1],
                                         rowsum.rearrange("p t i w -> p (t i) w")[:, :, c0:c1], AX.X, ALU.add)

            def mix_copy(i, bank):
                dve.wait_ge(mix_made, i + 1)
                dve.tensor_copy(mix_out, psum[0:AG, bank, :]).then_inc(mix_ready, 1)

            def pwo_copy(i, bank, first=False):
                dve.wait_ge(pw_ready, i + 1)
                if not first:
                    dve.wait_ge(at_loaded, 32 * i)
                dve.tensor_tensor(pwo, psum[:, bank, 0:CT * AG].rearrange("p (t a) -> p t a", t=CT),
                                  par[:, 5, :].rearrange("p (t o) -> p t o", o=1).broadcast_to([P, CT, AG]), ALU.add)\
                    .then_inc(pwo_ready, 1)

            def x_rest(i, n):
                dve.wait_ge(x_high, NT * i + n + 1)
                dve.tensor_tensor(ring(n, 1), xn[:, :, token_tile(n)], ring(n, 0).bitcast(F32), ALU.subtract)\
                    .then_inc(x_low, 1)

            def g_rest(i, g):
                dve.wait_ge(g_high, 8 * i + g + 1)
                hi, lo = (g_k_hi, g_k_lo) if g < CT else (g_q_hi, g_q_lo)
                dve.tensor_tensor(lo[:, g % CT, :], psum[:, 4 + g % 4, 0:AGS], hi[:, g % CT, :].bitcast(F32), ALU.subtract)\
                    .then_inc(g_low, 1)

            dve.wait_ge(pool_setup, 1)
            for t in range(CT):
                dve.wait_ge(x_first[t], 16)
                for half in range(2):
                    ins = bn_stats(xin, t, half)
            link(ins, 0)
            channel_stats(range(CT), 0, stat_ready)
            for i in range(POOL):
                ins = pool_rows(0, i)
            link(ins, 0)
            for j in range(POOL):
                ins = pool_cols(j)
            ins.then_inc(pool_ready, 1)
            group_norm(gstat_ready, 0, 4, 0, range(CT), 0, norm_ready)
            dve.wait_ge(par_load, 16 * 9)
            link(dve.tensor_scalar(nv, par[:, 4, :], BN_EPS, None, ALU.add), 0)
            rsqrt(nv, ny, 0)
            link(dve.tensor_tensor(ny, ny, par[:, 1, :], ALU.mult), 0)
            link(dve.tensor_tensor(nt1, par[:, 0, :], par[:, 3, :], ALU.subtract), 0)
            link(dve.tensor_tensor(nt1, nt1, ny, ALU.mult), 0)
            link(dve.tensor_tensor(tapb[:], nt1, par[:, 2, :], ALU.add), 0)
            dve.tensor_tensor(tapw[:], tapw[:], ny.rearrange("p (t o) -> p t o", o=1).broadcast_to([P, CT, 9]),
                              ALU.mult).then_inc(v_tap, 1)
            mix_copy(0, 7)
            for t in range(CT):
                dve.wait_ge(pe_p1, t + 1)
                dve.tensor_copy(w_p1[:, t, :], psum[:, t, :]).then_inc(v_p1, 1)
            dve.wait_ge(pe_b1, 1)
            dve.tensor_tensor(b1p[:], psum[:, 6, 0:CT], par[:, 6, :], ALU.add).then_inc(v_b1, 1)
            dve.wait_ge(f_load, 16 * 4)
            for j, dst, gain in ((0, op_up[0:WIN_N, 0], 4.0), (0, op_up[0:WIN_N, 1], 4.0), (1, x2[0:WIN_N, 1, 0:PT_N], ROOT2)):
                ins = dve.scalar_tensor_tensor(
                    dst.rearrange("p (r s) -> p r s", r=2 * MR),
                    frow[j].rearrange("p (r o) -> p r o", o=1).broadcast_to([WIN_N, 2 * MR, 2 * MC]), gain,
                    fcol[j].rearrange("p (o s) -> p o s", o=1).broadcast_to([WIN_N, 2 * MR, 2 * MC]), ALU.mult, ALU.mult)
            ins.then_inc(v_op, 1)
            dve.wait_ge(row_load, 16)
            dve.wait_ge(x2_moved, 16)
            dve.tensor_tensor(m_bias[0:AG, :], m_bias[0:AG, :], x2[0:AG, 0, 0:C], ALU.add).then_inc(v_bias, 1)
            pwo_copy(0, 5, first=True)
            dve.wait_ge(pe_dn, 1)
            dve.tensor_copy(op_dn[:].rearrange("p a b -> p (a b)"), psum[:, 6, 0:WIN_N]).then_inc(v_dn, 1)
            dve.wait_ge(w2_load, 16)
            link(dve.tensor_copy(flat(w_2T_hl[:, 0]), flat(w2_in)), 0)
            dve.tensor_tensor(flat(w_2T_hl[:, 1]), flat(w2_in), flat(w_2T_hl[:, 0]).bitcast(F32), ALU.subtract).then_inc(w_split, 1)
            x_rest(0, 0)
            x_rest(0, 1)
            for g in range(8):
                g_rest(0, g)
            assert links[0] == CHAIN_BEFORE, ("CHAIN_BEFORE", links[0])

            def image(b, ahead):
                links[0] = 0
                base = CHAIN_BEFORE + CHAIN_IMAGE * b

                def k_max(n):
                    dve.wait_ge(sT_ready, NT * b + n + 1)
                    ins = dve.tensor_tensor(kmax_run, pT[:, 0, :] if n == 1 else kmax_run, pT[:, n, :], ALU.max)
                    if n < NT - 1:
                        link(ins, base)
                    else:
                        ins.then_inc(kmax_run_ready, 1)

                def k_max_end():
                    dve.wait_ge(kmax_turned, b + 1)
                    dve.tensor_reduce(kmax[:], psum[0:PAIR, 0, :].rearrange("p (t n) -> p t n", t=4), AX.X, ALU.max)\
                        .then_inc(kmax_ready, 1)

                def k_sub(n):
                    if n == 0:
                        dve.wait_ge(kmax_spread, b + 1)
                    dve.tensor_tensor(pT[:, n, :], pT[:, n, :], psum[:, 1, 0:AGS], ALU.subtract).then_inc(ksub_ready, 1)

                def xT_copy(n):
                    dve.wait_ge(xT_made, NT * b + n + 1)
                    dve.tensor_copy(xT[:, n, :], psum[:, 5, :]).then_inc(xT_ready[1], 1)

                def q_sub(n):
                    dve.wait_ge(sq_made, NT * b + n + 1)
                    s = psum[:, 2 + n % 2, 0:AGS].rearrange("p (h a) -> p h a", h=HEADS)
                    link(dve.tensor_reduce(qmax[:, n % 2, :].rearrange("p (h o) -> p h o", o=1), s, AX.X, ALU.max), base)
                    dve.tensor_tensor(qp[:, n % 4, :].rearrange("p (h a) -> p h a", h=HEADS), s,
                                      qmax[:, n % 2, :].rearrange("p (h o) -> p h o", o=1).broadcast_to([P, HEADS, AG]),
                                      ALU.subtract).then_inc(qsub_ready, 1)

                def q_sum(n):
                    dve.wait_ge(qexp_ready, NT * b + n + 1)
                    if n >= 2:
                        dve.wait_ge(qp_ready, NT * b + n - 1)
                    link(dve.tensor_reduce(qsum[:, n % 2, :].rearrange("p (h o) -> p h o", o=1),
                                           qp[:, n % 4, :].rearrange("p (h a) -> p h a", h=HEADS), AX.X, ALU.add), base)
                    dve.reciprocal(qsum[:, n % 2, :], qsum[:, n % 2, :]).then_inc(qrec_ready, 1)

                def qT_rest(n):
                    hi, src = qT_hi[0:PAIR, n], psum[0:PAIR, 6 + n % 2, :].rearrange("p (t n) -> p t n", t=4)
                    if n % 2:
                        dve.wait_ge(qT_made, NT * b + n + 1)
                        dve.tensor_copy(hi, src).then_inc(qT_ready[1], 1)
                    dve.wait_ge(qT_ready[n % 2], 4 * b + n // 2 + 1)
                    dve.tensor_tensor(qT_lo[0:PAIR, n], src, hi.bitcast(F32), ALU.subtract).then_inc(qT_low, 1)

                for n in range(NT):
                    if 2 <= n + 1 < NT:
                        x_rest(b, n + 1)
                    if n:
                        k_max(n)
                    if n % 2:
                        xT_copy(n)
                    if n == NT - 1:
                        q_sum(5)
                        q_sub(6)
                        k_max_end()
                    elif n:
                        q_sub(n - 1)
                        if n > 1:
                            q_sum(n - 2)
                    if n == 3:
                        dve.wait_ge(x2_moved, 16 + 16 * 8 * b)
                    if n >= 3:
                        qT_rest(n - 3)
                def xT_rest(n):
                    dve.wait_ge(xT_high, NT * b + n + 1)
                    xT_low_part(dve, n).then_inc(xT_low[0], 1)

                def p_rest(n):
                    dve.wait_ge(p_high, NT * b + n + 1)
                    dve.tensor_tensor(pT_ring(n, 1), pT[:, n, :], pT_ring(n, 0).bitcast(F32), ALU.subtract)\
                        .then_inc(p_low, 1)

                q_sum(6)
                k_sub(0)
                xT_rest(0)
                k_sub(1)
                p_rest(0)
                q_sub(7)
                k_sub(2)
                xT_rest(1)
                p_rest(1)
                q_sum(7)
                for n in range(2, NT):
                    if n + 1 < NT:
                        k_sub(n + 1)
                    if n in VECTOR_XT:
                        xT_rest(n)
                    p_rest(n)
                    if n == 3:
                        qT_rest(5)
                    if n == 5:
                        qT_rest(6)
                qT_rest(7)
                dve.wait_ge(agg_made, b + 1)
                for hh in range(2):
                    r, c = slice(HD * hh, HD * hh + HD), slice(AG * hh, AG * hh + AG)
                    ins = dve.tensor_copy(agg[r, :, c], psum[r, 0, 0:AGS].rearrange("p (t a) -> p t a", a=PAIR)[:, :, c])
                ins.then_inc(agg_ready, 1)
                dve.wait_ge(ksum_made, b + 1)
                dve.reciprocal(krec[:], psum[0:PAIR, 1, 0:CT]).then_inc(krec_ready, 1)
                dve.wait_ge(krec_ready, b + 1)

                def rest(low, high, src, t, ready, n):
                    dve.wait_ge(ready, n)
                    return dve.scalar_tensor_tensor(low[:, t, :], src, krec[:, t:t + 1], high[:, t, :].bitcast(F32),
                                                    ALU.mult, ALU.subtract)

                for t in range(4):
                    rest(f_lo, f_hi, psum[0:PAIR, 4 + t, :], t, f_ready, 4 * b + t + 1).then_inc(f_low, 1)
                dve.wait_ge(m_made, 4 * b + 1)
                link(dve.scalar_tensor_tensor(m_tmp, psum[0:PAIR, 0, :], krec[:, 0:1], m_bias[:], ALU.mult, ALU.add), base)
                link(dve.tensor_copy(m_hi[:, 0, :], m_tmp), base)
                link(dve.tensor_tensor(m_lo[:, 0, :], m_tmp, m_hi[:, 0, :].bitcast(F32), ALU.subtract), base, carried=False)

                def h1_again(i):
                    dve.wait_ge(h1_ready, 8 * b + i + 1)
                    if i >= 2:
                        dve.wait_ge(h1_low, 8 * b + i - 1)
                    dve.tensor_scalar(h1_tmp[:, i % 2, :], psum[:, (4 + i) % 8, :], b1p[:, i % 4:i % 4 + 1], 0.0,
                                      ALU.add, ALU.max).then_inc(h1_full, 1)

                for t in range(1, 4):
                    rest(m_lo, m_hi, psum[0:PAIR, t, :], t, m_high, 3 * b + t).then_inc(m_low, 1)
                for i in range(8):
                    h1_again(i)

                def pad(t, n):
                    c0, at, cn = SPANS[n]
                    dve.tensor_scalar(xpad[:, t, n, 5:5 + H, at:at + cn],
                                      x2[:, t, :].rearrange("p (h w) -> p h w", h=H)[:, :, c0:c0 + cn],
                                      rstd[1][:, t:t + 1], shift[1][:, t:t + 1], ALU.mult, ALU.add)\
                        .then_inc(xpad_ready[1], 1)

                for i in range(NT):
                    t, cs = i // 2, slice(HALF * (i % 2), HALF * (i % 2) + HALF)
                    dve.wait_ge(o_made, NT * b + i + 1)
                    dve.tensor_tensor(x2[:, t, cs], psum[:, (4 + i) % 8, :], xin[:, t, cs], ALU.add).then_inc(x2_ready, 1)
                    if i:
                        dve.wait_ge(x2_ready, NT * b + i)
                        ins = bn_stats(x2, (i - 1) // 2, (i - 1) % 2)
                    if i == 4:
                        link(ins, base, carried=False)
                        channel_stats(range(2), base, stat1_ready)
                    if i == 5:
                        group_norm(gstat1_ready, 2 * b, 7, 1, range(2), base, norm1_ready)
                        dve.wait_ge(norm1_ready, 2 * b + 1)
                        for n in range(len(COLS)):
                            pad(1, n)
                dve.wait_ge(x2_ready, NT * b + NT)
                link(bn_stats(x2, CT - 1, 1), base, carried=False)
                channel_stats(range(2, CT), base, stat1_ready)

                def leaky(s):
                    dve.wait_ge(relu_ready, STEPS * b + s + 1)
                    y = ypt[:, s % RING, :]
                    dve.scalar_tensor_tensor(y, psum[:, 6 + s % 2, :], SLOPE, y, ALU.mult, ALU.add).then_inc(up_read, 1)

                def clamp(s):
                    dve.wait_ge(up_read, STEPS * b + s + 1)
                    y = ypt[:, s % RING, :]
                    dve.tensor_scalar(y, y, CLAMP / ROOT2, -CLAMP / ROOT2, ALU.min, ALU.max).then_inc(y_ready, 1)

                def z_add(pair, z):
                    dve.wait_ge(z_made, 6 * b + 3 * pair + z + 1)
                    if z:
                        dve.wait_ge(z_ready, 12 * b + 6 * pair + 2 * z)
                    r0, r1 = SECTION_ROWS[z]
                    for c in range(2):
                        xs = x2[:, 2 * pair + c, W * r0:W * r1]
                        dve.tensor_tensor(xs, psum[:, z_bank(pair, z, c), 0:W * (r1 - r0)], xs, ALU.add).then_inc(z_ready, 1)

                for s in range(STEPS):
                    leaky(s)
                    clamp(s)
                    if s in Z_AT:
                        z_add(*Z_AT[s])
                    if 0 <= s - NORM1_AT < NORM_PARTS:
                        group_norm(gstat1_ready, 2 * b + 1, 3, 1, range(2, CT), base, norm1_ready, s - NORM1_AT)
                    if 0 <= s - PAD1_AT < len(COLS):
                        if s == PAD1_AT:
                            dve.wait_ge(norm1_ready, 2 * b + 2)
                        pad(3, s - PAD1_AT)
                    if not ahead:
                        continue
                    if 0 <= s - BN_AT < 2 * CT:
                        if s == BN_AT:
                            dve.wait_ge(x_loaded, 16 * CT * (b + 1))
                        ins = bn_stats(xin, (s - BN_AT) // 2, (s - BN_AT) % 2)
                        if s == BN_AT + 2 * CT - 1:
                            link(ins, base, carried=False)
                            channel_stats(range(CT), base, stat_ready)
                    if 0 <= s - ROWS_AT < POOL:
                        ins = pool_rows(b + 1, s - ROWS_AT)
                        if s == ROWS_AT + POOL - 1:
                            link(ins, base, carried=False)
                    if s in COLS_AT:
                        for j in COLS_AT[s]:
                            ins = pool_cols(j)
                        if POOL - 1 in COLS_AT[s]:
                            ins.then_inc(pool_ready, 1)
                    if 0 <= s - NORM_AT < NORM_PARTS:
                        group_norm(gstat_ready, b + 1, 2, 0, range(CT), base, norm_ready, s - NORM_AT)
                    if s == MIX_AT + 1:
                        mix_copy(b + 1, 0)
                    if s == PW_AT + 1:
                        pwo_copy(b + 1, 0)
                z_add(*Z_LAST)
                if ahead:
                    x_rest(b + 1, 0)
                    x_rest(b + 1, 1)
                    for g in range(8):
                        g_rest(b + 1, g)
                    assert links[0] == CHAIN_IMAGE, ("CHAIN_IMAGE", links[0])

            with dve.Fori(0, B - 1, 1) as b:
                image(b, True)
            image(B - 1, False)

        @block.tensor
        def _(pe):
            def mm(out_, lhsT, rhs, start, stop, **kw):
                return pe.matmul(out_, lhsT, rhs, start=start, stop=stop, **kw)

            def mm3(out_, a_hi, a_lo, b_hi, b_lo, first, last):
                mm(out_, a_hi, b_lo, first, False)
                mm(out_, a_lo, b_hi, False, False)
                return mm(out_, a_hi, b_hi, False, last)

            def group_stats(i, bank, tiles_, ready, made):
                pe.wait_ge(ready, i + 1)
                ts = slice(tiles_[0], tiles_[-1] + 1)
                mm(psum[:, bank, 0:2 * len(tiles_)], gmean[:], stat[:, ts, :].rearrange("p t s -> p (t s)"), True, True)\
                    .then_inc(made, 1)

            def mix(i, bank):
                pe.wait_ge(pn_ready, i + 1)
                for t in range(CT):
                    ins = mm(psum[0:AG, bank, P * t:P * t + P], pooled[:, t].rearrange("p i j -> p (i j)"), ident[:],
                             True, True)
                ins.then_inc(mix_made, 1)

            def pointwise(i, bank):
                pe.wait_ge(pw_load, 16 * (i + 1))
                pe.wait_ge(conv_ready, i + 1)
                for o in range(CT):
                    for k in range(CT):
                        ins = mm(psum[:, bank, AG * o:AG * o + AG], w_pwT[:, k, P * o:P * o + P],
                                 conv[:, k].rearrange("p i j -> p (i j)"), k == 0, k == CT - 1)
                ins.then_inc(pw_ready, 1)

            def turn_agents(i):
                pe.wait_ge(at_loaded, 32 * (i + 1))
                for t in range(HEADS // 2):
                    ins = pe.transpose(psum[:, 1, PAIR * t:PAIR * t + PAIR], at_in[:, t, :], ident[0:PAIR, 0:PAIR])
                ins.then_inc(at_turned, 1)

            def fold_agents(i, prior):
                pe.wait_ge(at_ready, i + 1)
                for g in range(8):
                    prior(g)
                    w = w_k if g < CT else w_q
                    for t in range(HEADS // 2):
                        ins = mm(psum[:, 4 + g % 4, PAIR * t:PAIR * t + PAIR], w[:, t, P * (g % CT):P * (g % CT) + P],
                                 at_bd[:, t, :], True, True)
                    ins.then_inc(g_made, 1)

            pe.wait_ge(pool_setup, 1)
            group_stats(0, 4, range(CT), stat_ready, gstat_ready)
            mix(0, 7)
            pe.wait_ge(p1_load, 32)
            for m in range(CT):
                for k in range(CT):
                    ins = mm(psum[:, m, :], pw_in[:, k, P * m:P * m + P], p1_in[:, k, :], k == 0, k == CT - 1)
                ins.then_inc(pe_p1, 1)
            pe.wait_ge(par_load, 16 * 9)
            for m in range(CT):
                for k in range(CT):
                    ins = mm(psum[:, 6, m:m + 1], p1_in[:, k, P * m:P * m + P], par[:, 7, k:k + 1], k == 0, k == CT - 1)
            ins.then_inc(pe_b1, 1)
            pointwise(0, 5)
            pe.wait_ge(v_b1, 1)
            pe.wait_ge(v_op, 1)
            pe.transpose(psum[:, 6, 0:WIN_N], x2[0:WIN_N, 1, 0:PT_N], ident[0:WIN_N, 0:WIN_N]).then_inc(pe_dn, 1)
            pe.wait_ge(v_p1, CT)
            turn_agents(0)
            pe.wait_ge(gs_read[0], 1)
            pe.wait_ge(kq_load, 32)

            def first_prior(g):
                if g == 1:
                    pe.wait_ge(pwo_ready, 1)
                if g == 2:
                    pe.wait_ge(v_dn, 1)
                if g == 3:
                    pe.wait_ge(mix_ready, 1)
                if g >= 4:
                    pe.wait_ge(g_low, g - 3)
            fold_agents(0, first_prior)
            pe.wait_ge(v_bias, 1)
            pe.wait_ge(w_split, 1)
            pe.wait_ge(v_load, 16)
            pe.wait_ge(proj_load, 16)

            def image(b, ahead):
                def k_scores(n):
                    if n >= 2:
                        pe.wait_ge(sT_ready, NT * b + n - 1)
                    pe.wait_ge(x_low, NT * b + n + 1)
                    for k in range(CT):
                        ins = mm3(psum[:, n % 2, 0:AGS], ring(n, 0)[:, k, :], ring(n, 1)[:, k, :],
                                  g_k_hi[:, k, :], g_k_lo[:, k, :], k == 0, k == CT - 1)
                    ins.then_inc(sk_made, 1)

                def turn_max():
                    pe.wait_ge(kmax_run_ready, b + 1)
                    for t in range(4):
                        ins = pe.transpose(psum[0:PAIR, 0, P * t:P * t + P], kmax_run[:, PAIR * t:PAIR * t + PAIR], ident[:])
                    ins.then_inc(kmax_turned, 1)

                def spread_max():
                    pe.wait_ge(kmax_ready, b + 1)
                    for t in range(4):
                        ins = mm(psum[:, 1, PAIR * t:PAIR * t + PAIR], kmax[:, t:t + 1].broadcast_to([PAIR, P]),
                                 ident[0:PAIR, 0:PAIR], True, True)
                    ins.then_inc(kmax_spread, 1)

                def turn_x(n):
                    if n < 2:
                        pe.wait_ge(g_low, 8 * b + 5 + n)
                    if n >= 2:
                        pe.wait_ge(xT_ready[n % 2], 4 * b + n // 2)
                    for k in range(CT):
                        ins = pe.transpose(psum[:, 4 + n % 2, P * k:P * k + P], xn[:, k, token_tile(n)], ident[:])
                    ins.then_inc(xT_made, 1)

                def q_scores(n):
                    if n == 0:
                        pe.wait_ge(g_low, 8 * (b + 1))
                    if n >= 2:
                        pe.wait_ge(qsub_ready, NT * b + n - 1)
                    for k in range(CT):
                        ins = mm3(psum[:, 2 + n % 2, 0:AGS], ring(n, 0)[:, k, :], ring(n, 1)[:, k, :],
                                  g_q_hi[:, k, :], g_q_lo[:, k, :], k == 0, k == CT - 1)
                    ins.then_inc(sq_made, 1)

                def aggregate_x(n):
                    if n in POOL_XT:
                        pe.wait_ge(xT_low[1], len(POOL_XT) * b + POOL_XT.index(n) + 1)
                    else:
                        pe.wait_ge(xT_low[0], len(VECTOR_XT) * b + VECTOR_XT.index(n) + 1)
                    pe.wait_ge(p_low, NT * b + n + 1)
                    if n == 0:
                        for j in range(2):
                            pe.wait_ge(xT_ready[j], 4 * b + 4)
                        pe.wait_ge(qsub_ready, NT * b + NT - 1)
                    for t in range(CT):
                        ts = slice(P * t, P * t + P)
                        ins = mm3(psum[:, PX_BANKS[t], 0:AGS], xT_ring(n, 0)[:, ts], xT_ring(n, 1)[:, ts],
                                  pT_ring(n, 0), pT_ring(n, 1), n == 0, n == NT - 1)
                        if n == NT - 1:
                            ins.then_inc(px_made, 1)
                    if n < NT - 1:
                        ins.then_inc(px_step, 1)

                def turn_q(n):
                    pe.wait_ge(qp_ready, NT * b + n + 1)
                    if n >= 2:
                        pe.wait_ge(qT_low, NT * b + n - 1)
                    for t in range(4):
                        ins = pe.transpose(psum[0:PAIR, 6 + n % 2, P * t:P * t + P],
                                           qp[:, n % 4, PAIR * t:PAIR * t + PAIR], ident[:])
                    ins.then_inc(qT_made, 1)

                pe.wait_ge(g_low, 8 * b + 4)
                pe.wait_ge(xn_ready, CT * (b + 1))
                for n in range(NT):
                    k_scores(n)
                    turn_x(n)
                    if n:
                        q_scores(n - 1)
                    if n >= 3:
                        turn_q(n - 3)
                turn_max()
                q_scores(7)
                spread_max()
                turn_q(5)
                turn_q(6)
                for n in range(NT):
                    aggregate_x(n)
                turn_q(7)
                pe.wait_ge(px_ready, 4 * b + 4)
                for t in range(4):
                    for k in range(CT):
                        ins = mm(psum[:, 0, PAIR * t:PAIR * t + PAIR], w_vT[:, k, P * t:P * t + P],
                                 pxT[:, k, PAIR * t:PAIR * t + PAIR], k == 0, k == CT - 1)
                ins.then_inc(agg_made, 1)
                pe.wait_ge(ksum_run_ready, b + 1)
                for t in range(4):
                    ins = mm(psum[0:PAIR, 1, t:t + 1], ksum_run[:, PAIR * t:PAIR * t + PAIR], ones[:], True, True)
                ins.then_inc(ksum_made, 1)
                pe.wait_ge(agg_ready, b + 1)
                for t in range(4):
                    if t == 0:
                        pe.wait_ge(px_ready, 4 * b + 4)
                    if t >= 2:
                        pe.wait_ge(qT_low, NT * b + NT - 2 + t - 1)
                    mm(psum[0:PAIR, 4 + t, :], agg[:, t, :], w_p1[:, t, :], True, True).then_inc(f_made, 1)
                for t in range(4):
                    if t == 1:
                        pe.wait_ge(krec_ready, b + 1)
                    if t == 3:
                        pe.wait_ge(qsub_ready, NT * b + NT)
                    mm(psum[0:PAIR, t, :], agg[:, t, :], w_projT[:, t, :], True, True).then_inc(m_made, 1)
                for i in range(8):
                    nh, f = i // 4, i % 4
                    if i == 0:
                        pe.wait_ge(qT_low, NT * b + NT)
                    if i < 4:
                        if i == 0:
                            pe.wait_ge(f_low, 4 * b + 4)
                    elif i == 4:
                        pe.wait_ge(m_low, 3 * b + 3)
                    ns, fs = slice(4 * nh, 4 * nh + 4), slice(P * f, P * f + P)
                    for t in range(4):
                        ins = mm3(psum[:, (4 + i) % 8, :], f_hi[:, t, fs], f_lo[:, t, fs],
                                  qT_hi[0:PAIR, ns, t, :], qT_lo[0:PAIR, ns, t, :], t == 0, t == 3)
                    ins.then_inc(h1_made, 1)
                for i in range(NT):
                    if i % 4 == 0:
                        pe.wait_ge(h1_low, 8 * b + i + 4)
                        pe.wait_ge(h1_ready, 8 * b + i + 4)
                    bank = psum[:, (4 + i) % 8, :]
                    for t in range(4):
                        mm3(bank, qT_hi[0:PAIR, i, t, :], qT_lo[0:PAIR, i, t, :], m_hi[:, t, :], m_lo[:, t, :], t == 0, False)
                    for k in range(CT):
                        ts = slice(P * i, P * i + P)
                        ins = mm3(bank, h1_hi[:, k, ts], h1_lo[:, k, ts], w_2T_hl[:, 0, k, :], w_2T_hl[:, 1, k, :],
                                  False, k == CT - 1)
                    ins.then_inc(o_made, 1)
                    if i == 5:
                        pe.wait_ge(x2_ready, NT * b + 4)
                        group_stats(2 * b, 7, range(2), stat1_ready, gstat1_ready)

                def cut(s):
                    if s >= 2:
                        pe.wait_ge(win_ready, STEPS * b + s - 1)
                    pair, item = s // ITEMS, s % ITEMS
                    for j in range(2):
                        m, n = PATCHES[2 * item + j]
                        for c in range(2):
                            at = P * (2 * j + c)
                            ins = pe.transpose(psum[0:WIN_N, 4 + s % 2, at:at + P],
                                               xpad_run[:, 2 * pair + c, n // MC, WW * m:WW * (m + WH)], ident[:])
                    ins.then_inc(win_made, 1)

                def up(s):
                    pe.wait_ge(win_ready, STEPS * b + s + 1)
                    if s >= 2:
                        pe.wait_ge(up_read, STEPS * b + s - 1)
                    rows, pair = slice(0, WIN_N + 2), s // ITEMS
                    mm(psum[:, 6 + s % 2, :], op_up[:, pair, :], xwin[rows, s % RING, :], True, True).then_inc(up_made, 1)

                def down(s):
                    pe.wait_ge(y_ready, STEPS * b + s + 1)
                    pair, item = s // ITEMS, s % ITEMS
                    for j in range(2):
                        p = 2 * item + j
                        z, ks, ls, ws, wl = down_part(p)
                        first, last = p == SECTION_PATCHES[z][0], p == SECTION_PATCHES[z][-1]
                        if first and 3 * pair + z >= 2:
                            pe.wait_ge(z_ready, 12 * b + 2 * (3 * pair + z) - 2)
                        if first and (pair, z) == (0, 1):
                            pe.wait_ge(gs_read[1], 2 * b + 2)
                        if first and (pair, z) == (1, 0) and ahead:
                            pe.wait_ge(gs_read[0], b + 2)
                        if first and (pair, z) == (1, 1) and ahead:
                            pe.wait_ge(mix_ready, b + 2)
                        for c in range(2):
                            out_ = psum[:, z_bank(pair, z, c), :].rearrange("p (k l) -> p k l", l=W)[:, ks, ls]
                            at = P * (2 * j + c)
                            ins = mm(out_, ypt[:, s % RING, at:at + P], op_dn[:, ws, wl], first, last, skip_group_check=True)
                        if last:
                            ins.then_inc(z_made, 1)

                pe.wait_ge(border_ready, CT * b + 2)
                for j in range(2):
                    pe.wait_ge(xpad_ready[j], 2 * len(COLS) * b + len(COLS))
                cut(0)
                cut(1)
                pe.wait_ge(bias_load, 32 * (b + 1))
                up(0)
                for s in range(STEPS + 1):
                    if s == 0:
                        pe.wait_ge(x2_ready, NT * b + NT)
                    if s + 2 == ITEMS:
                        pe.wait_ge(border_ready, CT * (b + 1))
                        for j in range(2):
                            pe.wait_ge(xpad_ready[j], 2 * len(COLS) * (b + 1))
                    if s + 2 < STEPS:
                        cut(s + 2)
                    if s + 1 < STEPS:
                        up(s + 1)
                    if s:
                        down(s - 1)
                    if s == STAT1_AT:
                        group_stats(2 * b + 1, 3, range(2, CT), stat1_ready, gstat1_ready)
                    if not ahead:
                        continue
                    if s == STAT_AT:
                        pe.wait_ge(z_ready, 12 * b + 4)
                        group_stats(b + 1, 2, range(CT), stat_ready, gstat_ready)
                    if s == MIX_AT:
                        pe.wait_ge(z_ready, 12 * b + 6)
                        mix(b + 1, 0)
                    if s == PW_AT:
                        pe.wait_ge(z_ready, 12 * b + 10)
                        pointwise(b + 1, 0)
                    if s == TURN_AT:
                        turn_agents(b + 1)
                if ahead:
                    def prior(g):
                        if g < 2:
                            pe.wait_ge(win_ready, STEPS * (b + 1))
                        elif g < 4:
                            pe.wait_ge(up_read, STEPS * (b + 1))
                        else:
                            pe.wait_ge(g_low, 8 * (b + 1) + g - 3)
                    fold_agents(b + 1, prior)

            with pe.Fori(0, B - 1, 1) as b:
                image(b, True)
            image(B - 1, False)


def kernel(**inputs):
    import numpy as np
    import concourse.bacc as bacc
    from concourse.bass_utils import run_bass_kernel_spmd as run

    def a(name):
        return np.asarray(inputs[name])

    kv = a("L0_conv_kv_w")
    arrays = {
        "x": a("x").reshape(B, C, N),
        "wq": a("L0_conv_q_w"), "wk": kv[:C], "wvT": kv[C:].T,
        "pwT": a("L0_conv_pw_w").reshape(C, C).T,
        "projT": a("L0_conv_proj_w").T, "proj": a("L0_conv_proj_w"),
        "w1T": a("L0_conv_enh1_w").T, "w2T": a("L0_conv_enh2_w").T,
        "dw_w": a("L0_conv_dw_w").reshape(C, 9), "dw_b": a("L0_conv_dw_b"),
        "bn_g": a("L0_conv_bn_gamma"), "bn_b": a("L0_conv_bn_beta"),
        "bn_m": a("L0_conv_bn_mean"), "bn_v": a("L0_conv_bn_var"),
        "pw_b": a("L0_conv_pw_b"), "proj_b": a("L0_conv_proj_b"),
        "enh1_b": a("L0_conv_enh1_b"), "enh2_b": a("L0_conv_enh2_b"),
        "bias": a("L1_conv_bias"), "up_f": a("L1_conv_up_filter")[::-1], "down_f": a("L1_conv_down_filter"),
    }
    arrays = {f"in_{k}": np.ascontiguousarray(v) for k, v in arrays.items()}
    nc = bacc.Bacc("TRN2", target_bir_lowering=False, num_devices=1)
    args = [nc.dram_tensor(k, v.shape, mybir.dt.from_np(v.dtype), kind="ExternalInput").ap() for k, v in arrays.items()]
    out = nc.dram_tensor("out", (B, C, N), F32, kind="ExternalOutput").ap()
    agent_dram = nc.dram_tensor("agent_scratch", (2, C * AG), F32, kind="Internal").ap()
    filt_dram = nc.dram_tensor("filter_scratch", (2, FILT), F32, kind="Internal").ap()
    build(nc, *args, out, agent_dram, filt_dram)
    got = run(nc, [arrays], core_ids=[0]).results[0]["out"]
    return got.reshape(B, C, H, W)
```
